# Optimizing a Trainium2 kernel written in Bass

```python
import numpy as np
import jax
import jax.numpy as jnp

def _softmax(x, axis=-1):
    return jax.nn.softmax(x, axis=axis)

def _gelu(x):
    return jax.nn.gelu(x, approximate=True)

def _silu(x):
    return jax.nn.silu(x)

def _sigmoid(x):
    return jax.nn.sigmoid(x)

def _layernorm(x, axis=-1, eps=1e-05):
    m = jnp.mean(x, axis=axis, keepdims=True)
    v = jnp.var(x, axis=axis, keepdims=True)
    return (x - m) / jnp.sqrt(v + eps)

def _scatter_add(tgt, idx, src, axis=0):
    return tgt.at[idx].add(src)

def _segment_sum(src, seg, n):
    return jax.ops.segment_sum(src, seg, n)
kernel_name = 'mk_decoder_postln_d2_seqx_r8_027c34'

def setup_inputs(seed: int=0):
    np.random.seed(seed)
    _w = jnp.asarray

    def _rec_inputs():
        import jax
        import jax.numpy as jnp
        _rk = jax.random.key(seed)
        x = -0.0005207 + 1.001 * jax.random.normal(jax.random.fold_in(_rk, 1), (64, 64, 256), jnp.float32)
        _lenS = 64 - jax.random.randint(jax.random.fold_in(_rk, 7), (64,), 0, max(1, 64 // 4) + 1, jnp.int32)
        _lenS2 = 64 - jax.random.randint(jax.random.fold_in(_rk, 8), (64,), 0, max(1, 64 // 4) + 1, jnp.int32)
        _ctx_2048P = jax.random.normal(jax.random.fold_in(_rk, 12), (64, 16, 256), jnp.float32)
        _ctx_2048c = jax.random.dirichlet(jax.random.fold_in(_rk, 512), 0.3 * jnp.ones((16,), jnp.float32), (64, 64))
        _ctx_2048t = jnp.einsum('bsk,bkd->bsd', _ctx_2048c, _ctx_2048P)
        _ctx_2048t = _ctx_2048t * jax.lax.rsqrt(jnp.mean(jnp.square(_ctx_2048t)) + 1e-12) * 0.953939
        ctx_2048 = -5.72187e-05 + 0.999849 * (_ctx_2048t + 0.3 * jax.random.normal(jax.random.fold_in(_rk, 612), (64, 64, 256), jnp.float32))
        _validS = jnp.arange(64)[None, :] < _lenS[:, None]
        _validS2 = jnp.arange(64)[None, :] < _lenS2[:, None]
        _causal = jnp.tril(jnp.ones((64, 64), dtype=bool))
        mask_BxSx4224_bf0 = jnp.logical_not(jnp.ones((64, 64, 528), dtype=bool))
        mask_BxSxS2_ff0 = jnp.where(jnp.ones((64, 64, 64), dtype=bool), 0.0, -1000000000.0).astype(jnp.float32)
        return (x, ctx_2048, mask_BxSx4224_bf0, mask_BxSxS2_ff0)
    x, ctx_2048, mask_BxSx4224_bf0, mask_BxSxS2_ff0 = _rec_inputs()

    def _L0_attn_setup():
        import math
        import jax, jax.numpy as jnp
        import numpy as np
        B, T, E, H = (2, 256, 256, 16)
        D = E // H

        def _alibi_slopes(n):
            start = 2.0 ** (-2.0 ** (-(math.log2(n) - 3)))
            return np.array([start * start ** i for i in range(n)], dtype=np.float32)
        key = jax.random.key(seed)
        ks = jax.random.split(key, 5)
        w_scale = 0.02
        return {'x': jax.random.normal(ks[0], (B, T, E), dtype=jnp.float32), 'Wq': jax.random.normal(ks[1], (E, E), dtype=jnp.float32) * w_scale, 'bq': jnp.zeros((E,), jnp.float32), 'Wk': jax.random.normal(ks[2], (E, E), dtype=jnp.float32) * w_scale, 'bk': jnp.zeros((E,), jnp.float32), 'Wv': jax.random.normal(ks[3], (E, E), dtype=jnp.float32) * w_scale, 'bv': jnp.zeros((E,), jnp.float32), 'Wo': jax.random.normal(ks[4], (E, E), dtype=jnp.float32) * w_scale, 'bo': jnp.zeros((E,), jnp.float32), 'slopes': jnp.asarray(_alibi_slopes(H))}
    _L0_attn_all = _L0_attn_setup()
    _L0_attn_in = {k: v for k, v in _L0_attn_all.items() if k in ('Wq', 'bq', 'Wk', 'bk', 'Wv', 'bv', 'Wo', 'bo', 'slopes')}
    del _L0_attn_all

    def _L0_xattn_setup():
        import jax, jax.numpy as jnp
        import numpy as np
        import math
        DIM = 256
        B, Q_LEN, KV_LEN = (8, 128, 512)
        key = jax.random.key(seed)
        ks = jax.random.split(key, 8)
        x = jax.random.normal(ks[0], (B, Q_LEN, DIM), dtype=jnp.float32)
        mask = jnp.zeros((B, Q_LEN, KV_LEN + Q_LEN), dtype=bool)
        k_cache = jax.random.normal(ks[1], (B, KV_LEN, DIM), dtype=jnp.float32)
        v_cache = jax.random.normal(ks[2], (B, KV_LEN, DIM), dtype=jnp.float32)
        scale = 1.0 / math.sqrt(DIM)
        wq = jax.random.normal(ks[3], (DIM, DIM), dtype=jnp.float32) * scale
        wk = jax.random.normal(ks[4], (DIM, DIM), dtype=jnp.float32) * scale
        wv = jax.random.normal(ks[5], (DIM, DIM), dtype=jnp.float32) * scale
        wo = jax.random.normal(ks[6], (DIM, DIM), dtype=jnp.float32) * scale
        return {'x': x, 'mask': mask, 'k_cache': k_cache, 'v_cache': v_cache, 'wq': wq, 'wk': wk, 'wv': wv, 'wo': wo}
    _L0_xattn_all = _L0_xattn_setup()
    _L0_xattn_in = {k: v for k, v in _L0_xattn_all.items() if k in ('wq', 'wk', 'wv', 'wo')}
    del _L0_xattn_all

    def _L0_ffn_setup():
        import jax, jax.numpy as jnp
        import numpy as np
        Q = 127.0

        def _round_ste(v):
            return v + jax.lax.stop_gradient(jnp.round(v) - v)

        def quantize_rowwise(x):
            absmax = jnp.max(jnp.abs(x), axis=1, keepdims=True)
            q = jnp.clip(_round_ste(x * (Q / absmax)), -Q, Q)
            return (q, absmax)

        def quantize_global(w):
            absmax = jnp.max(jnp.abs(w))
            q = jnp.clip(_round_ste(w * (Q / absmax)), -Q, Q)
            return (q, absmax)

        def int8_matmul_dequant_bias(a_q, b_q_t, state_a, state_b, bias):
            acc = jnp.matmul(a_q, b_q_t)
            return acc * (state_a * state_b / (Q * Q)) + bias
        key = jax.random.key(seed)
        k1, k2, k3, k4, k5 = jax.random.split(key, 5)
        B, S, D, H = (4, 256, 256, 1024)
        x = jax.random.normal(k1, (B, S, D), dtype=jnp.float32)
        W1 = jax.random.normal(k2, (H, D), dtype=jnp.float32) * (1.0 / np.sqrt(D))
        B1 = jax.random.normal(k3, (H,), dtype=jnp.float32) * 0.02
        W2 = jax.random.normal(k4, (D, H), dtype=jnp.float32) * (1.0 / np.sqrt(H))
        B2 = jax.random.normal(k5, (D,), dtype=jnp.float32) * 0.02
        return {'x': x, 'W1': W1, 'B1': B1, 'W2': W2, 'B2': B2}
    _L0_ffn_all = _L0_ffn_setup()
    _L0_ffn_in = {k: v for k, v in _L0_ffn_all.items() if k in ('W1', 'B1', 'W2', 'B2')}
    del _L0_ffn_all

    def _L1_attn_setup():
        import jax, jax.numpy as jnp
        import numpy as np
        NUM_HEADS = 16

        def _l2_normalize_complex(z):
            n = jnp.sqrt(jnp.sum(jnp.abs(z) ** 2, axis=-1, keepdims=True))
            return z / n
        key = jax.random.key(seed)
        k1, k2, k3, k4 = jax.random.split(key, 4)
        B, S, D = (4, 512, 256)
        scale = 1.0 / np.sqrt(D)
        return {'x': jax.random.normal(k1, (B, S, D), dtype=jnp.float32), 'W_q': jax.random.normal(k2, (D, D), dtype=jnp.float32) * scale, 'W_kv': jax.random.normal(k3, (D, D), dtype=jnp.float32) * scale, 'W_o': jax.random.normal(k4, (D, D), dtype=jnp.float32) * scale}
    _L1_attn_all = _L1_attn_setup()
    _L1_attn_in = {k: v for k, v in _L1_attn_all.items() if k in ('W_q', 'W_kv', 'W_o')}
    del _L1_attn_all

    def _L1_xattn_setup():
        import jax, jax.numpy as jnp
        import numpy as np
        NUM_HEADS = 16
        EPS = 1e-08

        def _dyn_quant(x):
            s = jnp.maximum(jnp.max(jnp.abs(x), axis=-1, keepdims=True) / 127.0, EPS)
            q = jnp.clip(jnp.round(x / s), -127.0, 127.0)
            return (q, s)

        def _quant_weight(w):
            s = jnp.maximum(jnp.max(jnp.abs(w), axis=1, keepdims=True) / 127.0, EPS)
            q = jnp.clip(jnp.round(w / s), -127.0, 127.0)
            return (q, s)

        def _w8a8_linear(x, w, b):
            qx, sx = _dyn_quant(x)
            qw, sw = _quant_weight(w)
            y = jnp.einsum('bnc,oc->bno', qx, qw) * (sx * sw[:, 0])
            return y + b
        key = jax.random.key(seed)
        ks = jax.random.split(key, 9)
        B, N, L, C = (2, 512, 64, 256)
        sc = 0.02
        return {'x': jax.random.normal(ks[0], (B, N, C), jnp.float32), 'cond': jax.random.normal(ks[1], (B, L, C), jnp.float32), 'mask': jnp.zeros((B, N, L), jnp.float32), 'wq': jax.random.normal(ks[2], (C, C), jnp.float32) * sc, 'bq': jnp.zeros((C,), jnp.float32), 'wk': jax.random.normal(ks[3], (C, C), jnp.float32) * sc, 'bk': jnp.zeros((C,), jnp.float32), 'wv': jax.random.normal(ks[4], (C, C), jnp.float32) * sc, 'bv': jnp.zeros((C,), jnp.float32), 'wo': jax.random.normal(ks[5], (C, C), jnp.float32) * sc, 'bo': jnp.zeros((C,), jnp.float32)}
    _L1_xattn_all = _L1_xattn_setup()
    _L1_xattn_in = {k: v for k, v in _L1_xattn_all.items() if k in ('wq', 'bq', 'wk', 'bk', 'wv', 'bv', 'wo', 'bo')}
    del _L1_xattn_all

    def _L1_ffn_setup():
        import jax, jax.numpy as jnp
        import numpy as np
        B, S, H = (2, 128, 256)
        E, K = (8, 2)
        F = 176
        FS = 704
        NORM_TOPK = False

        def _swiglu(x, wg, wu, wd):
            return jax.nn.silu(x @ wg) * (x @ wu) @ wd
        key = jax.random.key(seed)
        ks = jax.random.split(key, 9)
        s = 0.02
        return {'hidden_states': jax.random.normal(ks[0], (B, S, H), dtype=jnp.float32), 'Wr': jax.random.normal(ks[1], (H, E), dtype=jnp.float32) * s, 'Wg': jax.random.normal(ks[2], (E, H, F), dtype=jnp.float32) * s, 'Wu': jax.random.normal(ks[3], (E, H, F), dtype=jnp.float32) * s, 'Wd': jax.random.normal(ks[4], (E, F, H), dtype=jnp.float32) * s, 'Sg': jax.random.normal(ks[5], (H, FS), dtype=jnp.float32) * s, 'Su': jax.random.normal(ks[6], (H, FS), dtype=jnp.float32) * s, 'Sd': jax.random.normal(ks[7], (FS, H), dtype=jnp.float32) * s, 'Wsg': jax.random.normal(ks[8], (H, 1), dtype=jnp.float32) * s}
    _L1_ffn_all = _L1_ffn_setup()
    _L1_ffn_in = {k: v for k, v in _L1_ffn_all.items() if k in ('Wr', 'Wg', 'Wu', 'Wd', 'Sg', 'Su', 'Sd', 'Wsg')}
    del _L1_ffn_all
    return {'x': x, 'ctx_2048': ctx_2048, 'mask_BxSx4224_bf0': mask_BxSx4224_bf0, 'mask_BxSxS2_ff0': mask_BxSxS2_ff0, 'L0_attn_Wq': _L0_attn_in['Wq'], 'L0_attn_bq': _L0_attn_in['bq'], 'L0_attn_Wk': _L0_attn_in['Wk'], 'L0_attn_bk': _L0_attn_in['bk'], 'L0_attn_Wv': _L0_attn_in['Wv'], 'L0_attn_bv': _L0_attn_in['bv'], 'L0_attn_Wo': _L0_attn_in['Wo'], 'L0_attn_bo': _L0_attn_in['bo'], 'L0_attn_slopes': _L0_attn_in['slopes'], 'L0_xattn_wq': _L0_xattn_in['wq'], 'L0_xattn_wk': _L0_xattn_in['wk'], 'L0_xattn_wv': _L0_xattn_in['wv'], 'L0_xattn_wo': _L0_xattn_in['wo'], 'L0_ffn_W1': _L0_ffn_in['W1'], 'L0_ffn_B1': _L0_ffn_in['B1'], 'L0_ffn_W2': _L0_ffn_in['W2'], 'L0_ffn_B2': _L0_ffn_in['B2'], 'L1_attn_W_q': _L1_attn_in['W_q'], 'L1_attn_W_kv': _L1_attn_in['W_kv'], 'L1_attn_W_o': _L1_attn_in['W_o'], 'L1_xattn_wq': _L1_xattn_in['wq'], 'L1_xattn_bq': _L1_xattn_in['bq'], 'L1_xattn_wk': _L1_xattn_in['wk'], 'L1_xattn_bk': _L1_xattn_in['bk'], 'L1_xattn_wv': _L1_xattn_in['wv'], 'L1_xattn_bv': _L1_xattn_in['bv'], 'L1_xattn_wo': _L1_xattn_in['wo'], 'L1_xattn_bo': _L1_xattn_in['bo'], 'L1_ffn_Wr': _L1_ffn_in['Wr'], 'L1_ffn_Wg': _L1_ffn_in['Wg'], 'L1_ffn_Wu': _L1_ffn_in['Wu'], 'L1_ffn_Wd': _L1_ffn_in['Wd'], 'L1_ffn_Sg': _L1_ffn_in['Sg'], 'L1_ffn_Su': _L1_ffn_in['Su'], 'L1_ffn_Sd': _L1_ffn_in['Sd'], 'L1_ffn_Wsg': _L1_ffn_in['Wsg']}

def reference(x, ctx_2048, mask_BxSx4224_bf0, mask_BxSxS2_ff0, L0_attn_Wq, L0_attn_bq, L0_attn_Wk, L0_attn_bk, L0_attn_Wv, L0_attn_bv, L0_attn_Wo, L0_attn_bo, L0_attn_slopes, L0_xattn_wq, L0_xattn_wk, L0_xattn_wv, L0_xattn_wo, L0_ffn_W1, L0_ffn_B1, L0_ffn_W2, L0_ffn_B2, L1_attn_W_q, L1_attn_W_kv, L1_attn_W_o, L1_xattn_wq, L1_xattn_bq, L1_xattn_wk, L1_xattn_bk, L1_xattn_wv, L1_xattn_bv, L1_xattn_wo, L1_xattn_bo, L1_ffn_Wr, L1_ffn_Wg, L1_ffn_Wu, L1_ffn_Wd, L1_ffn_Sg, L1_ffn_Su, L1_ffn_Sd, L1_ffn_Wsg):
    import jax
    import jax.numpy as jnp

    def _L0_attn_ref(x, Wq, bq, Wk, bk, Wv, bv, Wo, bo, slopes):
        import math
        import jax, jax.numpy as jnp
        import numpy as np
        B, T, E, H = (2, 256, 256, 16)
        D = E // H

        def _alibi_slopes(n):
            start = 2.0 ** (-2.0 ** (-(math.log2(n) - 3)))
            return np.array([start * start ** i for i in range(n)], dtype=np.float32)
        b, t, e = x.shape
        h, d = (H, e // H)
        scaling = d ** (-0.5)
        q = (jnp.einsum('bte,fe->btf', x, Wq) + bq) * scaling
        k = jnp.einsum('bte,fe->btf', x, Wk) + bk
        v = jnp.einsum('bte,fe->btf', x, Wv) + bv
        q = q.reshape(b, t, h, d)
        k = k.reshape(b, t, h, d)
        v = v.reshape(b, t, h, d)
        scores = jnp.einsum('bihd,bjhd->bhij', q, k)
        pos = jnp.arange(t)
        alibi = -jnp.abs(pos[None, :] - pos[:, None]).astype(scores.dtype)
        scores = scores + slopes[:, None, None] * alibi
        probs = jax.nn.softmax(scores.astype(jnp.float32), axis=-1).astype(scores.dtype)
        out = jnp.einsum('bhij,bjhd->bihd', probs, v).reshape(b, t, e)
        return jnp.einsum('bte,fe->btf', out, Wo) + bo

    def _L0_xattn_ref(x, mask, k_cache, v_cache, wq, wk, wv, wo):
        import jax, jax.numpy as jnp
        import numpy as np
        import math
        DIM = 256
        B, Q_LEN, KV_LEN = (8, 128, 512)
        q = jnp.einsum('bsd,ed->bse', x, wq)
        k_new = jnp.einsum('bsd,ed->bse', x, wk)
        v_new = jnp.einsum('bsd,ed->bse', x, wv)
        k = jnp.concatenate([k_cache, k_new], axis=1)
        v = jnp.concatenate([v_cache, v_new], axis=1)
        scale = 1.0 / math.sqrt(q.shape[-1])
        scores = jnp.einsum('bqd,bkd->bqk', q, k) * scale
        attn = jax.nn.softmax(scores, axis=-1)
        out = jnp.einsum('bqk,bkd->bqd', attn, v)
        return jnp.einsum('bqd,ed->bqe', out, wo)

    def _L0_ffn_ref(x, W1, B1, W2, B2):
        import jax, jax.numpy as jnp
        import numpy as np
        Q = 127.0

        def _round_ste(v):
            return v + jax.lax.stop_gradient(jnp.round(v) - v)

        def quantize_rowwise(x):
            absmax = jnp.max(jnp.abs(x), axis=1, keepdims=True)
            q = jnp.clip(_round_ste(x * (Q / absmax)), -Q, Q)
            return (q, absmax)

        def quantize_global(w):
            absmax = jnp.max(jnp.abs(w))
            q = jnp.clip(_round_ste(w * (Q / absmax)), -Q, Q)
            return (q, absmax)

        def int8_matmul_dequant_bias(a_q, b_q_t, state_a, state_b, bias):
            acc = jnp.matmul(a_q, b_q_t)
            return acc * (state_a * state_b / (Q * Q)) + bias
        X1 = x.reshape(-1, x.shape[-1])
        X1_q, sX1 = quantize_rowwise(X1)
        W1_q, sW1 = quantize_global(W1)
        X2_pre = int8_matmul_dequant_bias(X1_q, W1_q.T, sX1, sW1, B1)
        X2 = jax.nn.gelu(X2_pre, approximate=True)
        X2_q, sX2 = quantize_rowwise(X2)
        W2_q, sW2 = quantize_global(W2)
        out = int8_matmul_dequant_bias(X2_q, W2_q.T, sX2, sW2, B2)
        return out.reshape(*x.shape[:-1], -1)

    def _L1_attn_ref(x, W_q, W_kv, W_o):
        import jax, jax.numpy as jnp
        import numpy as np
        NUM_HEADS = 16

        def _l2_normalize_complex(z):
            n = jnp.sqrt(jnp.sum(jnp.abs(z) ** 2, axis=-1, keepdims=True))
            return z / n
        B, S, D = x.shape
        H = NUM_HEADS
        hd = D // H
        q = (x @ W_q.T).reshape(B, S, H, hd)
        kv = (x @ W_kv.T).reshape(B, S, H, hd)
        qf = jnp.fft.fft(q, axis=-1)
        kvf = jnp.fft.fft(kv, axis=-1)
        qf = _l2_normalize_complex(qf)
        kvf = _l2_normalize_complex(kvf)
        kvf = jnp.cumsum(kvf, axis=1)
        qv = qf * kvf
        values_hat = jnp.fft.ifft(qv, axis=-1).real.astype(x.dtype)
        values_hat = values_hat.reshape(B, S, D)
        return values_hat @ W_o.T

    def _L1_xattn_ref(x, cond, mask, wq, bq, wk, bk, wv, bv, wo, bo):
        import jax, jax.numpy as jnp
        import numpy as np
        NUM_HEADS = 16
        EPS = 1e-08

        def _dyn_quant(x):
            s = jnp.maximum(jnp.max(jnp.abs(x), axis=-1, keepdims=True) / 127.0, EPS)
            q = jnp.clip(jnp.round(x / s), -127.0, 127.0)
            return (q, s)

        def _quant_weight(w):
            s = jnp.maximum(jnp.max(jnp.abs(w), axis=1, keepdims=True) / 127.0, EPS)
            q = jnp.clip(jnp.round(w / s), -127.0, 127.0)
            return (q, s)

        def _w8a8_linear(x, w, b):
            qx, sx = _dyn_quant(x)
            qw, sw = _quant_weight(w)
            y = jnp.einsum('bnc,oc->bno', qx, qw) * (sx * sw[:, 0])
            return y + b
        B, N, C = x.shape
        L = cond.shape[1]
        H = NUM_HEADS
        D = C // H
        inv_sqrt_d = np.float32(1.0 / np.sqrt(D))
        q = _w8a8_linear(x, wq, bq).reshape(B, N, H, D).transpose(0, 2, 1, 3)
        k = (cond @ wk.T + bk).reshape(B, L, H, D).transpose(0, 2, 1, 3)
        v = (cond @ wv.T + bv).reshape(B, L, H, D).transpose(0, 2, 1, 3)
        scores = jnp.einsum('bhnd,bhld->bhnl', q, k) * inv_sqrt_d + mask[:, None]
        attn = jax.nn.softmax(scores, axis=-1)
        o = jnp.einsum('bhnl,bhld->bhnd', attn, v)
        o = o.transpose(0, 2, 1, 3).reshape(B, N, C)
        return _w8a8_linear(o, wo, bo)

    def _L1_ffn_ref(hidden_states, Wr, Wg, Wu, Wd, Sg, Su, Sd, Wsg):
        import jax, jax.numpy as jnp
        import numpy as np
        B, S, H = (2, 128, 256)
        E, K = (8, 2)
        F = 176
        FS = 704
        NORM_TOPK = False

        def _swiglu(x, wg, wu, wd):
            return jax.nn.silu(x @ wg) * (x @ wu) @ wd
        b, s, h = hidden_states.shape
        x = hidden_states.reshape(-1, h)
        router_logits = x @ Wr
        probs = jax.nn.softmax(router_logits.astype(jnp.float32), axis=-1)
        routing_weights, selected = jax.lax.top_k(probs, K)
        if NORM_TOPK:
            routing_weights = routing_weights / routing_weights.sum(-1, keepdims=True)
        routing_weights = routing_weights.astype(x.dtype)
        C = jnp.einsum('tk,tke->te', routing_weights, jax.nn.one_hot(selected, E, dtype=x.dtype))
        expert_out = jax.vmap(lambda wg, wu, wd: _swiglu(x, wg, wu, wd))(Wg, Wu, Wd)
        moe_out = jnp.einsum('te,eth->th', C, expert_out)
        shared = _swiglu(x, Sg, Su, Sd)
        shared = jax.nn.sigmoid(x @ Wsg) * shared
        out = (moe_out + shared).reshape(b, s, h)
        return out
    x = _layernorm(x + _L0_attn_ref(x, L0_attn_Wq, L0_attn_bq, L0_attn_Wk, L0_attn_bk, L0_attn_Wv, L0_attn_bv, L0_attn_Wo, L0_attn_bo, L0_attn_slopes), axis=-1)
    x = _layernorm(x + _L0_xattn_ref(x, mask_BxSx4224_bf0, ctx_2048, ctx_2048, L0_xattn_wq, L0_xattn_wk, L0_xattn_wv, L0_xattn_wo), axis=-1)
    x = _layernorm(x + _L0_ffn_ref(x, L0_ffn_W1, L0_ffn_B1, L0_ffn_W2, L0_ffn_B2), axis=-1)
    x = _layernorm(x + _L1_attn_ref(x, L1_attn_W_q, L1_attn_W_kv, L1_attn_W_o), axis=-1)
    x = _layernorm(x + _L1_xattn_ref(x, ctx_2048, mask_BxSxS2_ff0, L1_xattn_wq, L1_xattn_bq, L1_xattn_wk, L1_xattn_bk, L1_xattn_wv, L1_xattn_bv, L1_xattn_wo, L1_xattn_bo), axis=-1)
    x = _layernorm(x + _L1_ffn_ref(x, L1_ffn_Wr, L1_ffn_Wg, L1_ffn_Wu, L1_ffn_Wd, L1_ffn_Sg, L1_ffn_Su, L1_ffn_Sd, L1_ffn_Wsg), axis=-1)
    return x

_drawn_inputs = setup_inputs


def setup_inputs(seed=0):
    import zlib

    import numpy as np

    out = dict(_drawn_inputs(seed))
    spreads = {'L0_attn_bq': (0.0, 0.8),
     'L0_attn_bk': (0.0, 0.8),
     'L0_attn_bv': (0.0, 0.1),
     'L0_attn_bo': (0.0, 0.1),
     'L1_xattn_bq': (0.0, 0.8),
     'L1_xattn_bk': (0.0, 0.8),
     'L1_xattn_bv': (0.0, 0.274),
     'L1_xattn_bo': (0.0, 0.1)}
    factors = {'L0_attn_Wq': 7.637,
     'L0_attn_Wk': 7.511,
     'L0_attn_slopes': 2.925,
     'L0_ffn_B1': 3.623,
     'L0_ffn_B2': 3.169,
     'L1_xattn_wq': 8.0,
     'L1_xattn_wk': 8.0,
     'L1_ffn_Wr': 8.0,
     'L1_ffn_Wg': 8.0,
     'L1_ffn_Wu': 8.0,
     'L1_ffn_Wd': 8.0,
     'L1_ffn_Sg': 4.04,
     'L1_ffn_Su': 4.005,
     'L1_ffn_Sd': 4.003,
     'L1_ffn_Wsg': 8.0}
    for name, (base, spread) in spreads.items():
        noise = np.random.default_rng([zlib.crc32(name.encode()), seed]).standard_normal(out[name].shape)
        drawn = base * np.exp(spread * noise) if base else spread * noise
        out[name] = jnp.asarray(drawn.astype(out[name].dtype))
    for name, factor in factors.items():
        out[name] = (out[name] * factor).astype(out[name].dtype)
    return out
```

```python
from contextlib import ExitStack

import numpy as np

import concourse.bass as bass
from concourse import mybir
from concourse.alu_op_type import AluOpType as ALU

F32 = mybir.dt.float32
BF16 = mybir.dt.bfloat16
ACT = mybir.ActivationFunctionType
X = mybir.AxisListType.X
XY = mybir.AxisListType.XY
ABSMAX = bass.bass_isa.ReduceOp.absmax

BATCH, SEQ, D = 64, 64, 256
P = 128
NT = BATCH * SEQ // P
KC = D // P
H, HD = 16, 16
HQ = 4
F1 = 1024
E8, FE, FS = 8, 176, 704
NU = E8 + FS // FE
FH = NU * FE
NH = -(-FH // P)
QMAX = 127.0
QEPS = 1e-8
EPS = 1e-5
ROUND = 1.5 * 2.0 ** 23
N_READY = 14


class Named:
    pass


def past(count):
    return not isinstance(count, int) or count > 0


def apart(k, eng, *counts):
    for count in counts:
        if not isinstance(count, int):
            eng.compute_val(count)
    eng.wait_ge(k.filled, 2)


def over_tiles(eng, skew, step):
    lead = 4
    for t in range(lead):
        step(t, t % 2)
    with eng.Fori(lead, NT - 1, 2) as i:
        step(i, 0)
        step(i + 1, 1)
    for t in range(NT, NT + skew):
        step(t, t % 2)


def landed(u, parity, n):
    return 8 * n * (u - parity) + 16 * n


def live(t, s):
    return not isinstance(t, int) or 0 <= t - s < NT


def declare(nc, ctx, io):
    def sb(name, shape, dt=F32):
        return ctx.enter_context(nc.sbuf_tensor(name, shape, dt))

    k = Named()
    k.nc, k.io, k.sb = nc, io, sb
    k.sem = lambda name: ctx.enter_context(nc.semaphore(name))
    k.ps = ctx.enter_context(nc.psum_tensor("ps", [P, 8, 512], F32))
    k.x = sb("x_res", [P, NT, D])
    k.shared = sb("shared", [P, 8192])
    k.q_all = k.shared[:].rearrange("p (t c n) -> p t c n", t=NT, c=KC)
    k.h_rows = k.shared[:, 0:2 * FH].rearrange("p (b n) -> p b n", b=2)
    k.h_t = k.shared[:, 2 * FH:2 * FH + NH * P].rearrange("p (c n) -> p c n", c=NH)
    k.ident = sb("ident", [P, P])
    k.ones = sb("ones", [P, P])
    k.mask4 = sb("mask4", [P, HQ])
    k.mask2 = sb("mask2", [P, 2])
    k.half = sb("minus_half", [P, 32])
    k.xs = sb("x_rows", [P, 2, D])
    k.xt1 = sb("x_turned", [P, KC, P])
    k.xtq = sb("x_turned_q", [P, KC, P], BF16)
    k.sc = sb("scores", [P, 2, H, SEQ])
    k.wide = k.sc[:].rearrange("p b h j -> p b (h j)")
    k.mx, k.rs, k.ri = sb("row_max", [P, 2, H]), sb("row_sum", [P, 2, H]), sb("row_inv", [P, 2, H])
    k.pt = sb("probs_t", [P, 8, P])
    k.qt, k.kt = sb("q_t", [P, 2, KC, P]), sb("k_masked", [P, KC, HQ, P])
    k.vb = sb("v_pairs", [P, 2, 2, D])
    k.on, k.ot = sb("o_rows", [P, D]), sb("o_t", [P, KC, P])
    k.xt = sb("x_t", [P, 2, KC, 2, 2, SEQ])
    k.om = sb("o_quant", [P, 2, 4])
    k.msk = sb("mask_in", [P, 2, SEQ])
    k.r = sb("r", [P, 2, D])
    k.bn = sb("bn", [P, 2, 6])
    k.mv = sb("mv", [P, 2, 2])
    k.rstd = sb("rstd", [P, 2, 1])
    k.ln_sum, k.ln_stats, k.ln_mv, k.ln_eps, k.ln_rstd, k.x_ready = (
        k.sem("ln_" + n) for n in ("sum", "stats", "mv", "eps", "rstd", "x_ready"))
    return k


def norm_stats(k, dve, ph, u, p):
    dve.wait_ge(k.ln_sum, ph * NT + u + 1)
    dve.bn_stats(k.bn[:, p, :], k.r[:, p, :]).then_inc(k.ln_stats, 1)
    apart(k, dve, ph * NT + u + 1)
    dve.wait_ge(k.ln_stats, ph * NT + u + 1)
    dve.bn_aggr(k.mv[:, p, :], k.bn[:, p, :]).then_inc(k.ln_mv, 1)


def norm_rstd(k, pool, ph, u, p):
    apart(k, pool, ph * NT + u + 1)
    pool.wait_ge(k.ln_mv, ph * NT + u + 1)
    pool.tensor_scalar(k.rstd[:, p, :], k.mv[:, p, 1:2], EPS, None, ALU.add).then_inc(k.ln_eps, 1)
    pool.wait_ge(k.ln_eps, ph * NT + u + 1)
    pool.tensor_tensor(k.rstd[:, p, :], k.rstd[:, p, :], k.half[:, 0:1], ALU.pow).then_inc(k.ln_rstd, 1)


def norm_apply(k, dve, ph, u, p, out):
    dve.wait_ge(k.ln_rstd, ph * NT + u + 1)
    dve.tensor_scalar(out, k.r[:, p, :], k.mv[:, p, 0:1], k.rstd[:, p, :], ALU.subtract,
                      ALU.mult).then_inc(k.x_ready, 1)


def setup(k):
    nc, io, sb = k.nc, k.io, k.sb
    s_ld, s_ld2, s_fill = k.sem("w_loaded"), k.sem("x_loaded"), k.sem("filled")
    k.filled = s_fill
    k.s_ld2 = s_ld2
    loads = []

    def w(name, shape):
        t = sb("w_" + name, shape)
        loads.append((t, io[name]))
        return t
    k.a0 = {n: w("a0_" + n, [P, KC, D]) for n in ("wq", "wk", "wv", "wo")}
    k.a0_bq, k.a0_bk, k.a0_bv = (w("a0_" + n, [P, KC]) for n in ("bq", "bk", "bv"))
    k.a0_bo = w("a0_bo", [P, D])
    slopes, dist = w("slopes", [P, H]), w("dist", [P, SEQ])
    k.alibi = sb("alibi", [P, H, SEQ])
    k.c0 = {n: w("c0_" + n, [P, KC, D]) for n in ("wq", "wk", "wv", "wo")}
    k.w1q = sb("w1q", [P, KC, F1], BF16)
    k.w2q = sb("w2q", [P, F1 // P, D], BF16)
    k.b1, k.b2 = w("b1", [P, F1]), w("b2", [P, D])
    w1f = k.shared[:, 0:2048].rearrange("p (c n) -> p c n", c=KC)
    w2f = k.shared[:, 2048:4096].rearrange("p (c n) -> p c n", c=F1 // P)
    k.gmax, k.wscale = sb("gmax", [P, 2]), sb("wscale", [P, 2])
    amax, wrq = sb("amax", [P, 6]), sb("wrq", [P, 6])
    k.f_in, k.f_out = sb("f_in", [P, KC, 2 * D]), sb("f_out", [P, 3, D])
    k.tri = w("tri", [P, P])
    fnat = {n: k.shared[:, 4096 + 512 * i:4608 + 512 * i].rearrange("p (c n) -> p c n", c=KC)
            for i, n in enumerate(("f_wq", "f_wkv", "f_wo", "dft"))}
    idft = k.shared[:, 6144:6912].rearrange("p (c n) -> p c n", c=KC)
    k.c1 = {n: w("c1_" + n, [P, KC, D]) for n in ("wk", "wv")}
    k.c1_bk, k.c1_bq, k.c1_bv, k.c1_bo = (w("c1_bk", [P, KC]), w("c1_bq", [P, D]),
                                          w("c1_bv", [P, D]), w("c1_bo", [P, D]))
    k.c1_wqq, k.c1_woq = sb("c1_wqq", [P, KC, D], BF16), sb("c1_woq", [P, KC, D], BF16)
    k.c1_sq, k.c1_so = sb("c1_sq", [P, D]), sb("c1_so", [P, D])
    cnat = [k.shared[:, 6912:7424].rearrange("p (c n) -> p c n", c=KC),
            k.shared[:, 7424:7936].rearrange("p (c n) -> p c n", c=KC)]
    wsr = sb("wsr", [P, 4])
    diag = sb("diag", [P, 4, P])
    k.rank = w("rank", [P, E8])
    k.wr = w("wr", [P, KC, E8 + 1])
    k.gu = w("gu", [P, KC, NU, 2 * FE])
    k.dn = sb("w_dn", [P, NH, D])
    loads += [(w1f, io["w1"]), (w2f, io["w2"]), (idft, io["idft"]),
              (cnat[0], io["c1_wq"]), (cnat[1], io["c1_wo"])]
    loads += [(fnat[n], io[n]) for n in fnat]
    loads += [(k.ident, io["ident"]), (k.mask4, io["mask4"]), (k.mask2, io["mask2"])]
    loads += [(k.dn[:, 0:NH - 1, :], io["dn"]), (k.dn[0:FH - (NH - 1) * P, NH - 1, :], io["dn_tail"])]
    s_am, s_gm, s_ws, s_q, s_tr, s_ev = (k.sem("w_" + n) for n in
                                         ("absmax", "allmax", "scale", "quant", "turned", "done"))
    s_mm = k.sem("w_mm")
    k.w_done = s_ev
    NX = 8
    n_loads = 16 * len(loads)

    def load(sp):
        for i in range(NX):
            n = NT // NX
            sp.dma_start(k.x[:, n * i:n * (i + 1), :], io["x"][:, n * i:n * (i + 1), :]).then_inc(s_ld2, 16)
        for dst, src in loads:
            sp.dma_start(dst if isinstance(dst, bass.AP) else dst[:], src).then_inc(s_ld, 16)

    def pool(e):
        e.memset(k.half[:], -0.5).then_inc(s_fill, 1)
        e.memset(k.ones[:], 1.0).then_inc(s_fill, 1)
        e.wait_ge(s_am, 2)
        e.partition_all_reduce(k.gmax[:], amax[:, 0:2], P, ABSMAX).then_inc(s_gm, 1)
        e.wait_ge(s_ld2, 16 * NX)
        e.wait_ge(s_fill, 2)

    n_done = [0]

    def done(ins):
        ins.then_inc(s_ev, 1)
        n_done[0] += 1

    def vector(e):
        e.wait_ge(s_ld, n_loads)
        e.tensor_reduce(amax[:, 0:1], w1f, XY, ALU.max, apply_absolute_value=True).then_inc(s_am, 1)
        e.tensor_reduce(amax[:, 1:2], w2f, XY, ALU.max, apply_absolute_value=True).then_inc(s_am, 1)
        e.tensor_reduce(amax[:, 2:4], cnat[0], X, ALU.max, apply_absolute_value=True).then_inc(s_am, 1)
        e.tensor_reduce(amax[:, 4:6], cnat[1], X, ALU.max, apply_absolute_value=True).then_inc(s_am, 1)
        done(e.tensor_tensor(k.alibi[:], slopes[:].unsqueeze(2).broadcast_to([P, H, SEQ]),
                             dist[:].unsqueeze(1).broadcast_to([P, H, SEQ]), ALU.mult))
        done(e.tensor_scalar(k.a0_bq[:], k.a0_bq[:], 0.25, None, ALU.mult))
        done(e.tensor_scalar(k.c1_bq[:], k.c1_bq[:], 0.25, None, ALU.mult))
        e.wait_ge(s_am, 4)
        e.tensor_scalar(wsr[:], amax[:, 2:6], 1.0 / QMAX, QEPS, ALU.mult, ALU.max).then_inc(s_ws, 1)
        e.wait_ge(s_ws, 1)
        e.reciprocal(wrq[:, 2:6], wsr[:]).then_inc(s_ws, 1)
        e.wait_ge(s_ws, 2)
        for j in range(4):
            e.tensor_scalar(cnat[j // 2][:, j % 2, :], cnat[j // 2][:, j % 2, :], wrq[:, 2 + j:3 + j], ROUND,
                            ALU.mult, ALU.add).then_inc(s_q, 1)
            e.tensor_scalar(diag[:, j, :], k.ident[:], wsr[:, j:j + 1], None, ALU.mult).then_inc(s_q, 1)
        e.wait_ge(s_gm, 1)
        e.reciprocal(wrq[:, 0:2], k.gmax[:]).then_inc(s_ws, 1)
        done(e.tensor_scalar(k.wscale[:], k.gmax[:], 1.0 / (QMAX * QMAX), None, ALU.mult))
        e.wait_ge(s_ws, 3)
        e.tensor_scalar(wrq[:, 0:2], wrq[:, 0:2], QMAX, None, ALU.mult).then_inc(s_ws, 1)
        e.wait_ge(s_ws, 4)
        e.tensor_scalar(w1f, w1f, wrq[:, 0:1], ROUND, ALU.mult, ALU.add).then_inc(s_q, 1)
        e.tensor_scalar(w2f, w2f, wrq[:, 1:2], ROUND, ALU.mult, ALU.add).then_inc(s_q, 1)
        e.wait_ge(s_q, 10)
        done(e.tensor_scalar(k.w1q[:], w1f, ROUND, None, ALU.subtract))
        done(e.tensor_scalar(k.w2q[:], w2f, ROUND, None, ALU.subtract))
        for j in range(2):
            e.wait_ge(s_tr, j + 1)
            done(e.tensor_scalar((k.c1_wqq, k.c1_woq)[j][:].rearrange("p c (o n) -> p c o n", o=KC),
                                 k.ps[:, j, :].rearrange("p (o c n) -> p c o n", o=KC, c=KC),
                                 ROUND, None, ALU.subtract))
        e.wait_ge(s_mm, 1)
        done(e.tensor_scalar(k.c1_sq[:], k.ps[:, 2, 0:D], 0.25, None, ALU.mult))
        done(e.tensor_copy(k.c1_so[:], k.ps[:, 2, D:2 * D]))
        e.wait_ge(s_mm, 2)
        for i in range(2):
            done(e.tensor_copy(k.f_in[:, :, D * i:D * i + D], k.ps[:, 3 + i, :].rearrange("p (c n) -> p c n", c=KC)))
        done(e.tensor_copy(k.f_out[:, 0:2, :], k.ps[:, 5, :].rearrange("p (c n) -> p c n", c=2)))
        done(e.tensor_copy(k.f_out[:, 2, :], k.ps[:, 6, 0:D]))
        assert n_done[0] == N_READY
        e.wait_ge(s_ev, N_READY)
        e.wait_ge(s_ld2, 16 * NX)

    def tensor(e):
        e.wait_ge(s_ld, n_loads)
        e.wait_ge(s_fill, 2)
        e.wait_ge(s_q, 8)
        for j in range(2):
            for o in range(KC):
                for c in range(KC):
                    m = e.transpose(k.ps[:, j, (o * KC + c) * P:(o * KC + c + 1) * P],
                                    cnat[j][:, o, c * P:(c + 1) * P], k.ident[:])
            m.then_inc(s_tr, 1)
        for j in range(4):
            m = e.matmul(k.ps[:, 2, j * P:(j + 1) * P], k.ones[:], diag[:, j, :], start=True, stop=True)
        m.then_inc(s_mm, 1)
        for i, n in enumerate(("f_wq", "f_wkv")):
            for c in range(KC):
                for f in range(KC):
                    m = e.matmul(k.ps[:, 3 + i, c * D:(c + 1) * D], fnat[n][:, f, c * P:(c + 1) * P],
                                 fnat["dft"][:, f, :], start=(f == 0), stop=(f == KC - 1))
        for c in range(3):
            for f in range(KC):
                m = e.matmul(k.ps[:, 5 + c // 2, c % 2 * D:(c % 2 + 1) * D], idft[:, f, c * P:(c + 1) * P],
                             fnat["f_wo"][:, f, :], start=(f == 0), stop=(f == KC - 1))
        m.then_inc(s_mm, 1)
        e.wait_ge(k.w_done, N_READY)

    def scalar(e):
        e.wait_ge(s_ld, n_loads)
        e.wait_ge(k.w_done, N_READY)

    return {"sync": load, "gpsimd": pool, "vector": vector, "tensor": tensor, "scalar": scalar}


def heads_attention(k, ph, cross):
    nc, io, sb, ps = k.nc, k.io, k.sb, k.ps
    b = ph * NT
    name = f"h{ph}_"
    if not cross:
        k.heads = Named()
        (k.heads.kproj, k.heads.vproj, k.heads.q_out, k.heads.k_out, k.heads.v_out, k.heads.scored,
            k.heads.biased, k.heads.maxed, k.heads.shifted, k.heads.exped, k.heads.summed, k.heads.inverted,
            k.heads.turned, k.heads.p_a, k.heads.p_v, k.heads.weighed, k.heads.o_norm, k.heads.o_turned,
            k.heads.ot_out, k.heads.y_done, k.heads.bias_in) = (
            k.sem("h_" + n) for n in ("kproj", "vproj", "q_out", "k_out", "v_out", "scored", "biased", "maxed",
            "shifted", "exped", "summed", "inverted", "turned", "p_a", "p_v", "weighed", "o_norm", "o_turned",
            "ot_out", "y_done", "bias_in"))
    s = k.heads
    base = NT if cross else 0
    if cross:
        cs = Named()
        (cs.o_out, cs.v_bias, cs.o_max, cs.o_scale, cs.o_inv, cs.y_scaled) = (
            k.sem("hc_" + n) for n in ("o_out", "v_bias", "o_max", "o_scale", "o_inv", "y_scaled"))
    loaded = [k.sem(name + "loaded_even"), k.sem(name + "loaded_odd")]
    S, PT, QK, V, O, Y = ps[:, 0:2, :], ps[:, 2:4, :], ps[:, 4, :], ps[:, 5, :], ps[:, 6, 0:D], ps[:, 7, :]
    OT, YY = Y[:, 0:D], Y[:, D:2 * D]
    wk, wv = (k.c1["wk"], k.c1["wv"]) if cross else (k.a0["wk"], k.a0["wv"])
    bk = k.c1_bk if cross else k.a0_bk

    n_in = 3 if cross else 1

    def sync(e):
        def step(t, p):
            if live(t, 0):
                if past(t - 1):
                    e.wait_ge(s.vproj, base + t - 1)
                if cross:
                    if past(t - 1):
                        e.wait_ge(s.scored, base + t - 1)
                    if past(t - 1):
                        e.wait_ge(s.biased, base + t - 1)
                e.dma_start(k.xt[:, p], io["ctx_t" if cross else "x_t"][t]).then_inc(loaded[p], 16)
                if cross:
                    e.wait_ge(k.q_ready, NT)
                    e.dma_start(k.qt[:, p], k.q_all[:, t]).then_inc(loaded[p], 16)
                    e.dma_start(k.msk[:, p], io["mask"][t]).then_inc(loaded[p], 16)
        over_tiles(e, 2, step)

    def tensor(e):
        def step(t, p):
            q = 1 - p
            if live(t, 1):
                apart(k, e, base + t, base + t - 1)
                if not cross:
                    e.wait_ge(s.q_out, base + t)
                e.wait_ge(s.k_out, base + t)
                if past(t - 1):
                    e.wait_ge(s.biased, base + t - 1)
                for rg in range(2):
                    for c in range(KC):
                        for bt in range(2):
                            rows = slice(64 * rg, 64 * rg + 64)
                            m = e.matmul(S[64 * bt:64 * bt + 64, rg, c * D:(c + 1) * D],
                                         k.qt[rows, q, c, 64 * bt:64 * bt + 64],
                                         k.kt[rows, c, :, 64 * bt:64 * bt + 64], start=True, stop=True)
                m.then_inc(s.scored, 1)
            if live(t, 2):
                e.wait_ge(s.exped, base + t - 1)
                if past(t - 2):
                    e.wait_ge(s.p_a, base + t - 2)
                if past(t - 2):
                    e.wait_ge(s.p_v, base + t - 2)
                for n in range(8):
                    m = e.transpose(PT[:, n // 4, n % 4 * P:(n % 4 + 1) * P], k.sc[:, p, 2 * n:2 * n + 2, :], k.ident[:])
                m.then_inc(s.turned, 1)
            if live(t, 0):
                e.wait_ge(loaded[p], landed(t, p, n_in))
                if not cross:
                    if past(t):
                        e.wait_ge(s.q_out, base + t)
                if past(t):
                    e.wait_ge(s.k_out, base + t)
                for o, wt in ((0, None if cross else k.a0["wq"]), (1, wk)):
                    if wt is None:
                        continue
                    for c in range(KC):
                        for i in range(KC):
                            m = e.matmul(QK[:, (2 * o + c) * P:(2 * o + c + 1) * P], wt[:, i, c * P:(c + 1) * P],
                                         k.xt[:, p, i, :, 0, :], start=(i == 0), stop=(i == KC - 1))
                m.then_inc(s.kproj, 1)
            if live(t, 2):
                e.wait_ge(s.p_a, base + t - 1)
                e.wait_ge(s.p_v, base + t - 1)
                e.wait_ge(s.v_out, base + t - 1)
                if past(t - 2):
                    e.wait_ge(s.o_norm, base + t - 2)
                for n in range(8):
                    for bt in range(2):
                        m = e.matmul(O[64 * bt:64 * bt + 64, 32 * n:32 * n + 32], k.pt[:, n, 64 * bt:64 * bt + 64],
                                     k.vb[:, p, bt, 32 * n:32 * n + 32], start=True, stop=True)
                m.then_inc(s.weighed, 1)
            if live(t, 0):
                if past(t):
                    e.wait_ge(s.v_out, base + t)
                for bt in range(2):
                    for i in range(KC):
                        m = e.matmul(V[:, bt * D:(bt + 1) * D], k.xt[:, p, i, bt], wv[:, i, :], start=(i == 0), stop=(i == KC - 1))
                m.then_inc(s.vproj, 1)
            if live(t, 2):
                if cross:
                    e.wait_ge(cs.o_out, t - 1)
                else:
                    e.wait_ge(s.o_norm, base + t - 1)
                if past(b + t - 2):
                    e.wait_ge(k.ln_sum, b + t - 2)
                for c in range(KC):
                    m = e.transpose(OT[:, c * P:(c + 1) * P], k.on[:, c * P:(c + 1) * P], k.ident[:])
                m.then_inc(s.o_turned, 1)
                e.wait_ge(s.ot_out, base + t - 1)
                for c in range(KC):
                    m = e.matmul(YY, (k.xtq if cross else k.ot)[:, c, :], (k.c1_woq if cross else k.a0["wo"])[:, c, :],
                                 start=(c == 0), stop=(c == KC - 1))
                m.then_inc(s.y_done, 1)
        over_tiles(e, 2, step)
        e.wait_ge(k.x_ready, b + NT)

    def scalar(e):
        def step(t, p):
            q = 1 - p
            if live(t, 2):
                e.wait_ge(s.turned, base + t - 1)
                if past(t - 2):
                    e.wait_ge(s.weighed, base + t - 2)
                nc.scalar.copy(k.pt[:, 0:4, :], PT[:, 0, :].rearrange("p (n i) -> p n i", n=4)).then_inc(s.p_a, 1)
            if live(t, 0) and not cross:
                e.wait_ge(s.k_out, base + t + 1)
                if past(t):
                    e.wait_ge(s.scored, base + t)
                for c in range(KC):
                    m = nc.scalar.activation(k.qt[:, p, c, :], QK[:, c * P:(c + 1) * P], ACT.Identity,
                                             bias=k.a0_bq[:, c:c + 1], scale=0.25)
                m.then_inc(s.q_out, 1)
            if live(t, 1):
                e.wait_ge(s.shifted, base + t)
                nc.scalar.activation(k.sc[:, q], k.sc[:, q], ACT.Exp).then_inc(s.exped, 1)
            if live(t, 2):
                e.wait_ge(s.o_turned, base + t - 1)
                if past(t - 2):
                    e.wait_ge(s.y_done, base + t - 2)
                if cross:
                    nc.scalar.activation(k.xtq[:], OT.rearrange("p (c n) -> p c n", c=KC), ACT.Copy,
                                         bias=-ROUND).then_inc(s.ot_out, 1)
                else:
                    for c in range(KC):
                        m = nc.scalar.activation(k.ot[:, c, :], OT[:, c * P:(c + 1) * P], ACT.Identity,
                                                 bias=k.a0_bv[:, c:c + 1])
                    m.then_inc(s.ot_out, 1)
            if live(t, 0):
                e.wait_ge(s.vproj, base + t + 1)
                if past(t - 1):
                    e.wait_ge(s.weighed, base + t - 1)
                for hh in range(2):
                    vv = V.rearrange("p (b g h d) -> p b g h d", b=2, g=8, h=2)[:, :, :, hh, :]
                    oo = k.vb[:, p].rearrange("p b (g h d) -> p b g h d", g=8, h=2)[:, :, :, hh, :]
                    m = nc.scalar.activation(oo, vv, ACT.Copy, scale=k.mask2[:, hh:hh + 1])
                m.then_inc(s.v_out, 1)
        over_tiles(e, 2, step)

    def vector(e):
        def step(t, p):
            q = 1 - p
            if live(t, 1):
                e.wait_ge(s.scored, base + t)
                if past(t - 2):
                    e.wait_ge(s.turned, base + t - 2)
                if past(t - 2):
                    e.wait_ge(s.inverted, base + t - 2)
                if cross:
                    other = k.msk[:, q].unsqueeze(1).broadcast_to([P, H, SEQ])
                else:
                    other = k.alibi[:]
                e.tensor_tensor(k.sc[:, q], S.rearrange("p r (h j) -> p (r h) j", j=SEQ), other,
                                ALU.add).then_inc(s.biased, 1)
                e.wait_ge(s.biased, base + t)
                e.tensor_reduce(k.mx[:, q], k.sc[:, q], X, ALU.max).then_inc(s.maxed, 1)
            if live(t, 2):
                e.wait_ge(s.turned, base + t - 1)
                if past(t - 2):
                    e.wait_ge(s.weighed, base + t - 2)
                e.tensor_copy(k.pt[:, 4:8, :], PT[:, 1, :].rearrange("p (n i) -> p n i", n=4)).then_inc(s.p_v, 1)
            if live(t, 0):
                e.wait_ge(s.kproj, base + t + 1)
                if past(t):
                    e.wait_ge(s.scored, base + t)
                for c in range(KC):
                    m = e.scalar_tensor_tensor(
                        out=k.kt[:, c], in0=QK[:, (2 + c) * P:(3 + c) * P].unsqueeze(1).broadcast_to([P, HQ, P]),
                        scalar=bk[:, c:c + 1], in1=k.mask4[:].unsqueeze(2).broadcast_to([P, HQ, P]),
                        op0=ALU.add, op1=ALU.mult)
                m.then_inc(s.k_out, 1)
            if live(t, 2):
                e.wait_ge(s.weighed, base + t - 1)
                e.wait_ge(s.inverted, base + t - 1)
                if past(t - 2):
                    e.wait_ge(s.o_turned, base + t - 2)
                m = e.tensor_tensor(k.on[:].rearrange("p (h d) -> p h d", h=H), O.rearrange("p (h d) -> p h d", h=H),
                                    k.ri[:, p].unsqueeze(2).broadcast_to([P, H, HD]), ALU.mult)
                m.then_inc(s.o_norm, 1)
                if cross:
                    e.wait_ge(s.o_norm, base + t - 1)
                    e.tensor_tensor(k.on[:], k.on[:], k.c1_bv[:], ALU.add).then_inc(cs.v_bias, 1)
                    e.wait_ge(cs.v_bias, t - 1)
                    e.tensor_reduce(k.om[:, p, 0:1], k.on[:], X, ALU.max, apply_absolute_value=True).then_inc(cs.o_max, 1)
                    e.wait_ge(cs.o_max, t - 1)
                    e.tensor_scalar(k.om[:, p, 1:2], k.om[:, p, 0:1], 1.0 / QMAX, QEPS, ALU.mult,
                                    ALU.max).then_inc(cs.o_scale, 1)
                    e.wait_ge(cs.o_scale, t - 1)
                    e.reciprocal(k.om[:, p, 2:3], k.om[:, p, 1:2]).then_inc(cs.o_inv, 1)
                    e.wait_ge(cs.o_inv, t - 1)
                    e.tensor_scalar(k.on[:], k.on[:], k.om[:, p, 2:3], ROUND, ALU.mult, ALU.add).then_inc(cs.o_out, 1)
            if live(t, 1):
                e.wait_ge(s.exped, base + t)
                e.tensor_reduce(k.rs[:, q], k.sc[:, q], X, ALU.add).then_inc(s.summed, 1)
                e.wait_ge(s.summed, base + t)
                e.reciprocal(k.ri[:, q], k.rs[:, q]).then_inc(s.inverted, 1)
            if live(t, 2):
                e.wait_ge(s.y_done, base + t - 1)
                e.wait_ge(s.bias_in, base + t - 1)
                if cross:
                    e.scalar_tensor_tensor(out=k.r[:, p, :], in0=YY, scalar=k.om[:, p, 1:2], in1=k.c1_so[:],
                                           op0=ALU.mult, op1=ALU.mult).then_inc(cs.y_scaled, 1)
                    e.wait_ge(cs.y_scaled, t - 1)
                    e.tensor_tensor(k.r[:, p, :], k.r[:, p, :], k.x[:, t - 2, :], ALU.add).then_inc(k.ln_sum, 1)
                else:
                    e.tensor_tensor(k.r[:, p, :], YY, k.x[:, t - 2, :], ALU.add).then_inc(k.ln_sum, 1)
                norm_stats(k, e, ph, t - 2, p)
                norm_apply(k, e, ph, t - 2, p, k.x[:, t - 2, :])
        over_tiles(e, 2, step)

    def gpsimd(e):
        def step(t, p):
            q = 1 - p
            if live(t, 1):
                e.wait_ge(s.maxed, base + t)
                e.tensor_tensor(k.sc[:, q], k.sc[:, q], k.mx[:, q].unsqueeze(2).broadcast_to([P, H, SEQ]),
                                ALU.subtract).then_inc(s.shifted, 1)
            if live(t, 2):
                norm_rstd(k, e, ph, t - 2, p)
            if live(t, 0):
                if cross:
                    e.wait_ge(k.q_ready, NT)
                e.tensor_tensor(k.x[:, t, :], k.x[:, t, :], (k.c1_bo if cross else k.a0_bo)[:],
                                ALU.add).then_inc(s.bias_in, 1)
        over_tiles(e, 2, step)

    return {"sync": sync, "gpsimd": gpsimd, "vector": vector, "tensor": tensor, "scalar": scalar}


def quantised_queries(k, ph):
    nc, ps = k.nc, k.ps
    b = ph * NT
    s = Named()
    (s.maxed, s.scaled, s.inverted, s.rounded, s.turned, s.xt_out, s.projected, s.dequant, s.q_rows, s.q_turned) = (
        k.sem("qq_" + n) for n in ("maxed", "scaled", "inverted", "rounded", "turned", "xt_out", "projected",
        "dequant", "q_rows", "q_turned"))
    k.q_ready = k.sem("q_ready")
    XT, Q, QT = ps[:, 0, 0:D], ps[:, 1, 0:D], ps[:, 2, 0:D]

    def vector(e):
        if past(b):
            e.wait_ge(k.x_ready, b)

        def step(t, p):
            q = 1 - p
            if live(t, 0):
                if past(t - 1):
                    e.wait_ge(s.rounded, t - 1)
                e.tensor_reduce(k.om[:, p, 0:1], k.x[:, t, :], X, ALU.max, apply_absolute_value=True).then_inc(s.maxed, 1)
                e.wait_ge(s.maxed, t + 1)
                if past(t - 1):
                    e.wait_ge(s.dequant, t - 1)
                e.tensor_scalar(k.om[:, p, 1:2], k.om[:, p, 0:1], 1.0 / QMAX, QEPS, ALU.mult,
                                ALU.max).then_inc(s.scaled, 1)
                e.wait_ge(s.scaled, t + 1)
                e.reciprocal(k.om[:, p, 2:3], k.om[:, p, 1:2]).then_inc(s.inverted, 1)
                e.wait_ge(s.inverted, t + 1)
                if past(t - 1):
                    e.wait_ge(s.turned, t - 1)
                e.tensor_scalar(k.xs[:, p, :], k.x[:, t, :], k.om[:, p, 2:3], ROUND, ALU.mult,
                                ALU.add).then_inc(s.rounded, 1)
            if live(t, 1):
                e.wait_ge(s.projected, t)
                if past(t - 2):
                    e.wait_ge(s.q_turned, t - 2)
                e.scalar_tensor_tensor(out=k.r[:, q, :], in0=Q, scalar=k.om[:, q, 1:2], in1=k.c1_sq[:],
                                       op0=ALU.mult, op1=ALU.mult).then_inc(s.dequant, 1)
                e.wait_ge(s.dequant, t)
                e.tensor_tensor(k.r[:, q, :], k.r[:, q, :], k.c1_bq[:], ALU.add).then_inc(s.q_rows, 1)
        over_tiles(e, 2, step)

    def tensor(e):
        def step(t, p):
            if live(t, 1):
                e.wait_ge(s.xt_out, t)
                if past(t - 1):
                    e.wait_ge(s.dequant, t - 1)
                for c in range(KC):
                    m = e.matmul(Q, k.xtq[:, c, :], k.c1_wqq[:, c, :], start=(c == 0), stop=(c == KC - 1))
                m.then_inc(s.projected, 1)
            if live(t, 0):
                e.wait_ge(s.rounded, t + 1)
                if past(t):
                    e.wait_ge(s.xt_out, t)
                for c in range(KC):
                    m = e.transpose(XT[:, c * P:(c + 1) * P], k.xs[:, p, c * P:(c + 1) * P], k.ident[:])
                m.then_inc(s.turned, 1)
            if live(t, 2):
                e.wait_ge(s.q_rows, t - 1)
                if past(t - 2):
                    e.wait_ge(k.q_ready, t - 2)
                for c in range(KC):
                    m = e.transpose(QT[:, c * P:(c + 1) * P], k.r[:, p, c * P:(c + 1) * P], k.ident[:])
                m.then_inc(s.q_turned, 1)
        over_tiles(e, 2, step)
        e.wait_ge(k.q_ready, NT)

    def scalar(e):
        def step(t, p):
            if live(t, 0):
                e.wait_ge(s.turned, t + 1)
                if past(t):
                    e.wait_ge(s.projected, t)
                nc.scalar.activation(k.xtq[:], XT.rearrange("p (c n) -> p c n", c=KC), ACT.Copy,
                                     bias=-ROUND).then_inc(s.xt_out, 1)
            if live(t, 2):
                e.wait_ge(s.q_turned, t - 1)
                nc.scalar.copy(k.q_all[:, t - 2], QT.rearrange("p (c n) -> p c n", c=KC)).then_inc(k.q_ready, 1)
        over_tiles(e, 2, step)

    return {"vector": vector, "tensor": tensor, "scalar": scalar}


def wide_attention(k, ph):
    nc, io, sb, ps = k.nc, k.io, k.sb, k.ps
    b = ph * NT
    s = Named()
    (s.staged, s.x_turned, s.xt_out, s.qk, s.v, s.q_out, s.k_out, s.v_out, s.scored, s.maxed, s.negated,
        s.exped, s.inverted, s.turned, s.pt_out, s.weighed, s.o_out, s.y_done) = (
        k.sem("wa_" + n) for n in ("staged", "x_turned", "xt_out", "qk", "v", "q_out", "k_out", "v_out",
        "scored", "maxed", "negated", "exped", "inverted", "turned", "pt_out", "weighed", "o_out", "y_done"))
    s.ctx = [k.sem("wa_ctx_even"), k.sem("wa_ctx_odd")]
    kk = k.shared[:, 0:1024].rearrange("p (q c b o j) -> p q c b o j", q=2, c=KC, b=2, o=2)
    vv = k.shared[:, 1024:2048].rearrange("p (q b n) -> p q b n", q=2, b=2)
    pr, ptt = k.shared[:, 2048:2176], k.shared[:, 2176:2304]
    st = sb("wide_stats", [P, 2, 4])
    XT, V, S, PT, O, Y = (ps[:, 0, 0:D], ps[:, 2, :], ps[:, 3, 0:P], ps[:, 4, 0:P], ps[:, 5, 0:D],
                          ps[:, 6, 0:D])
    QK = (ps[:, 1, 0:D], ps[:, 7, 0:D])
    W, SCALE = k.c0, D ** -0.5

    def sync(e):
        def step(t, p):
            if live(t, 0):
                if past(t - 1):
                    e.wait_ge(s.scored, t - 1)
                if past(t - 1):
                    e.wait_ge(s.weighed, t - 1)
                for c in range(KC):
                    e.dma_start(kk[:, p, c, :, 0, :], io["ctx_t"][t, :, c, :, 0, :]).then_inc(s.ctx[p], 16)
                e.dma_start(vv[0:SEQ, p], io["ctx"][t]).then_inc(s.ctx[p], 16)
        over_tiles(e, 1, step)

    def gpsimd(e):
        def step(t, p):
            if live(t, 0):
                if past(b):
                    e.wait_ge(k.x_ready, b)
                if past(t - 1):
                    e.wait_ge(s.x_turned, t - 1)
                e.tensor_copy(k.xs[:, p, :], k.x[:, t, :]).then_inc(s.staged, 1)
            if live(t, 1):
                norm_rstd(k, e, ph, t - 1, 1 - p)
        over_tiles(e, 1, step)

    def tensor(e):
        def step(t, p):
            q = 1 - p
            if live(t, 0):
                e.wait_ge(s.staged, t + 1)
                if past(t):
                    e.wait_ge(s.xt_out, t)
                for c in range(KC):
                    m = e.transpose(XT[:, c * P:(c + 1) * P], k.xs[:, p, c * P:(c + 1) * P], k.ident[:])
                m.then_inc(s.x_turned, 1)
            if live(t, 1):
                e.wait_ge(s.q_out, t)
                e.wait_ge(s.k_out, t)
                e.wait_ge(s.ctx[q], landed(t - 1, q, 3))
                if past(t - 1):
                    e.wait_ge(s.exped, t - 1)
                for bt in range(2):
                    for c in range(KC):
                        m = e.matmul(S[64 * bt:64 * bt + 64, :], k.qt[:, 0, c, 64 * bt:64 * bt + 64],
                                     kk[:, q, c, bt], start=(c == 0), stop=(c == KC - 1))
                m.then_inc(s.scored, 1)
            if live(t, 0):
                e.wait_ge(s.xt_out, t + 1)
                if past(t):
                    e.wait_ge(s.q_out, t)
                if past(t):
                    e.wait_ge(s.k_out, t)
                for o, n in enumerate(("wq", "wk")):
                    for c in range(KC):
                        for i in range(KC):
                            m = e.matmul(QK[o][:, c * P:(c + 1) * P], W[n][:, i, c * P:(c + 1) * P],
                                         k.xt1[:, i, :], start=(i == 0), stop=(i == KC - 1))
                m.then_inc(s.qk, 1)
            if live(t, 1):
                e.wait_ge(s.exped, t)
                if past(t - 1):
                    e.wait_ge(s.pt_out, t - 1)
                e.transpose(PT, pr, k.ident[:]).then_inc(s.turned, 1)
            if live(t, 0):
                if past(t):
                    e.wait_ge(s.v_out, t)
                for bt in range(2):
                    for i in range(KC):
                        m = e.matmul(V[SEQ:P, bt * D:(bt + 1) * D], k.xt1[:, i, 64 * bt:64 * bt + 64],
                                     W["wv"][:, i, :], start=(i == 0), stop=(i == KC - 1))
                m.then_inc(s.v, 1)
            if live(t, 1):
                e.wait_ge(s.pt_out, t)
                e.wait_ge(s.v_out, t)
                if past(t - 1):
                    e.wait_ge(s.o_out, t - 1)
                for c in range(KC):
                    for bt in range(2):
                        m = e.matmul(O[:, c * P + 64 * bt:c * P + 64 * bt + 64], vv[:, q, bt, c * P:(c + 1) * P],
                                     ptt[:, 64 * bt:64 * bt + 64], start=True, stop=True)
                m.then_inc(s.weighed, 1)
                e.wait_ge(s.o_out, t)
                if past(b + t - 1):
                    e.wait_ge(k.ln_sum, b + t - 1)
                for c in range(KC):
                    m = e.matmul(Y, k.ot[:, c, :], W["wo"][:, c, :], start=(c == 0), stop=(c == KC - 1))
                m.then_inc(s.y_done, 1)
        over_tiles(e, 1, step)
        e.wait_ge(k.x_ready, b + NT)

    def scalar(e):
        def step(t, p):
            q = 1 - p
            if live(t, 0):
                e.wait_ge(s.x_turned, t + 1)
                if past(t):
                    e.wait_ge(s.v, t)
                nc.scalar.copy(k.xt1[:], XT.rearrange("p (c n) -> p c n", c=KC)).then_inc(s.xt_out, 1)
            if live(t, 1):
                e.wait_ge(s.negated, t)
                if past(t - 1):
                    e.wait_ge(s.turned, t - 1)
                nc.scalar.activation(pr, S, ACT.Exp, bias=st[:, q, 1:2], scale=SCALE,
                                     accum_out=st[:, q, 2:3]).then_inc(s.exped, 1)
            if live(t, 0):
                e.wait_ge(s.qk, t + 1)
                if past(t):
                    e.wait_ge(s.scored, t)
                nc.scalar.copy(k.qt[:, 0], QK[0].rearrange("p (c n) -> p c n", c=KC)).then_inc(s.q_out, 1)
            if live(t, 1):
                e.wait_ge(s.turned, t)
                if past(t - 1):
                    e.wait_ge(s.weighed, t - 1)
                nc.scalar.copy(ptt, PT).then_inc(s.pt_out, 1)
            if live(t, 0):
                e.wait_ge(s.v, t + 1)
                if past(t - 1):
                    e.wait_ge(s.weighed, t - 1)
                nc.scalar.copy(vv[SEQ:P, p], V[SEQ:P, :].rearrange("p (b n) -> p b n", b=2)).then_inc(s.v_out, 1)
        over_tiles(e, 1, step)

    def vector(e):
        def step(t, p):
            q = 1 - p
            if live(t, 1):
                e.wait_ge(s.scored, t)
                e.tensor_reduce(st[:, q, 0:1], S, X, ALU.max).then_inc(s.maxed, 1)
                e.wait_ge(s.maxed, t)
                e.tensor_scalar(st[:, q, 1:2], st[:, q, 0:1], -SCALE, None, ALU.mult).then_inc(s.negated, 1)
            if live(t, 0):
                e.wait_ge(s.qk, t + 1)
                if past(t - 1):
                    e.wait_ge(s.scored, t - 1)
                for c in range(KC):
                    m = e.tensor_copy(kk[:, p, c, :, 1, :], QK[1][:, c * P:(c + 1) * P].rearrange(
                        "p (b j) -> p b j", b=2))
                m.then_inc(s.k_out, 1)
            if live(t, 1):
                e.wait_ge(s.exped, t)
                e.reciprocal(st[:, q, 3:4], st[:, q, 2:3]).then_inc(s.inverted, 1)
                e.wait_ge(s.weighed, t)
                if past(t - 1):
                    e.wait_ge(s.y_done, t - 1)
                e.tensor_copy(k.ot[:], O.rearrange("p (c n) -> p c n", c=KC)).then_inc(s.o_out, 1)
                e.wait_ge(s.y_done, t)
                e.wait_ge(s.inverted, t)
                e.scalar_tensor_tensor(out=k.r[:, q, :], in0=Y, scalar=st[:, q, 3:4], in1=k.x[:, t - 1, :],
                                       op0=ALU.mult, op1=ALU.add).then_inc(k.ln_sum, 1)
                norm_stats(k, e, ph, t - 1, q)
                norm_apply(k, e, ph, t - 1, q, k.x[:, t - 1, :])
        over_tiles(e, 1, step)

    return {"sync": sync, "gpsimd": gpsimd, "vector": vector, "tensor": tensor, "scalar": scalar}


def quantised_ffn(k, ph):
    nc, ps = k.nc, k.ps
    b = ph * NT
    s = Named()
    (s.bias_in, s.maxed, s.inverted, s.scaled, s.out_scale, s.rounded, s.x_turned, s.xt_out, s.hidden, s.pre,
        s.gelu, s.h_max, s.h_inv, s.h_scale, s.h_out_scale, s.h_rounded, s.h_turned, s.ht_a, s.ht_v, s.y_done) = (
        k.sem("ff_" + n) for n in ("bias_in", "maxed", "inverted", "scaled", "out_scale", "rounded", "x_turned",
        "xt_out", "hidden", "pre", "gelu", "h_max", "h_inv", "h_scale", "h_out_scale", "h_rounded", "h_turned",
        "ht_a", "ht_v", "y_done"))
    ht = k.shared[:, 3968:4480].bitcast(BF16).rearrange("p (c n) -> p c n", c=F1 // P)
    fs = k.sb("ffn_scales", [P, 2, 8])
    XT, HB, HT, Y = ps[:, 0, 0:D], ps[:, 1:3, :], ps[:, 3:5, :], ps[:, 5, 0:D]

    def gpsimd(e):
        def step(t, p):
            if live(t, 2):
                norm_rstd(k, e, ph, t - 2, p)
            if live(t, 0):
                e.wait_ge(s.rounded, t + 1)
                e.tensor_tensor(k.x[:, t, :], k.x[:, t, :], k.b2[:], ALU.add).then_inc(s.bias_in, 1)
        over_tiles(e, 2, step)

    def scales(e, u, p, o, src, sem_in, maxed, inverted, scaled, out_scale, wscale, free):
        e.tensor_reduce(fs[:, p, o:o + 1], src, X, ALU.max, apply_absolute_value=True).then_inc(maxed, 1)
        e.wait_ge(maxed, u + 1)
        e.reciprocal(fs[:, p, o + 1:o + 2], fs[:, p, o:o + 1]).then_inc(inverted, 1)
        e.tensor_scalar(fs[:, p, o + 2:o + 3], fs[:, p, o:o + 1], wscale, None, ALU.mult).then_inc(out_scale, 1)
        e.wait_ge(inverted, u + 1)
        e.tensor_scalar(fs[:, p, o + 3:o + 4], fs[:, p, o + 1:o + 2], QMAX, None, ALU.mult).then_inc(scaled, 1)
        e.wait_ge(scaled, u + 1)

    def vector(e):
        if past(b):
            e.wait_ge(k.x_ready, b)

        def step(t, p):
            q = 1 - p
            if live(t, 1):
                e.wait_ge(s.hidden, t)
                e.wait_ge(s.out_scale, t)
                if past(t - 2):
                    e.wait_ge(s.h_turned, t - 2)
                e.scalar_tensor_tensor(out=k.wide[:, q], in0=HB.rearrange("p b n -> p (b n)"),
                                       scalar=fs[:, q, 2:3], in1=k.b1[:], op0=ALU.mult,
                                       op1=ALU.add).then_inc(s.pre, 1)
            if live(t, 0):
                scales(e, t, p, 0, k.x[:, t, :], None, s.maxed, s.inverted, s.scaled, s.out_scale,
                       k.wscale[:, 0:1], None)
                if past(t - 1):
                    e.wait_ge(s.x_turned, t - 1)
                e.tensor_scalar(k.xs[:, p, :], k.x[:, t, :], fs[:, p, 3:4], ROUND, ALU.mult,
                                ALU.add).then_inc(s.rounded, 1)
            if live(t, 2):
                e.wait_ge(s.h_turned, t - 1)
                if past(t - 2):
                    e.wait_ge(s.y_done, t - 2)
                e.tensor_scalar(ht[:, 4:8, :], HT[:, 1, :].rearrange("p (n i) -> p n i", n=4), ROUND, None,
                                ALU.subtract).then_inc(s.ht_v, 1)
            if live(t, 1):
                e.wait_ge(s.gelu, t)
                scales(e, t - 1, q, 4, k.wide[:, q], None, s.h_max, s.h_inv, s.h_scale, s.h_out_scale,
                       k.wscale[:, 1:2], None)
                e.tensor_scalar(k.wide[:, q], k.wide[:, q], fs[:, q, 7:8], ROUND, ALU.mult,
                                ALU.add).then_inc(s.h_rounded, 1)
            if live(t, 2):
                e.wait_ge(s.y_done, t - 1)
                e.wait_ge(s.bias_in, t - 1)
                e.wait_ge(s.h_out_scale, t - 1)
                e.scalar_tensor_tensor(out=k.r[:, p, :], in0=Y, scalar=fs[:, p, 6:7], in1=k.x[:, t - 2, :],
                                       op0=ALU.mult, op1=ALU.add).then_inc(k.ln_sum, 1)
                norm_stats(k, e, ph, t - 2, p)
                norm_apply(k, e, ph, t - 2, p, k.x[:, t - 2, :])
        over_tiles(e, 2, step)

    def tensor(e):
        def step(t, p):
            q = 1 - p
            if live(t, 1):
                e.wait_ge(s.xt_out, t)
                if past(t - 1):
                    e.wait_ge(s.pre, t - 1)
                for n in range(2):
                    for c in range(KC):
                        m = e.matmul(HB[:, n, :], k.xtq[:, c, :], k.w1q[:, c, n * 512:(n + 1) * 512],
                                     start=(c == 0), stop=(c == KC - 1))
                m.then_inc(s.hidden, 1)
            if live(t, 2):
                e.wait_ge(s.h_rounded, t - 1)
                if past(t - 2):
                    e.wait_ge(s.ht_a, t - 2)
                if past(t - 2):
                    e.wait_ge(s.ht_v, t - 2)
                for n in range(F1 // P):
                    m = e.transpose(HT[:, n // 4, n % 4 * P:(n % 4 + 1) * P], k.wide[:, p, n * P:(n + 1) * P],
                                    k.ident[:])
                m.then_inc(s.h_turned, 1)
            if live(t, 0):
                e.wait_ge(s.rounded, t + 1)
                if past(t):
                    e.wait_ge(s.xt_out, t)
                for c in range(KC):
                    m = e.transpose(XT[:, c * P:(c + 1) * P], k.xs[:, p, c * P:(c + 1) * P], k.ident[:])
                m.then_inc(s.x_turned, 1)
            if live(t, 2):
                e.wait_ge(s.ht_a, t - 1)
                e.wait_ge(s.ht_v, t - 1)
                if past(b + t - 2):
                    e.wait_ge(k.ln_sum, b + t - 2)
                for n in range(F1 // P):
                    m = e.matmul(Y, ht[:, n, :], k.w2q[:, n, :], start=(n == 0), stop=(n == F1 // P - 1))
                m.then_inc(s.y_done, 1)
        over_tiles(e, 2, step)
        e.wait_ge(k.x_ready, b + NT)

    def scalar(e):
        def step(t, p):
            q = 1 - p
            if live(t, 2):
                e.wait_ge(s.h_turned, t - 1)
                if past(t - 2):
                    e.wait_ge(s.y_done, t - 2)
                nc.scalar.activation(ht[:, 0:4, :], HT[:, 0, :].rearrange("p (n i) -> p n i", n=4), ACT.Copy,
                                     bias=-ROUND).then_inc(s.ht_a, 1)
            if live(t, 1):
                e.wait_ge(s.pre, t)
                nc.scalar.activation(k.wide[:, q], k.wide[:, q], ACT.Gelu_apprx_tanh).then_inc(s.gelu, 1)
            if live(t, 0):
                e.wait_ge(s.x_turned, t + 1)
                if past(t):
                    e.wait_ge(s.hidden, t)
                nc.scalar.activation(k.xtq[:], XT.rearrange("p (c n) -> p c n", c=KC), ACT.Copy,
                                     bias=-ROUND).then_inc(s.xt_out, 1)
        over_tiles(e, 2, step)

    return {"gpsimd": gpsimd, "vector": vector, "tensor": tensor, "scalar": scalar}


def fourier_attention(k, ph):
    nc, ps = k.nc, k.ps
    b = ph * NT
    s = Named()
    (s.staged, s.x_turned, s.xt_out, s.projected, s.squared, s.norm2, s.inv, s.normed, s.q_turned, s.qt_out,
        s.cumulated, s.p_main, s.p_cross, s.p_sum, s.y_done) = (
        k.sem("fa_" + n) for n in ("staged", "x_turned", "xt_out", "projected", "squared", "norm2", "inv",
        "normed", "q_turned", "qt_out", "cumulated", "p_main", "p_cross", "p_sum", "y_done"))
    n2 = k.sb("norms", [P, 2, 2 * H])
    qk = k.shared[:, 2304:3328].rearrange("p (q n) -> p q n", q=2)
    pr = k.shared[:, 3328:3712].rearrange("p (c n) -> p c n", c=3)
    cr = k.shared[:, 3712:3968].rearrange("p (c n) -> p c n", c=2)
    sq = k.wide[:, 0, 0:2 * D]
    XT, A, QT, C, Y = ps[:, 0, 0:D], ps[:, 1, :], ps[:, 2, 0:D], ps[:, 3, 0:D], ps[:, 4, 0:D]

    def gpsimd(e):
        def step(t, p):
            q = 1 - p
            if live(t, 0):
                if past(b):
                    e.wait_ge(k.x_ready, b)
                if past(t - 1):
                    e.wait_ge(s.x_turned, t - 1)
                e.tensor_copy(k.xs[:, p, :], k.x[:, t, :]).then_inc(s.staged, 1)
            if live(t, 1):
                e.wait_ge(s.p_cross, 2 * t)
                if past(t - 1):
                    e.wait_ge(s.y_done, t - 1)
                e.tensor_tensor(pr[:, 2, :], cr[:, 0, :], cr[:, 1, :], ALU.add).then_inc(s.p_sum, 1)
            if live(t, 0):
                e.wait_ge(s.norm2, t + 1)
                e.tensor_tensor(n2[:, p], n2[:, p], k.half[:], ALU.pow).then_inc(s.inv, 1)
            if live(t, 1):
                norm_rstd(k, e, ph, t - 1, q)
        over_tiles(e, 1, step)

    def tensor(e):
        def step(t, p):
            q = 1 - p
            if live(t, 0):
                e.wait_ge(s.staged, t + 1)
                if past(t):
                    e.wait_ge(s.xt_out, t)
                for c in range(KC):
                    m = e.transpose(XT[:, c * P:(c + 1) * P], k.xs[:, p, c * P:(c + 1) * P], k.ident[:])
                m.then_inc(s.x_turned, 1)
            if live(t, 1):
                e.wait_ge(s.normed, t)
                if past(t - 1):
                    e.wait_ge(s.qt_out, t - 1)
                if past(2 * (t - 1)):
                    e.wait_ge(s.p_cross, 2 * (t - 1))
                if past(t - 1):
                    e.wait_ge(s.p_main, t - 1)
                for c in range(KC):
                    m = e.transpose(QT[:, c * P:(c + 1) * P], qk[:, q, c * P:(c + 1) * P], k.ident[:])
                m.then_inc(s.q_turned, 1)
                for c in range(KC):
                    m = e.matmul(C[:, c * P:(c + 1) * P], qk[:, q, D + c * P:D + (c + 1) * P], k.tri[:],
                                 start=True, stop=True)
                m.then_inc(s.cumulated, 1)
            if live(t, 0):
                e.wait_ge(s.xt_out, t + 1)
                if past(t):
                    e.wait_ge(s.normed, t)
                for i in range(KC):
                    m = e.matmul(A, k.xt1[:, i, :], k.f_in[:, i, :], start=(i == 0), stop=(i == KC - 1))
                m.then_inc(s.projected, 1)
            if live(t, 1):
                e.wait_ge(s.p_main, t)
                e.wait_ge(s.p_sum, t)
                if past(b + t - 1):
                    e.wait_ge(k.ln_sum, b + t - 1)
                for c in range(3):
                    m = e.matmul(Y, pr[:, c, :], k.f_out[:, c, :], start=(c == 0), stop=(c == 2))
                m.then_inc(s.y_done, 1)
        over_tiles(e, 1, step)
        e.wait_ge(k.x_ready, b + NT)

    def scalar(e):
        def step(t, p):
            if live(t, 0):
                e.wait_ge(s.x_turned, t + 1)
                if past(t):
                    e.wait_ge(s.projected, t)
                nc.scalar.copy(k.xt1[:], XT.rearrange("p (c n) -> p c n", c=KC)).then_inc(s.xt_out, 1)
            if live(t, 1):
                e.wait_ge(s.q_turned, t)
                if past(t - 1):
                    e.wait_ge(s.p_main, t - 1)
                if past(2 * (t - 1)):
                    e.wait_ge(s.p_cross, 2 * (t - 1))
                nc.scalar.copy(k.qt[:, 0], QT.rearrange("p (c n) -> p c n", c=KC)).then_inc(s.qt_out, 1)
            if live(t, 0):
                e.wait_ge(s.projected, t + 1)
                if past(t):
                    e.wait_ge(s.norm2, t)
                nc.scalar.activation(sq, A, ACT.Square).then_inc(s.squared, 1)
        over_tiles(e, 1, step)

    def vector(e):
        def step(t, p):
            q = 1 - p
            if live(t, 1):
                e.wait_ge(s.qt_out, t)
                e.wait_ge(s.cumulated, t)
                if past(t - 1):
                    e.wait_ge(s.y_done, t - 1)
                if past(t - 1):
                    e.wait_ge(s.p_sum, t - 1)
                e.tensor_tensor(cr[:, 0, :], k.qt[:, 0, 0, :], C[:, P:D], ALU.mult).then_inc(s.p_cross, 1)
                e.tensor_tensor(cr[:, 1, :], k.qt[:, 0, 1, :], C[:, 0:P], ALU.mult).then_inc(s.p_cross, 1)
                e.tensor_tensor(pr[:, 0:2, :], k.qt[:, 0], C.rearrange("p (c n) -> p c n", c=2),
                                ALU.mult).then_inc(s.p_main, 1)
            if live(t, 0):
                e.wait_ge(s.squared, t + 1)
                e.tensor_reduce(n2[:, p].rearrange("p (s h) -> p s h", s=2),
                                sq.rearrange("p (s r h) -> p s h r", s=2, h=H), X, ALU.add).then_inc(s.norm2, 1)
                e.wait_ge(s.inv, t + 1)
                if past(t - 1):
                    e.wait_ge(s.cumulated, t - 1)
                inv = n2[:, p].rearrange("p (s h) -> p s h", s=2).unsqueeze(2).broadcast_to([P, 2, 16, H])
                e.tensor_tensor(qk[:, p].rearrange("p (s r h) -> p s r h", s=2, h=H),
                                A.rearrange("p (s r h) -> p s r h", s=2, h=H), inv, ALU.mult).then_inc(s.normed, 1)
            if live(t, 1):
                e.wait_ge(s.y_done, t)
                e.tensor_tensor(k.r[:, q, :], Y, k.x[:, t - 1, :], ALU.add).then_inc(k.ln_sum, 1)
                norm_stats(k, e, ph, t - 1, q)
                norm_apply(k, e, ph, t - 1, q, k.x[:, t - 1, :])
        over_tiles(e, 1, step)

    return {"gpsimd": gpsimd, "vector": vector, "tensor": tensor, "scalar": scalar}


def router(k, ph):
    nc, sb, ps = k.nc, k.sb, k.ps
    b = ph * NT
    s = Named()
    (s.staged, s.x_turned, s.xt_out, s.logit, s.exped) = (
        k.sem("ro_" + n) for n in ("staged", "x_turned", "xt_out", "logit", "exped"))
    s.logged, s.chain, k.coef_ready = k.sem("ro_logged"), k.sem("ro_chain"), k.sem("coef_ready")
    NE = E8 + 1
    lg = sb("logits", [P, NT, NE])
    k.coef = sb("coef", [P, NT, NE])
    w8 = [k.wide[:, i // 2, 256 * (i % 2):256 * (i % 2) + 256].rearrange("p (t e) -> p t e", e=E8) for i in range(4)]
    m1, rank = sb("router_max", [P, NT]), k.rank
    XT, L = ps[:, 0, 0:D], ps[:, 1, 0:NE]

    def gpsimd(e):
        def step(t, p):
            if live(t, 0):
                if past(b):
                    e.wait_ge(k.x_ready, b)
                if past(t - 1):
                    e.wait_ge(s.x_turned, t - 1)
                e.tensor_copy(k.xs[:, p, :], k.x[:, t, :]).then_inc(s.staged, 1)
        over_tiles(e, 0, step)

    def tensor(e):
        def step(t, p):
            if live(t, 0):
                e.wait_ge(s.staged, t + 1)
                if past(t):
                    e.wait_ge(s.xt_out, t)
                for c in range(KC):
                    m = e.transpose(XT[:, c * P:(c + 1) * P], k.xs[:, p, c * P:(c + 1) * P], k.ident[:])
                m.then_inc(s.x_turned, 1)
                e.wait_ge(s.xt_out, t + 1)
                if past(t):
                    e.wait_ge(s.logged, t)
                for i in range(KC):
                    m = e.matmul(L, k.xt1[:, i, :], k.wr[:, i, :], start=(i == 0), stop=(i == KC - 1))
                m.then_inc(s.logit, 1)
        over_tiles(e, 0, step)
        e.wait_ge(s.logged, NT)

    def scalar(e):
        def step(t, p):
            if live(t, 0):
                e.wait_ge(s.x_turned, t + 1)
                if past(t):
                    e.wait_ge(s.logit, t)
                nc.scalar.copy(k.xt1[:], XT.rearrange("p (c n) -> p c n", c=KC)).then_inc(s.xt_out, 1)
        over_tiles(e, 0, step)
        e.wait_ge(s.chain, 2)
        nc.scalar.activation(w8[0], w8[0], ACT.Exp).then_inc(s.exped, 1)
        nc.scalar.activation(k.coef[:, :, E8], lg[:, :, E8], ACT.Exp, scale=-1.0).then_inc(s.exped, 1)

    def vector(e):
        n = [0]

        def link(ins):
            n[0] += 1
            ins.then_inc(s.chain, 1)
            e.wait_ge(s.chain, n[0])

        def step(t, p):
            if live(t, 0):
                e.wait_ge(s.logit, t + 1)
                e.tensor_copy(lg[:, t, :], L).then_inc(s.logged, 1)
        over_tiles(e, 0, step)
        e.wait_ge(s.logged, NT)
        wide = [P, NT, E8]
        m = m1[:].unsqueeze(2).broadcast_to(wide)
        by_rank = rank[:].unsqueeze(1).broadcast_to(wide)
        pr, w, one, two = w8
        link(e.tensor_reduce(m1[:], lg[:, :, 0:E8], X, ALU.max))
        link(e.tensor_tensor(pr, lg[:, :, 0:E8], m, ALU.subtract))
        e.wait_ge(s.exped, 2)
        link(e.tensor_reduce(m1[:], pr, X, ALU.add))
        link(e.reciprocal(m1[:], m1[:]))
        link(e.tensor_tensor(pr, pr, m, ALU.mult))
        link(e.tensor_scalar(k.coef[:, :, E8], k.coef[:, :, E8], 1.0, None, ALU.add))
        link(e.reciprocal(k.coef[:, :, E8], k.coef[:, :, E8]))
        link(e.tensor_copy(w, pr))
        for mark in (one, two):
            link(e.tensor_reduce(m1[:], w, X, ALU.max))
            link(e.tensor_tensor(mark, w, m, ALU.is_equal))
            link(e.tensor_tensor(mark, mark, by_rank, ALU.mult))
            link(e.tensor_reduce(m1[:], mark, X, ALU.max))
            link(e.tensor_tensor(mark, mark, m, ALU.is_equal))
            link(e.tensor_tensor(w, w, mark, ALU.subtract))
        link(e.tensor_tensor(one, one, two, ALU.add))
        link(e.tensor_tensor(k.coef[:, :, 0:E8], pr, one, ALU.mult))
        e.tensor_copy(m1[:], m1[:]).then_inc(k.coef_ready, 1)

    return {"gpsimd": gpsimd, "vector": vector, "tensor": tensor, "scalar": scalar}


def experts(k, ph):
    nc, io, ps = k.nc, k.io, k.ps
    b = ph * NT
    s = Named()
    (s.staged, s.coef_in, s.x_turned, s.xt_out, s.gate_up, s.silu, s.hidden, s.h_turned, s.ht_out, s.down) = (
        k.sem("ex_" + n) for n in ("staged", "coef_in", "x_turned", "xt_out", "gate_up", "silu", "hidden",
        "h_turned", "ht_out", "down"))
    s.stored = [k.sem("ex_stored_even"), k.sem("ex_stored_odd")]
    co = k.sb("coef_tile", [P, 2, E8 + 1])
    act = k.shared[:, 6400:7104].rearrange("p (q u n) -> p q u n", q=2, u=2)
    out = k.shared[:, 7104:7616].rearrange("p (q n) -> p q n", q=2)
    XT, Y = ps[:, 0, 0:D], ps[:, 7, 0:D]
    GU = [ps[:, 1:3, :], ps[:, 3:5, :]]
    HT = [ps[:, 5, :], ps[:, 6, :]]
    PAIRS, GROUPS = NU // 2, -(-NH // 4)
    chunks = [[(n, min(P, FH - n * P)) for n in range(4 * g, min(4 * g + 4, NH))] for g in range(GROUPS)]
    h, ht = k.h_rows, k.h_t

    def gpsimd(e):
        e.wait_ge(k.coef_ready, 1)

        def step(t, p):
            if live(t, 0):
                if past(t - 1):
                    e.wait_ge(s.x_turned, t - 1)
                e.tensor_copy(k.xs[:, p, :], k.x[:, t, :]).then_inc(s.staged, 1)
                if past(NU * (t - 1)):
                    e.wait_ge(s.hidden, NU * (t - 1))
                e.tensor_copy(co[:, p], k.coef[:, t, :]).then_inc(s.coef_in, 1)
            if live(t, 1):
                norm_rstd(k, e, ph, t - 1, 1 - p)
        over_tiles(e, 1, step)

    def tensor(e):
        def step(t, p):
            q = 1 - p
            if live(t, 0):
                e.wait_ge(s.staged, t + 1)
                if past(t):
                    e.wait_ge(s.xt_out, t)
                for c in range(KC):
                    m = e.transpose(XT[:, c * P:(c + 1) * P], k.xs[:, p, c * P:(c + 1) * P], k.ident[:])
                m.then_inc(s.x_turned, 1)
                e.wait_ge(s.xt_out, t + 1)
            for j in range(PAIRS):
                if live(t, 0):
                    if past(NU * t + 2 * j - 2):
                        e.wait_ge(s.hidden, NU * t + 2 * j - 2)
                    for u in range(2):
                        for i in range(KC):
                            m = e.matmul(GU[j % 2][:, u, 0:2 * FE], k.xt1[:, i, :], k.gu[:, i, 2 * j + u, :],
                                         start=(i == 0), stop=(i == KC - 1))
                    m.then_inc(s.gate_up, 1)
                if live(t, 1) and j >= 1:
                    g = j - 1
                    e.wait_ge(s.ht_out, GROUPS * (t - 1) + g + 1)
                    if g == 0:
                        if past(b + t - 1):
                            e.wait_ge(k.ln_sum, b + t - 1)
                    for n, rows in chunks[g]:
                        m = e.matmul(Y, ht[0:rows, n, :], k.dn[0:rows, n, :], start=(n == 0), stop=(n == NH - 1))
                    m.then_inc(s.down, 1)
                    if g == GROUPS - 1:
                        pass
                if live(t, 1) and j < GROUPS:
                    apart(k, e, NU * t, GROUPS * (t - 1) + j - 1)
                    e.wait_ge(s.hidden, NU * t)
                    if past(GROUPS * (t - 1) + j - 1):
                        e.wait_ge(s.ht_out, GROUPS * (t - 1) + j - 1)
                    for n, rows in chunks[j]:
                        m = e.transpose(HT[j % 2][0:rows, (n - 4 * j) * P:(n - 4 * j + 1) * P],
                                        h[:, q, n * P:n * P + rows], k.ident[:])
                    m.then_inc(s.h_turned, 1)
        over_tiles(e, 1, step)

    def scalar(e):
        def step(t, p):
            if live(t, 0):
                e.wait_ge(s.x_turned, t + 1)
                if past(PAIRS * t):
                    e.wait_ge(s.gate_up, PAIRS * t)
                nc.scalar.copy(k.xt1[:], XT.rearrange("p (c n) -> p c n", c=KC)).then_inc(s.xt_out, 1)
            for j in range(PAIRS):
                if live(t, 0):
                    e.wait_ge(s.gate_up, PAIRS * t + j + 1)
                    if past(NU * t + 2 * j - 2):
                        e.wait_ge(s.hidden, NU * t + 2 * j - 2)
                    nc.scalar.activation(act[:, j % 2], GU[j % 2][:, :, 0:FE], ACT.Silu).then_inc(s.silu, 1)
                if live(t, 1) and j < GROUPS:
                    e.wait_ge(s.h_turned, GROUPS * (t - 1) + j + 1)
                    if past(GROUPS * (t - 2) + j + 1):
                        e.wait_ge(s.down, GROUPS * (t - 2) + j + 1)
                    n0, nn, rows = chunks[j][0][0], len(chunks[j]), chunks[j][0][1]
                    nc.scalar.copy(ht[0:rows, n0:n0 + nn, :], HT[j % 2][0:rows, 0:nn * P].rearrange(
                        "p (n i) -> p n i", n=nn)).then_inc(s.ht_out, 1)
        over_tiles(e, 1, step)

    def vector(e):
        def step(t, p):
            q = 1 - p
            for j in range(PAIRS):
                if live(t, 0):
                    e.wait_ge(s.silu, PAIRS * t + j + 1)
                    if j == 0:
                        e.wait_ge(s.coef_in, t + 1)
                        if past(GROUPS * (t - 1)):
                            e.wait_ge(s.h_turned, GROUPS * (t - 1))
                    for u in range(2):
                        unit = 2 * j + u
                        e.scalar_tensor_tensor(out=h[:, p, unit * FE:(unit + 1) * FE], in0=act[:, j % 2, u, :],
                                               scalar=co[:, p, min(unit, E8):min(unit, E8) + 1],
                                               in1=GU[j % 2][:, u, FE:2 * FE], op0=ALU.mult,
                                               op1=ALU.mult).then_inc(s.hidden, 1)
            if live(t, 1):
                e.wait_ge(s.down, GROUPS * t)
                e.tensor_tensor(k.r[:, q, :], Y, k.x[:, t - 1, :], ALU.add).then_inc(k.ln_sum, 1)
                norm_stats(k, e, ph, t - 1, q)
                if not isinstance(t, int) or t >= 3:
                    if past(landed(t - 3, q, 1)):
                        e.wait_ge(s.stored[q], landed(t - 3, q, 1))
                norm_apply(k, e, ph, t - 1, q, out[:, q, :])
        over_tiles(e, 1, step)

    def sync(e):
        def step(t, p):
            if live(t, 1):
                e.wait_ge(k.x_ready, b + t)
                e.dma_start(io["out"][t - 1], out[:, 1 - p, :]).then_inc(s.stored[1 - p], 16)
        over_tiles(e, 1, step)
        for stored in s.stored:
            e.wait_ge(stored, 8 * NT)

    return {"sync": sync, "gpsimd": gpsimd, "vector": vector, "tensor": tensor, "scalar": scalar}


STAGES = 7


def decoder_kernel(nc, io):
    with ExitStack() as ctx:
        k = declare(nc, ctx, io)
        stages = [setup(k), heads_attention(k, 0, False), wide_attention(k, 1), quantised_ffn(k, 2),
                  fourier_attention(k, 3), quantised_queries(k, 4), heads_attention(k, 4, True),
                  router(k, 5), experts(k, 5)]
        block = ctx.enter_context(nc.Block())

        @block.sync
        def _(e):
            for st in stages:
                if "sync" in st:
                    st["sync"](e)

        @block.gpsimd
        def _(e):
            for st in stages:
                if "gpsimd" in st:
                    st["gpsimd"](e)

        @block.scalar
        def _(e):
            for st in stages:
                if "scalar" in st:
                    st["scalar"](e)

        @block.vector
        def _(e):
            for st in stages:
                if "vector" in st:
                    st["vector"](e)

        @block.tensor
        def _(e):
            for st in stages:
                if "tensor" in st:
                    st["tensor"](e)


def head_order():
    return [((c * 8 + rg * HQ + hh) * HD + d) for rg in range(2) for c in range(KC) for hh in range(HQ)
            for d in range(HD)]


def constants():
    i = np.arange(P)
    c = {"ident": np.eye(P), "mask4": (i[:, None] // HD) % HQ == np.arange(HQ)[None],
         "mask2": i[:, None] // SEQ == np.arange(2)[None],
         "dist": -np.abs((i % SEQ)[:, None] - np.arange(SEQ)[None]),
         "tri": (i[:, None] // SEQ == i[None] // SEQ) & (i[:, None] <= i[None]),
         "rank": np.tile(E8 - np.arange(E8), (P, 1))}
    dft, idft = np.zeros((D, D)), np.zeros((D, 3 * P))
    n = np.arange(HD)
    for h in range(H):
        f = h * HD + n
        for j in range(8):
            re, im = j * H + h, P + j * H + h
            cos, sin = np.cos(2 * np.pi * j * n / HD), np.sin(2 * np.pi * j * n / HD)
            if j == 0:
                dft[f, re], dft[f, im] = 0.25, 0.25 * (-1.0) ** n
                idft[f, re], idft[f, im] = 1 / HD, (-1.0) ** n / HD
            else:
                dft[f, re], dft[f, im] = 2 ** 0.5 / 4 * cos, -(2 ** 0.5) / 4 * sin
                idft[f, re], idft[f, im], idft[f, 2 * P + re] = cos / HD, -cos / HD, -sin / HD
    c["dft"], c["idft"] = (a.reshape(KC, P, -1).transpose(1, 0, 2) for a in (dft, idft))
    return {n: np.ascontiguousarray(a, dtype=np.float32) for n, a in c.items()}


def layouts(a):
    def wt(w):
        return w.T.reshape(-1, P, w.shape[0]).transpose(1, 0, 2)

    def nat(w):
        return w.reshape(-1, P, w.shape[1]).transpose(1, 0, 2)

    def col(v):
        return v.reshape(-1, P).T

    def row(v):
        return np.broadcast_to(v[None], (P, v.shape[0]))

    def tiles_t(x):
        x = x.reshape(NT, 2, SEQ, KC, P).transpose(0, 4, 3, 1, 2)[:, :, :, :, None]
        return np.broadcast_to(x, (NT, P, KC, 2, 2, SEQ))
    o = head_order()
    x, ctx = a["x"].reshape(-1, D), a["ctx_2048"].reshape(-1, D)
    up = np.concatenate([a["L1_ffn_Wu"].transpose(1, 0, 2), a["L1_ffn_Su"].reshape(D, NU - E8, FE)], 1)
    gate = np.concatenate([a["L1_ffn_Wg"].transpose(1, 0, 2), a["L1_ffn_Sg"].reshape(D, NU - E8, FE)], 1)
    gu = np.concatenate([gate, up], 2).reshape(KC, P, NU, 2 * FE).transpose(1, 0, 2, 3)
    dn = np.concatenate([a["L1_ffn_Wd"].reshape(-1, D), a["L1_ffn_Sd"]], 0)
    main = (NH - 1) * P
    out = {
        "x": x.reshape(NT, P, D).transpose(1, 0, 2), "x_t": tiles_t(x), "ctx_t": tiles_t(ctx),
        "ctx": ctx.reshape(NT, 2, SEQ, D).transpose(0, 2, 1, 3),
        "mask": a["mask_BxSxS2_ff0"].reshape(NT, P, SEQ),
        "a0_wq": wt(a["L0_attn_Wq"]), "a0_wk": wt(a["L0_attn_Wk"]), "a0_wv": wt(a["L0_attn_Wv"][o]),
        "a0_wo": wt(a["L0_attn_Wo"][:, o]), "a0_bq": col(a["L0_attn_bq"]), "a0_bk": col(a["L0_attn_bk"]),
        "a0_bv": col(a["L0_attn_bv"][o]), "a0_bo": row(a["L0_attn_bo"]),
        "slopes": row(a["L0_attn_slopes"].reshape(KC, 2, HQ).transpose(1, 0, 2).reshape(-1)),
        "c0_wq": wt(a["L0_xattn_wq"]), "c0_wk": wt(a["L0_xattn_wk"]), "c0_wv": wt(a["L0_xattn_wv"]),
        "c0_wo": wt(a["L0_xattn_wo"]),
        "w1": wt(a["L0_ffn_W1"]), "w2": wt(a["L0_ffn_W2"]), "b1": row(a["L0_ffn_B1"]), "b2": row(a["L0_ffn_B2"]),
        "f_wq": nat(a["L1_attn_W_q"]), "f_wkv": nat(a["L1_attn_W_kv"]), "f_wo": wt(a["L1_attn_W_o"]),
        "c1_wq": nat(a["L1_xattn_wq"]), "c1_wo": nat(a["L1_xattn_wo"][:, o]), "c1_wk": wt(a["L1_xattn_wk"]),
        "c1_wv": wt(a["L1_xattn_wv"][o]), "c1_bk": col(a["L1_xattn_bk"]), "c1_bq": row(a["L1_xattn_bq"]),
        "c1_bv": row(a["L1_xattn_bv"][o]), "c1_bo": row(a["L1_xattn_bo"]),
        "wr": nat(np.concatenate([a["L1_ffn_Wr"], a["L1_ffn_Wsg"]], 1)), "gu": gu,
        "dn": nat(dn[:main]), "dn_tail": dn[main:],
    }
    out = {n: np.ascontiguousarray(v) for n, v in out.items()}
    out.update(constants())
    return out


def kernel(**inputs):
    import concourse.bacc as _bacc
    from concourse.bass_utils import run_bass_kernel_spmd as _run

    nc = _bacc.Bacc("TRN2", target_bir_lowering=False, num_devices=1)
    arrays = layouts({n: np.asarray(v) for n, v in inputs.items()})
    io = {n: nc.dram_tensor(f"in_{n}", a.shape, mybir.dt.from_np(a.dtype), kind="ExternalInput").ap()
          for n, a in arrays.items()}
    io["out"] = nc.dram_tensor("out_0", (NT, P, D), F32, kind="ExternalOutput").ap()
    decoder_kernel(nc, io)
    r = _run(nc, [{f"in_{n}": a for n, a in arrays.items()}], core_ids=[0])
    return r.results[0]["out_0"].reshape(BATCH, SEQ, D)
```

```python
from contextlib import ExitStack

import numpy as np

import concourse.bass as bass
from concourse import mybir
from concourse.alu_op_type import AluOpType as ALU

F32 = mybir.dt.float32
BF16 = mybir.dt.bfloat16
ACT = mybir.ActivationFunctionType
X = mybir.AxisListType.X
XY = mybir.AxisListType.XY
ABSMAX = bass.bass_isa.ReduceOp.absmax

BATCH, SEQ, D = 64, 64, 256
P = 128
NT = BATCH * SEQ // P
KC = D // P
H, HD = 16, 16
HQ = 4
F1 = 1024
E8, FE, FS = 8, 176, 704
NU = E8 + FS // FE
FH = NU * FE
NH = -(-FH // P)
QMAX = 127.0
QEPS = 1e-8
EPS = 1e-5
ROUND = 1.5 * 2.0 ** 23
N_READY = 16


class Named:
    pass


def past(count):
    return not isinstance(count, int) or count > 0


def apart(k, eng, *counts):
    for count in counts:
        if not isinstance(count, int):
            eng.compute_val(count)
    eng.wait_ge(k.filled, 2)


def over_tiles(eng, skew, step):
    lead = 6 if skew > 3 else 4
    for t in range(lead):
        step(t, t % 2)
    with eng.Fori(lead, NT - 1, 2) as i:
        step(i, 0)
        step(i + 1, 1)
    for t in range(NT, NT + skew):
        step(t, t % 2)


def landed(u, parity, n):
    return 8 * n * (u - parity) + 16 * n


def live(t, s):
    return not isinstance(t, int) or 0 <= t - s < NT


def stage_rows(k, sp, t, p, staged, x_turned):
    if past(t - 1):
        sp.wait_ge(x_turned, t - 1)
    sp.dma_start(k.xs[:, p, :], k.x[:, t, :]).then_inc(staged[p], 16)


def declare(nc, ctx, io):
    def sb(name, shape, dt=F32):
        return ctx.enter_context(nc.sbuf_tensor(name, shape, dt))

    k = Named()
    k.nc, k.io, k.sb = nc, io, sb
    k.sem = lambda name: ctx.enter_context(nc.semaphore(name))
    k.ps = ctx.enter_context(nc.psum_tensor("ps", [P, 8, 512], F32))
    k.x = sb("x_res", [P, NT, D])
    k.shared = sb("shared", [P, 8192])
    k.q_all = k.shared[:].rearrange("p (t c n) -> p t c n", t=NT, c=KC)
    k.h_rows = k.shared[:, 0:2 * FH].rearrange("p (b n) -> p b n", b=2)
    k.h_t = k.shared[:, 2 * FH:2 * FH + NH * P].rearrange("p (c n) -> p c n", c=NH)
    k.ident = sb("ident", [P, P])
    k.ones = sb("ones", [P, P])
    k.mask4 = sb("mask4", [P, HQ])
    k.mask2 = sb("mask2", [P, 2])
    k.half = sb("minus_half", [P, 32])
    k.xs = sb("x_rows", [P, 2, D])
    k.xt1 = sb("x_turned", [P, KC, P])
    k.xtq = sb("x_turned_q", [P, KC, P], BF16)
    k.sc = sb("scores", [P, 2, H, SEQ])
    k.wide = k.sc[:].rearrange("p b h j -> p b (h j)")
    k.mx, k.ri = sb("row_max", [P, 2, H]), sb("row_inv", [P, H])
    k.pt = sb("probs_t", [P, 8, P])
    k.qt, k.kt = sb("q_t", [P, 2, KC, P]), sb("k_masked", [P, KC, HQ, P])
    k.vb = sb("v_pairs", [P, 2, 2, 8, 34])
    k.on, k.ot = sb("o_rows", [P, D]), sb("o_t", [P, KC, P])
    k.xt = sb("x_t", [P, 2, KC, 2, 2, SEQ])
    k.om = sb("o_quant", [P, 2, 4])
    k.msk = sb("mask_in", [P, 2, SEQ])
    k.r = sb("r", [P, 2, D])
    k.bn = sb("bn", [P, 2, 6])
    k.mv = sb("mv", [P, 2, 2])
    k.rstd = sb("rstd", [P, 2, 1])
    k.ln_sum, k.ln_stats, k.ln_mv, k.ln_eps, k.ln_rstd, k.x_ready = (
        k.sem("ln_" + n) for n in ("sum", "stats", "mv", "eps", "rstd", "x_ready"))
    return k


def norm_stats(k, dve, ph, u, p):
    dve.wait_ge(k.ln_sum, ph * NT + u + 1)
    dve.bn_stats(k.bn[:, p, :], k.r[:, p, :]).then_inc(k.ln_stats, 1)
    apart(k, dve, ph * NT + u + 1)
    dve.wait_ge(k.ln_stats, ph * NT + u + 1)
    dve.bn_aggr(k.mv[:, p, :], k.bn[:, p, :]).then_inc(k.ln_mv, 1)


def norm_rstd(k, pool, ph, u, p):
    apart(k, pool, ph * NT + u + 1)
    pool.wait_ge(k.ln_mv, ph * NT + u + 1)
    pool.tensor_scalar(k.rstd[:, p, :], k.mv[:, p, 1:2], EPS, None, ALU.add).then_inc(k.ln_eps, 1)
    pool.wait_ge(k.ln_eps, ph * NT + u + 1)
    pool.tensor_tensor(k.rstd[:, p, :], k.rstd[:, p, :], k.half[:, 0:1], ALU.pow).then_inc(k.ln_rstd, 1)


def norm_apply(k, dve, ph, u, p, out):
    dve.wait_ge(k.ln_rstd, ph * NT + u + 1)
    dve.tensor_scalar(out, k.r[:, p, :], k.mv[:, p, 0:1], k.rstd[:, p, :], ALU.subtract,
                      ALU.mult).then_inc(k.x_ready, 1)


def setup(k):
    nc, io, sb = k.nc, k.io, k.sb
    s_ld, s_ld2, s_fill = k.sem("w_loaded"), k.sem("x_loaded"), k.sem("filled")
    k.filled = s_fill
    k.s_ld2 = s_ld2
    loads = []

    def w(name, shape):
        t = sb("w_" + name, shape)
        loads.append((t, io[name]))
        return t
    k.a0 = {n: w("a0_" + n, [P, KC, D]) for n in ("wq", "wk", "wv", "wo")}
    k.a0_bq, k.a0_bk, k.a0_bv = (w("a0_" + n, [P, KC]) for n in ("bq", "bk", "bv"))
    k.a0_bo = w("a0_bo", [P, D])
    slopes, dist = w("slopes", [P, H]), w("dist", [P, SEQ])
    k.alibi = sb("alibi", [P, H, SEQ])
    k.c0 = {n: w("c0_" + n, [P, KC, D]) for n in ("wq", "wk", "wv", "wo")}
    k.w1q = sb("w1q", [P, KC, F1], BF16)
    k.w2q = sb("w2q", [P, F1 // P, D], BF16)
    k.b1, k.b2 = w("b1", [P, F1]), w("b2", [P, D])
    w1f = k.shared[:, 0:2048].rearrange("p (c n) -> p c n", c=KC)
    w2f = k.shared[:, 2048:4096].rearrange("p (c n) -> p c n", c=F1 // P)
    k.gmax, k.wscale = sb("gmax", [P, 2]), sb("wscale", [P, 2])
    amax, wrq = sb("amax", [P, 6]), sb("wrq", [P, 6])
    k.f_in, k.f_out = sb("f_in", [P, KC, 2 * D]), sb("f_out", [P, 3, D])
    k.tri = w("tri", [P, P])
    fnat = {n: k.shared[:, 4096 + 512 * i:4608 + 512 * i].rearrange("p (c n) -> p c n", c=KC)
            for i, n in enumerate(("f_wq", "f_wkv", "f_wo", "dft"))}
    idft = k.shared[:, 6144:6912].rearrange("p (c n) -> p c n", c=KC)
    k.c1 = {n: w("c1_" + n, [P, KC, D]) for n in ("wk", "wv")}
    k.c1_bk, k.c1_bq, k.c1_bv, k.c1_bo = (w("c1_bk", [P, KC]), w("c1_bq", [P, D]),
                                          w("c1_bv", [P, D]), w("c1_bo", [P, D]))
    k.c1_wqq, k.c1_woq = sb("c1_wqq", [P, KC, D], BF16), sb("c1_woq", [P, KC, D], BF16)
    k.c1_sq, k.c1_so = sb("c1_sq", [P, D]), sb("c1_so", [P, D])
    cnat = [k.shared[:, 6912:7424].rearrange("p (c n) -> p c n", c=KC),
            k.shared[:, 7424:7936].rearrange("p (c n) -> p c n", c=KC)]
    wsr = sb("wsr", [P, 4])
    diag = sb("diag", [P, 4, P])
    k.rank = w("rank", [P, E8])
    k.wr = w("wr", [P, KC, E8 + 1])
    k.gu = w("gu", [P, KC, NU, 2 * FE])
    k.dn = sb("w_dn", [P, NH, D])
    loads += [(w1f, io["w1"]), (w2f, io["w2"]), (idft, io["idft"]),
              (cnat[0], io["c1_wq"]), (cnat[1], io["c1_wo"])]
    loads += [(fnat[n], io[n]) for n in fnat]
    loads += [(k.ident, io["ident"]), (k.mask4, io["mask4"]), (k.mask2, io["mask2"])]
    loads += [(k.dn[:, 0:NH - 1, :], io["dn"]), (k.dn[0:FH - (NH - 1) * P, NH - 1, :], io["dn_tail"])]
    s_am, s_gm, s_ws, s_q, s_tr, s_ev = (k.sem("w_" + n) for n in
                                         ("absmax", "allmax", "scale", "quant", "turned", "done"))
    s_mm = k.sem("w_mm")
    k.w_done = s_ev
    NX = 8
    n_loads = 16 * len(loads)

    def load(sp):
        for i in range(NX):
            n = NT // NX
            sp.dma_start(k.x[:, n * i:n * (i + 1), :], io["x"][:, n * i:n * (i + 1), :]).then_inc(s_ld2, 16)
        for dst, src in loads:
            sp.dma_start(dst if isinstance(dst, bass.AP) else dst[:], src).then_inc(s_ld, 16)

    def pool(e):
        e.memset(k.half[:], -0.5).then_inc(s_fill, 1)
        e.memset(k.ones[:], 1.0).then_inc(s_fill, 1)
        e.wait_ge(s_am, 2)
        e.partition_all_reduce(k.gmax[:], amax[:, 0:2], P, ABSMAX).then_inc(s_gm, 1)
        e.wait_ge(s_ld2, 16 * NX)
        e.wait_ge(s_fill, 2)

    n_done = [0]

    def done(ins):
        ins.then_inc(s_ev, 1)
        n_done[0] += 1

    def vector(e):
        e.wait_ge(s_ld, n_loads)
        e.tensor_reduce(amax[:, 0:1], w1f, XY, ALU.max, apply_absolute_value=True).then_inc(s_am, 1)
        e.tensor_reduce(amax[:, 1:2], w2f, XY, ALU.max, apply_absolute_value=True).then_inc(s_am, 1)
        e.tensor_reduce(amax[:, 2:4], cnat[0], X, ALU.max, apply_absolute_value=True).then_inc(s_am, 1)
        e.tensor_reduce(amax[:, 4:6], cnat[1], X, ALU.max, apply_absolute_value=True).then_inc(s_am, 1)
        for q in range(2):
            done(e.tensor_copy(k.vb[:, q, :, :, 32:34], k.mask2[:].unsqueeze(1).unsqueeze(1).broadcast_to([P, 2, 8, 2])))
        done(e.tensor_tensor(k.alibi[:], slopes[:].unsqueeze(2).broadcast_to([P, H, SEQ]),
                             dist[:].unsqueeze(1).broadcast_to([P, H, SEQ]), ALU.mult))
        done(e.tensor_scalar(k.a0_bq[:], k.a0_bq[:], 0.25, None, ALU.mult))
        done(e.tensor_scalar(k.c1_bq[:], k.c1_bq[:], 0.25, None, ALU.mult))
        e.wait_ge(s_am, 4)
        e.tensor_scalar(wsr[:], amax[:, 2:6], 1.0 / QMAX, QEPS, ALU.mult, ALU.max).then_inc(s_ws, 1)
        e.wait_ge(s_ws, 1)
        e.reciprocal(wrq[:, 2:6], wsr[:]).then_inc(s_ws, 1)
        e.wait_ge(s_ws, 2)
        for j in range(4):
            e.tensor_scalar(cnat[j // 2][:, j % 2, :], cnat[j // 2][:, j % 2, :], wrq[:, 2 + j:3 + j], ROUND,
                            ALU.mult, ALU.add).then_inc(s_q, 1)
            e.tensor_scalar(diag[:, j, :], k.ident[:], wsr[:, j:j + 1], None, ALU.mult).then_inc(s_q, 1)
        e.wait_ge(s_gm, 1)
        e.reciprocal(wrq[:, 0:2], k.gmax[:]).then_inc(s_ws, 1)
        done(e.tensor_scalar(k.wscale[:], k.gmax[:], 1.0 / (QMAX * QMAX), None, ALU.mult))
        e.wait_ge(s_ws, 3)
        e.tensor_scalar(wrq[:, 0:2], wrq[:, 0:2], QMAX, None, ALU.mult).then_inc(s_ws, 1)
        e.wait_ge(s_ws, 4)
        e.tensor_scalar(w1f, w1f, wrq[:, 0:1], ROUND, ALU.mult, ALU.add).then_inc(s_q, 1)
        e.tensor_scalar(w2f, w2f, wrq[:, 1:2], ROUND, ALU.mult, ALU.add).then_inc(s_q, 1)
        e.wait_ge(s_q, 10)
        done(e.tensor_scalar(k.w1q[:], w1f, ROUND, None, ALU.subtract))
        done(e.tensor_scalar(k.w2q[:], w2f, ROUND, None, ALU.subtract))
        for j in range(2):
            e.wait_ge(s_tr, j + 1)
            done(e.tensor_scalar((k.c1_wqq, k.c1_woq)[j][:].rearrange("p c (o n) -> p c o n", o=KC),
                                 k.ps[:, j, :].rearrange("p (o c n) -> p c o n", o=KC, c=KC),
                                 ROUND, None, ALU.subtract))
        e.wait_ge(s_mm, 1)
        done(e.tensor_scalar(k.c1_sq[:], k.ps[:, 2, 0:D], 0.25, None, ALU.mult))
        done(e.tensor_copy(k.c1_so[:], k.ps[:, 2, D:2 * D]))
        e.wait_ge(s_mm, 2)
        for i in range(2):
            done(e.tensor_copy(k.f_in[:, :, D * i:D * i + D], k.ps[:, 3 + i, :].rearrange("p (c n) -> p c n", c=KC)))
        done(e.tensor_copy(k.f_out[:, 0:2, :], k.ps[:, 5, :].rearrange("p (c n) -> p c n", c=2)))
        done(e.tensor_copy(k.f_out[:, 2, :], k.ps[:, 6, 0:D]))
        assert n_done[0] == N_READY
        e.wait_ge(s_ev, N_READY)
        e.wait_ge(s_ld2, 16 * NX)

    def tensor(e):
        e.wait_ge(s_ld, n_loads)
        e.wait_ge(s_fill, 2)
        e.wait_ge(s_q, 8)
        for j in range(2):
            for o in range(KC):
                for c in range(KC):
                    m = e.transpose(k.ps[:, j, (o * KC + c) * P:(o * KC + c + 1) * P],
                                    cnat[j][:, o, c * P:(c + 1) * P], k.ident[:])
            m.then_inc(s_tr, 1)
        for j in range(4):
            m = e.matmul(k.ps[:, 2, j * P:(j + 1) * P], k.ones[:], diag[:, j, :], start=True, stop=True)
        m.then_inc(s_mm, 1)
        for i, n in enumerate(("f_wq", "f_wkv")):
            for c in range(KC):
                for f in range(KC):
                    m = e.matmul(k.ps[:, 3 + i, c * D:(c + 1) * D], fnat[n][:, f, c * P:(c + 1) * P],
                                 fnat["dft"][:, f, :], start=(f == 0), stop=(f == KC - 1))
        for c in range(3):
            for f in range(KC):
                m = e.matmul(k.ps[:, 5 + c // 2, c % 2 * D:(c % 2 + 1) * D], idft[:, f, c * P:(c + 1) * P],
                             fnat["f_wo"][:, f, :], start=(f == 0), stop=(f == KC - 1))
        m.then_inc(s_mm, 1)
        e.wait_ge(k.w_done, N_READY)

    def scalar(e):
        e.wait_ge(s_ld, n_loads)
        e.wait_ge(k.w_done, N_READY)

    return {"sync": load, "gpsimd": pool, "vector": vector, "tensor": tensor, "scalar": scalar}


def heads_attention(k, ph, cross):
    nc, io, sb, ps = k.nc, k.io, k.sb, k.ps
    b = ph * NT
    name = f"h{ph}_"
    if not cross:
        k.heads = Named()
        (k.heads.kproj, k.heads.vproj, k.heads.q_out, k.heads.k_out, k.heads.v_out, k.heads.scored,
            k.heads.biased, k.heads.maxed, k.heads.shifted, k.heads.exped, k.heads.inverted,
            k.heads.turned, k.heads.p_a, k.heads.weighed, k.heads.o_norm, k.heads.o_turned,
            k.heads.ot_out, k.heads.y_done, k.heads.bias_in) = (
            k.sem("h_" + n) for n in ("kproj", "vproj", "q_out", "k_out", "v_out", "scored", "biased", "maxed",
            "shifted", "exped", "inverted", "turned", "p_a", "weighed", "o_norm", "o_turned",
            "ot_out", "y_done", "bias_in"))
    s = k.heads
    base = NT if cross else 0
    if cross:
        cs = Named()
        (cs.o_out, cs.v_bias, cs.o_max, cs.o_scale, cs.o_inv, cs.y_scaled) = (
            k.sem("hc_" + n) for n in ("o_out", "v_bias", "o_max", "o_scale", "o_inv", "y_scaled"))
    loaded = [k.sem(name + "loaded_even"), k.sem(name + "loaded_odd")]
    S, PT, QK, V, O, Y = ps[:, 0:2, :], ps[:, 2:4, :], ps[:, 4, :], ps[:, 5, :], ps[:, 6, 0:272], ps[:, 7, :]
    O = O.rearrange("p (g n) -> p g n", g=8)
    OT, YY = Y[:, 0:D], Y[:, D:2 * D]
    wk, wv = (k.c1["wk"], k.c1["wv"]) if cross else (k.a0["wk"], k.a0["wv"])
    bk = k.c1_bk if cross else k.a0_bk

    n_in = 3 if cross else 1

    def sync(e):
        def step(t, p):
            if live(t, 0):
                if past(t - 1):
                    e.wait_ge(s.vproj, base + t - 1)
                if cross:
                    if past(t - 1):
                        e.wait_ge(s.scored, base + t - 1)
                    if past(t - 1):
                        e.wait_ge(s.biased, base + t - 1)
                e.dma_start(k.xt[:, p], io["ctx_t" if cross else "x_t"][t]).then_inc(loaded[p], 16)
                if cross:
                    e.wait_ge(k.q_ready, NT)
                    e.dma_start(k.qt[:, p], k.q_all[:, t]).then_inc(loaded[p], 16)
                    e.dma_start(k.msk[:, p], io["mask"][t]).then_inc(loaded[p], 16)
        over_tiles(e, 2, step)

    def tensor(e):
        def step(t, p):
            q = 1 - p
            if live(t, 1):
                apart(k, e, base + t, base + t - 1)
                if not cross:
                    e.wait_ge(s.q_out, base + t)
                e.wait_ge(s.k_out, base + t)
                if past(t - 1):
                    e.wait_ge(s.biased, base + t - 1)
                for rg in range(2):
                    for c in range(KC):
                        for bt in range(2):
                            rows = slice(64 * rg, 64 * rg + 64)
                            m = e.matmul(S[64 * bt:64 * bt + 64, rg, c * D:(c + 1) * D],
                                         k.qt[rows, q, c, 64 * bt:64 * bt + 64],
                                         k.kt[rows, c, :, 64 * bt:64 * bt + 64], start=True, stop=True)
                m.then_inc(s.scored, 1)
            if live(t, 2):
                e.wait_ge(s.exped, base + t - 1)
                if past(t - 2):
                    e.wait_ge(s.p_a, base + t - 2)
                for n in range(8):
                    m = e.transpose(PT[:, n // 4, n % 4 * P:(n % 4 + 1) * P], k.sc[:, p, 2 * n:2 * n + 2, :], k.ident[:])
                m.then_inc(s.turned, 1)
            if live(t, 0):
                e.wait_ge(loaded[p], landed(t, p, n_in))
                if not cross:
                    if past(t):
                        e.wait_ge(s.q_out, base + t)
                if past(t):
                    e.wait_ge(s.k_out, base + t)
                for o, wt in ((0, None if cross else k.a0["wq"]), (1, wk)):
                    if wt is None:
                        continue
                    for c in range(KC):
                        for i in range(KC):
                            m = e.matmul(QK[:, (2 * o + c) * P:(2 * o + c + 1) * P], wt[:, i, c * P:(c + 1) * P],
                                         k.xt[:, p, i, :, 0, :], start=(i == 0), stop=(i == KC - 1))
                m.then_inc(s.kproj, 1)
            if live(t, 2):
                e.wait_ge(s.p_a, base + t - 1)
                e.wait_ge(s.v_out, base + t - 1)
                if past(t - 2):
                    e.wait_ge(s.o_norm, base + t - 2)
                for n in range(8):
                    for bt in range(2):
                        m = e.matmul(O[64 * bt:64 * bt + 64, n, :], k.pt[:, n, 64 * bt:64 * bt + 64],
                                     k.vb[:, p, bt, n, :], start=True, stop=True)
                m.then_inc(s.weighed, 1)
            if live(t, 0):
                if past(t):
                    e.wait_ge(s.v_out, base + t)
                for bt in range(2):
                    for i in range(KC):
                        m = e.matmul(V[:, bt * D:(bt + 1) * D], k.xt[:, p, i, bt], wv[:, i, :], start=(i == 0), stop=(i == KC - 1))
                m.then_inc(s.vproj, 1)
            if live(t, 2):
                if cross:
                    e.wait_ge(cs.o_out, t - 1)
                else:
                    e.wait_ge(s.o_norm, base + t - 1)
                if past(b + t - 2):
                    e.wait_ge(k.ln_sum, b + t - 2)
                for c in range(KC):
                    m = e.transpose(OT[:, c * P:(c + 1) * P], k.on[:, c * P:(c + 1) * P], k.ident[:])
                m.then_inc(s.o_turned, 1)
                e.wait_ge(s.ot_out, base + t - 1)
                for c in range(KC):
                    m = e.matmul(YY, (k.xtq if cross else k.ot)[:, c, :], (k.c1_woq if cross else k.a0["wo"])[:, c, :],
                                 start=(c == 0), stop=(c == KC - 1))
                m.then_inc(s.y_done, 1)
        over_tiles(e, 2, step)
        e.wait_ge(k.x_ready, b + NT)

    def scalar(e):
        def step(t, p):
            q = 1 - p
            if live(t, 2):
                e.wait_ge(s.turned, base + t - 1)
                if past(t - 2):
                    e.wait_ge(s.weighed, base + t - 2)
                nc.scalar.copy(k.pt[:], PT.rearrange("p r (n i) -> p (r n) i", n=4)).then_inc(s.p_a, 1)
            if live(t, 0) and not cross:
                e.wait_ge(s.k_out, base + t + 1)
                if past(t):
                    e.wait_ge(s.scored, base + t)
                for c in range(KC):
                    m = nc.scalar.activation(k.qt[:, p, c, :], QK[:, c * P:(c + 1) * P], ACT.Identity,
                                             bias=k.a0_bq[:, c:c + 1], scale=0.25)
                m.then_inc(s.q_out, 1)
            if live(t, 1):
                e.wait_ge(s.shifted, base + t)
                nc.scalar.activation(k.sc[:, q], k.sc[:, q], ACT.Exp).then_inc(s.exped, 1)
            if live(t, 2):
                e.wait_ge(s.o_turned, base + t - 1)
                if past(t - 2):
                    e.wait_ge(s.y_done, base + t - 2)
                if cross:
                    nc.scalar.activation(k.xtq[:], OT.rearrange("p (c n) -> p c n", c=KC), ACT.Copy,
                                         bias=-ROUND).then_inc(s.ot_out, 1)
                else:
                    for c in range(KC):
                        m = nc.scalar.activation(k.ot[:, c, :], OT[:, c * P:(c + 1) * P], ACT.Identity,
                                                 bias=k.a0_bv[:, c:c + 1])
                    m.then_inc(s.ot_out, 1)
            if live(t, 0):
                e.wait_ge(s.vproj, base + t + 1)
                if past(t - 1):
                    e.wait_ge(s.weighed, base + t - 1)
                for hh in range(2):
                    vv = V.rearrange("p (b g h d) -> p b g h d", b=2, g=8, h=2)[:, :, :, hh, :]
                    oo = k.vb[:, p, :, :, HD * hh:HD * hh + HD]
                    m = nc.scalar.activation(oo, vv, ACT.Copy, scale=k.mask2[:, hh:hh + 1])
                m.then_inc(s.v_out, 1)
        over_tiles(e, 2, step)

    def vector(e):
        def step(t, p):
            q = 1 - p
            if live(t, 1):
                e.wait_ge(s.scored, base + t)
                if past(t - 2):
                    e.wait_ge(s.turned, base + t - 2)
                if cross:
                    other = k.msk[:, q].unsqueeze(1).broadcast_to([P, H, SEQ])
                else:
                    other = k.alibi[:]
                e.tensor_tensor(k.sc[:, q], S.rearrange("p r (h j) -> p (r h) j", j=SEQ), other,
                                ALU.add).then_inc(s.biased, 1)
                e.wait_ge(s.biased, base + t)
                e.tensor_reduce(k.mx[:, q], k.sc[:, q], X, ALU.max).then_inc(s.maxed, 1)
            if live(t, 3):
                norm_apply(k, e, ph, t - 3, q, k.x[:, t - 3, :])
            if live(t, 0):
                e.wait_ge(s.kproj, base + t + 1)
                if past(t):
                    e.wait_ge(s.scored, base + t)
                for c in range(KC):
                    m = e.scalar_tensor_tensor(
                        out=k.kt[:, c], in0=QK[:, (2 + c) * P:(3 + c) * P].unsqueeze(1).broadcast_to([P, HQ, P]),
                        scalar=bk[:, c:c + 1], in1=k.mask4[:].unsqueeze(2).broadcast_to([P, HQ, P]),
                        op0=ALU.add, op1=ALU.mult)
                m.then_inc(s.k_out, 1)
            if live(t, 2):
                e.wait_ge(s.weighed, base + t - 1)
                e.reciprocal(k.ri[:].rearrange("p (g h) -> p g h", g=8), O[:, :, 32:34]).then_inc(s.inverted, 1)
                e.wait_ge(s.inverted, base + t - 1)
                if past(t - 2):
                    e.wait_ge(s.o_turned, base + t - 2)
                inv = k.ri[:].rearrange("p (g h) -> p g h", g=8).unsqueeze(3).broadcast_to([P, 8, 2, HD])
                m = e.tensor_tensor(k.on[:].rearrange("p (g h d) -> p g h d", g=8, h=2),
                                    O[:, :, 0:32].rearrange("p g (h d) -> p g h d", h=2), inv, ALU.mult)
                m.then_inc(s.o_norm, 1)
                if cross:
                    e.wait_ge(s.o_norm, base + t - 1)
                    e.tensor_tensor(k.on[:], k.on[:], k.c1_bv[:], ALU.add).then_inc(cs.v_bias, 1)
                    e.wait_ge(cs.v_bias, t - 1)
                    e.tensor_reduce(k.om[:, p, 0:1], k.on[:], X, ALU.max, apply_absolute_value=True).then_inc(cs.o_max, 1)
                    e.wait_ge(cs.o_max, t - 1)
                    e.tensor_scalar(k.om[:, p, 1:2], k.om[:, p, 0:1], 1.0 / QMAX, QEPS, ALU.mult,
                                    ALU.max).then_inc(cs.o_scale, 1)
                    e.wait_ge(cs.o_scale, t - 1)
                    e.reciprocal(k.om[:, p, 2:3], k.om[:, p, 1:2]).then_inc(cs.o_inv, 1)
                    e.wait_ge(cs.o_inv, t - 1)
                    e.tensor_scalar(k.on[:], k.on[:], k.om[:, p, 2:3], ROUND, ALU.mult, ALU.add).then_inc(cs.o_out, 1)
            if live(t, 2):
                e.wait_ge(s.y_done, base + t - 1)
                e.wait_ge(s.bias_in, base + t - 1)
                if cross:
                    e.scalar_tensor_tensor(out=k.r[:, p, :], in0=YY, scalar=k.om[:, p, 1:2], in1=k.c1_so[:],
                                           op0=ALU.mult, op1=ALU.mult).then_inc(cs.y_scaled, 1)
                    e.wait_ge(cs.y_scaled, t - 1)
                    e.tensor_tensor(k.r[:, p, :], k.r[:, p, :], k.x[:, t - 2, :], ALU.add).then_inc(k.ln_sum, 1)
                else:
                    e.tensor_tensor(k.r[:, p, :], YY, k.x[:, t - 2, :], ALU.add).then_inc(k.ln_sum, 1)
                norm_stats(k, e, ph, t - 2, p)
        over_tiles(e, 3, step)

    def gpsimd(e):
        def step(t, p):
            q = 1 - p
            if live(t, 1):
                e.wait_ge(s.maxed, base + t)
                e.tensor_tensor(k.sc[:, q], k.sc[:, q], k.mx[:, q].unsqueeze(2).broadcast_to([P, H, SEQ]),
                                ALU.subtract).then_inc(s.shifted, 1)
            if live(t, 2):
                norm_rstd(k, e, ph, t - 2, p)
            if live(t, 0):
                if cross:
                    e.wait_ge(k.q_ready, NT)
                e.tensor_tensor(k.x[:, t, :], k.x[:, t, :], (k.c1_bo if cross else k.a0_bo)[:],
                                ALU.add).then_inc(s.bias_in, 1)
        over_tiles(e, 2, step)

    return {"sync": sync, "gpsimd": gpsimd, "vector": vector, "tensor": tensor, "scalar": scalar}


def quantised_queries(k, ph):
    nc, ps = k.nc, k.ps
    b = ph * NT
    s = Named()
    (s.maxed, s.scaled, s.inverted, s.rounded, s.turned, s.xt_out, s.projected, s.dequant, s.q_rows, s.q_turned) = (
        k.sem("qq_" + n) for n in ("maxed", "scaled", "inverted", "rounded", "turned", "xt_out", "projected",
        "dequant", "q_rows", "q_turned"))
    k.q_ready = k.sem("q_ready")
    XT, Q, QT = ps[:, 0, 0:D], ps[:, 1, 0:D], ps[:, 2, 0:D]

    def vector(e):
        if past(b):
            e.wait_ge(k.x_ready, b)

        def step(t, p):
            q = 1 - p
            if live(t, 0):
                if past(t - 1):
                    e.wait_ge(s.rounded, t - 1)
                e.tensor_reduce(k.om[:, p, 0:1], k.x[:, t, :], X, ALU.max, apply_absolute_value=True).then_inc(s.maxed, 1)
                e.wait_ge(s.maxed, t + 1)
                if past(t - 1):
                    e.wait_ge(s.dequant, t - 1)
                e.tensor_scalar(k.om[:, p, 1:2], k.om[:, p, 0:1], 1.0 / QMAX, QEPS, ALU.mult,
                                ALU.max).then_inc(s.scaled, 1)
                e.wait_ge(s.scaled, t + 1)
                e.reciprocal(k.om[:, p, 2:3], k.om[:, p, 1:2]).then_inc(s.inverted, 1)
                e.wait_ge(s.inverted, t + 1)
                if past(t - 1):
                    e.wait_ge(s.turned, t - 1)
                e.tensor_scalar(k.xs[:, p, :], k.x[:, t, :], k.om[:, p, 2:3], ROUND, ALU.mult,
                                ALU.add).then_inc(s.rounded, 1)
            if live(t, 1):
                e.wait_ge(s.projected, t)
                if past(t - 2):
                    e.wait_ge(s.q_turned, t - 2)
                e.scalar_tensor_tensor(out=k.r[:, q, :], in0=Q, scalar=k.om[:, q, 1:2], in1=k.c1_sq[:],
                                       op0=ALU.mult, op1=ALU.mult).then_inc(s.dequant, 1)
                e.wait_ge(s.dequant, t)
                e.tensor_tensor(k.r[:, q, :], k.r[:, q, :], k.c1_bq[:], ALU.add).then_inc(s.q_rows, 1)
        over_tiles(e, 2, step)

    def tensor(e):
        def step(t, p):
            if live(t, 1):
                e.wait_ge(s.xt_out, t)
                if past(t - 1):
                    e.wait_ge(s.dequant, t - 1)
                for c in range(KC):
                    m = e.matmul(Q, k.xtq[:, c, :], k.c1_wqq[:, c, :], start=(c == 0), stop=(c == KC - 1))
                m.then_inc(s.projected, 1)
            if live(t, 0):
                e.wait_ge(s.rounded, t + 1)
                if past(t):
                    e.wait_ge(s.xt_out, t)
                for c in range(KC):
                    m = e.transpose(XT[:, c * P:(c + 1) * P], k.xs[:, p, c * P:(c + 1) * P], k.ident[:])
                m.then_inc(s.turned, 1)
            if live(t, 2):
                e.wait_ge(s.q_rows, t - 1)
                if past(t - 2):
                    e.wait_ge(k.q_ready, t - 2)
                for c in range(KC):
                    m = e.transpose(QT[:, c * P:(c + 1) * P], k.r[:, p, c * P:(c + 1) * P], k.ident[:])
                m.then_inc(s.q_turned, 1)
        over_tiles(e, 2, step)
        e.wait_ge(k.q_ready, NT)

    def scalar(e):
        def step(t, p):
            if live(t, 0):
                e.wait_ge(s.turned, t + 1)
                if past(t):
                    e.wait_ge(s.projected, t)
                nc.scalar.activation(k.xtq[:], XT.rearrange("p (c n) -> p c n", c=KC), ACT.Copy,
                                     bias=-ROUND).then_inc(s.xt_out, 1)
            if live(t, 2):
                e.wait_ge(s.q_turned, t - 1)
                nc.scalar.copy(k.q_all[:, t - 2], QT.rearrange("p (c n) -> p c n", c=KC)).then_inc(k.q_ready, 1)
        over_tiles(e, 2, step)

    return {"vector": vector, "tensor": tensor, "scalar": scalar}


def wide_attention(k, ph):
    nc, io, sb, ps = k.nc, k.io, k.sb, k.ps
    b = ph * NT
    s = Named()
    (s.x_turned, s.xt_out, s.qk, s.v, s.q_out, s.k_out, s.v_out, s.scored, s.maxed, s.negated,
        s.exped, s.inverted, s.turned, s.pt_out, s.weighed, s.o_out, s.y_done) = (
        k.sem("wa_" + n) for n in ("x_turned", "xt_out", "qk", "v", "q_out", "k_out", "v_out",
        "scored", "maxed", "negated", "exped", "inverted", "turned", "pt_out", "weighed", "o_out", "y_done"))
    s.staged = [k.sem("wa_staged_even"), k.sem("wa_staged_odd")]
    s.ctx = [k.sem("wa_ctx_even"), k.sem("wa_ctx_odd")]
    kk = k.shared[:, 0:1024].rearrange("p (q c b o j) -> p q c b o j", q=2, c=KC, b=2, o=2)
    vv = k.shared[:, 1024:2048].rearrange("p (q b n) -> p q b n", q=2, b=2)
    pr, ptt = k.shared[:, 2048:2176], k.shared[:, 2176:2304]
    st = sb("wide_stats", [P, 2, 4])
    XT, V, S, PT, O, Y = (ps[:, 0, 0:D], ps[:, 2, :], ps[:, 3, 0:P], ps[:, 4, 0:P], ps[:, 5, 0:D],
                          ps[:, 6, 0:D])
    QK = (ps[:, 1, 0:D], ps[:, 7, 0:D])
    W, SCALE = k.c0, D ** -0.5

    def sync(e):
        if past(b):
            e.wait_ge(k.x_ready, b)

        def step(t, p):
            q = 1 - p
            if live(t, 0):
                stage_rows(k, e, t, p, s.staged, s.x_turned)
            if live(t, 1):
                if past(t - 2):
                    e.wait_ge(s.scored, t - 2)
                if past(t - 2):
                    e.wait_ge(s.weighed, t - 2)
                for c in range(KC):
                    e.dma_start(kk[:, q, c, :, 0, :], io["ctx_t"][t - 1, :, c, :, 0, :]).then_inc(s.ctx[q], 16)
                e.dma_start(vv[0:SEQ, q], io["ctx"][t - 1]).then_inc(s.ctx[q], 16)
        over_tiles(e, 4, step)

    def gpsimd(e):
        def step(t, p):
            if live(t, 3):
                norm_rstd(k, e, ph, t - 3, 1 - p)
        over_tiles(e, 4, step)

    def tensor(e):
        def step(t, p):
            q = 1 - p
            if live(t, 2):
                e.wait_ge(s.q_out, t - 1)
                e.wait_ge(s.k_out, t - 1)
                e.wait_ge(s.ctx[p], landed(t - 2, p, 3))
                if past(t - 2):
                    e.wait_ge(s.exped, t - 2)
                for bt in range(2):
                    for c in range(KC):
                        m = e.matmul(S[64 * bt:64 * bt + 64, :], k.qt[:, 0, c, 64 * bt:64 * bt + 64],
                                     kk[:, p, c, bt], start=(c == 0), stop=(c == KC - 1))
                m.then_inc(s.scored, 1)
            if live(t, 3):
                e.wait_ge(s.exped, t - 2)
                if past(t - 3):
                    e.wait_ge(s.pt_out, t - 3)
                e.transpose(PT, pr, k.ident[:]).then_inc(s.turned, 1)
            if live(t, 1):
                e.wait_ge(s.xt_out, t)
                if past(t - 1):
                    e.wait_ge(s.q_out, t - 1)
                if past(t - 1):
                    e.wait_ge(s.k_out, t - 1)
                for o, n in enumerate(("wq", "wk")):
                    for c in range(KC):
                        for i in range(KC):
                            m = e.matmul(QK[o][:, c * P:(c + 1) * P], W[n][:, i, c * P:(c + 1) * P],
                                         k.xt1[:, i, :], start=(i == 0), stop=(i == KC - 1))
                m.then_inc(s.qk, 1)
            if live(t, 3):
                e.wait_ge(s.pt_out, t - 2)
                e.wait_ge(s.v_out, t - 2)
                if past(t - 3):
                    e.wait_ge(s.o_out, t - 3)
                for c in range(KC):
                    for bt in range(2):
                        m = e.matmul(O[:, c * P + 64 * bt:c * P + 64 * bt + 64], vv[:, q, bt, c * P:(c + 1) * P],
                                     ptt[:, 64 * bt:64 * bt + 64], start=True, stop=True)
                m.then_inc(s.weighed, 1)
            if live(t, 1):
                if past(t - 1):
                    e.wait_ge(s.v_out, t - 1)
                for bt in range(2):
                    for i in range(KC):
                        m = e.matmul(V[SEQ:P, bt * D:(bt + 1) * D], k.xt1[:, i, 64 * bt:64 * bt + 64],
                                     W["wv"][:, i, :], start=(i == 0), stop=(i == KC - 1))
                m.then_inc(s.v, 1)
            if live(t, 0):
                e.wait_ge(s.staged[p], landed(t, p, 1))
                if past(t):
                    e.wait_ge(s.xt_out, t)
                for c in range(KC):
                    m = e.transpose(XT[:, c * P:(c + 1) * P], k.xs[:, p, c * P:(c + 1) * P], k.ident[:])
                m.then_inc(s.x_turned, 1)
            if live(t, 3):
                e.wait_ge(s.o_out, t - 2)
                if past(b + t - 3):
                    e.wait_ge(k.ln_sum, b + t - 3)
                for c in range(KC):
                    m = e.matmul(Y, k.ot[:, c, :], W["wo"][:, c, :], start=(c == 0), stop=(c == KC - 1))
                m.then_inc(s.y_done, 1)
        over_tiles(e, 4, step)
        e.wait_ge(k.x_ready, b + NT)

    def scalar(e):
        def step(t, p):
            q = 1 - p
            if live(t, 3):
                e.wait_ge(s.turned, t - 2)
                if past(t - 3):
                    e.wait_ge(s.weighed, t - 3)
                nc.scalar.copy(ptt, PT).then_inc(s.pt_out, 1)
            if live(t, 2):
                e.wait_ge(s.negated, t - 1)
                if past(t - 2):
                    e.wait_ge(s.turned, t - 2)
                nc.scalar.activation(pr, S, ACT.Exp, bias=st[:, p, 1:2], scale=SCALE,
                                     accum_out=st[:, p, 2:3]).then_inc(s.exped, 1)
            if live(t, 1):
                e.wait_ge(s.qk, t)
                if past(t - 1):
                    e.wait_ge(s.scored, t - 1)
                nc.scalar.copy(k.qt[:, 0], QK[0].rearrange("p (c n) -> p c n", c=KC)).then_inc(s.q_out, 1)
                e.wait_ge(s.v, t)
                if past(t - 2):
                    e.wait_ge(s.weighed, t - 2)
                nc.scalar.copy(vv[SEQ:P, q], V[SEQ:P, :].rearrange("p (b n) -> p b n", b=2)).then_inc(s.v_out, 1)
            if live(t, 0):
                e.wait_ge(s.x_turned, t + 1)
                if past(t):
                    e.wait_ge(s.v, t)
                nc.scalar.copy(k.xt1[:], XT.rearrange("p (c n) -> p c n", c=KC)).then_inc(s.xt_out, 1)
        over_tiles(e, 4, step)

    def vector(e):
        def step(t, p):
            q = 1 - p
            if live(t, 2):
                e.wait_ge(s.scored, t - 1)
                e.tensor_reduce(st[:, p, 0:1], S, X, ALU.max).then_inc(s.maxed, 1)
                e.wait_ge(s.maxed, t - 1)
                e.tensor_scalar(st[:, p, 1:2], st[:, p, 0:1], -SCALE, None, ALU.mult).then_inc(s.negated, 1)
            if live(t, 4):
                norm_apply(k, e, ph, t - 4, p, k.x[:, t - 4, :])
            if live(t, 3):
                e.wait_ge(s.exped, t - 2)
                e.reciprocal(st[:, q, 3:4], st[:, q, 2:3]).then_inc(s.inverted, 1)
            if live(t, 1):
                e.wait_ge(s.qk, t)
                if past(t - 2):
                    e.wait_ge(s.scored, t - 2)
                for c in range(KC):
                    m = e.tensor_copy(kk[:, q, c, :, 1, :], QK[1][:, c * P:(c + 1) * P].rearrange(
                        "p (b j) -> p b j", b=2))
                m.then_inc(s.k_out, 1)
            if live(t, 3):
                e.wait_ge(s.weighed, t - 2)
                if past(t - 3):
                    e.wait_ge(s.y_done, t - 3)
                e.tensor_copy(k.ot[:], O.rearrange("p (c n) -> p c n", c=KC)).then_inc(s.o_out, 1)
                e.wait_ge(s.y_done, t - 2)
                e.wait_ge(s.inverted, t - 2)
                e.scalar_tensor_tensor(out=k.r[:, q, :], in0=Y, scalar=st[:, q, 3:4], in1=k.x[:, t - 3, :],
                                       op0=ALU.mult, op1=ALU.add).then_inc(k.ln_sum, 1)
                norm_stats(k, e, ph, t - 3, q)
        over_tiles(e, 4, step)

    return {"sync": sync, "gpsimd": gpsimd, "vector": vector, "tensor": tensor, "scalar": scalar}


def quantised_ffn(k, ph):
    nc, ps = k.nc, k.ps
    b = ph * NT
    s = Named()
    (s.bias_in, s.maxed, s.inverted, s.scaled, s.out_scale, s.rounded, s.x_turned, s.xt_out, s.hidden, s.pre,
        s.gelu, s.h_max, s.h_inv, s.h_scale, s.h_out_scale, s.h_rounded, s.h_turned, s.ht_a, s.ht_v, s.y_done) = (
        k.sem("ff_" + n) for n in ("bias_in", "maxed", "inverted", "scaled", "out_scale", "rounded", "x_turned",
        "xt_out", "hidden", "pre", "gelu", "h_max", "h_inv", "h_scale", "h_out_scale", "h_rounded", "h_turned",
        "ht_a", "ht_v", "y_done"))
    ht = k.shared[:, 3968:4480].bitcast(BF16).rearrange("p (c n) -> p c n", c=F1 // P)
    fs = k.sb("ffn_scales", [P, 2, 8])
    XT, HB, HT, Y = ps[:, 0, 0:D], ps[:, 1:3, :], ps[:, 3:5, :], ps[:, 5, 0:D]

    def gpsimd(e):
        def step(t, p):
            if live(t, 2):
                norm_rstd(k, e, ph, t - 2, p)
            if live(t, 0):
                e.wait_ge(s.rounded, t + 1)
                e.tensor_tensor(k.x[:, t, :], k.x[:, t, :], k.b2[:], ALU.add).then_inc(s.bias_in, 1)
        over_tiles(e, 2, step)

    def scales(e, u, p, o, src, sem_in, maxed, inverted, scaled, out_scale, wscale, free):
        e.tensor_reduce(fs[:, p, o:o + 1], src, X, ALU.max, apply_absolute_value=True).then_inc(maxed, 1)
        e.wait_ge(maxed, u + 1)
        e.reciprocal(fs[:, p, o + 1:o + 2], fs[:, p, o:o + 1]).then_inc(inverted, 1)
        e.tensor_scalar(fs[:, p, o + 2:o + 3], fs[:, p, o:o + 1], wscale, None, ALU.mult).then_inc(out_scale, 1)
        e.wait_ge(inverted, u + 1)
        e.tensor_scalar(fs[:, p, o + 3:o + 4], fs[:, p, o + 1:o + 2], QMAX, None, ALU.mult).then_inc(scaled, 1)
        e.wait_ge(scaled, u + 1)

    def vector(e):
        if past(b):
            e.wait_ge(k.x_ready, b)

        def step(t, p):
            q = 1 - p
            if live(t, 1):
                e.wait_ge(s.hidden, t)
                e.wait_ge(s.out_scale, t)
                if past(t - 2):
                    e.wait_ge(s.h_turned, t - 2)
                e.scalar_tensor_tensor(out=k.wide[:, q], in0=HB.rearrange("p b n -> p (b n)"),
                                       scalar=fs[:, q, 2:3], in1=k.b1[:], op0=ALU.mult,
                                       op1=ALU.add).then_inc(s.pre, 1)
            if live(t, 3):
                norm_apply(k, e, ph, t - 3, q, k.x[:, t - 3, :])
            if live(t, 0):
                scales(e, t, p, 0, k.x[:, t, :], None, s.maxed, s.inverted, s.scaled, s.out_scale,
                       k.wscale[:, 0:1], None)
                if past(t - 1):
                    e.wait_ge(s.x_turned, t - 1)
                e.tensor_scalar(k.xs[:, p, :], k.x[:, t, :], fs[:, p, 3:4], ROUND, ALU.mult,
                                ALU.add).then_inc(s.rounded, 1)
            if live(t, 2):
                e.wait_ge(s.h_turned, t - 1)
                if past(t - 2):
                    e.wait_ge(s.y_done, t - 2)
                e.tensor_scalar(ht[:, 4:8, :], HT[:, 1, :].rearrange("p (n i) -> p n i", n=4), ROUND, None,
                                ALU.subtract).then_inc(s.ht_v, 1)
            if live(t, 1):
                e.wait_ge(s.gelu, t)
                scales(e, t - 1, q, 4, k.wide[:, q], None, s.h_max, s.h_inv, s.h_scale, s.h_out_scale,
                       k.wscale[:, 1:2], None)
                e.tensor_scalar(k.wide[:, q], k.wide[:, q], fs[:, q, 7:8], ROUND, ALU.mult,
                                ALU.add).then_inc(s.h_rounded, 1)
            if live(t, 2):
                e.wait_ge(s.y_done, t - 1)
                e.wait_ge(s.bias_in, t - 1)
                e.wait_ge(s.h_out_scale, t - 1)
                e.scalar_tensor_tensor(out=k.r[:, p, :], in0=Y, scalar=fs[:, p, 6:7], in1=k.x[:, t - 2, :],
                                       op0=ALU.mult, op1=ALU.add).then_inc(k.ln_sum, 1)
                norm_stats(k, e, ph, t - 2, p)
        over_tiles(e, 3, step)

    def tensor(e):
        def step(t, p):
            q = 1 - p
            if live(t, 1):
                e.wait_ge(s.xt_out, t)
                if past(t - 1):
                    e.wait_ge(s.pre, t - 1)
                for n in range(2):
                    for c in range(KC):
                        m = e.matmul(HB[:, n, :], k.xtq[:, c, :], k.w1q[:, c, n * 512:(n + 1) * 512],
                                     start=(c == 0), stop=(c == KC - 1))
                m.then_inc(s.hidden, 1)
            if live(t, 2):
                e.wait_ge(s.h_rounded, t - 1)
                if past(t - 2):
                    e.wait_ge(s.ht_a, t - 2)
                if past(t - 2):
                    e.wait_ge(s.ht_v, t - 2)
                for n in range(F1 // P):
                    m = e.transpose(HT[:, n // 4, n % 4 * P:(n % 4 + 1) * P], k.wide[:, p, n * P:(n + 1) * P],
                                    k.ident[:])
                m.then_inc(s.h_turned, 1)
            if live(t, 0):
                e.wait_ge(s.rounded, t + 1)
                if past(t):
                    e.wait_ge(s.xt_out, t)
                for c in range(KC):
                    m = e.transpose(XT[:, c * P:(c + 1) * P], k.xs[:, p, c * P:(c + 1) * P], k.ident[:])
                m.then_inc(s.x_turned, 1)
            if live(t, 2):
                e.wait_ge(s.ht_a, t - 1)
                e.wait_ge(s.ht_v, t - 1)
                if past(b + t - 2):
                    e.wait_ge(k.ln_sum, b + t - 2)
                for n in range(F1 // P):
                    m = e.matmul(Y, ht[:, n, :], k.w2q[:, n, :], start=(n == 0), stop=(n == F1 // P - 1))
                m.then_inc(s.y_done, 1)
        over_tiles(e, 2, step)
        e.wait_ge(k.x_ready, b + NT)

    def scalar(e):
        def step(t, p):
            q = 1 - p
            if live(t, 2):
                e.wait_ge(s.h_turned, t - 1)
                if past(t - 2):
                    e.wait_ge(s.y_done, t - 2)
                nc.scalar.activation(ht[:, 0:4, :], HT[:, 0, :].rearrange("p (n i) -> p n i", n=4), ACT.Copy,
                                     bias=-ROUND).then_inc(s.ht_a, 1)
            if live(t, 1):
                e.wait_ge(s.pre, t)
                nc.scalar.activation(k.wide[:, q], k.wide[:, q], ACT.Gelu_apprx_tanh).then_inc(s.gelu, 1)
            if live(t, 0):
                e.wait_ge(s.x_turned, t + 1)
                if past(t):
                    e.wait_ge(s.hidden, t)
                nc.scalar.activation(k.xtq[:], XT.rearrange("p (c n) -> p c n", c=KC), ACT.Copy,
                                     bias=-ROUND).then_inc(s.xt_out, 1)
        over_tiles(e, 2, step)

    return {"gpsimd": gpsimd, "vector": vector, "tensor": tensor, "scalar": scalar}


def fourier_attention(k, ph):
    nc, ps = k.nc, k.ps
    b = ph * NT
    s = Named()
    (s.x_turned, s.xt_out, s.projected, s.squared, s.norm2, s.root, s.inv, s.normed, s.q_turned, s.qt_out,
        s.cumulated, s.p_main, s.p_cross, s.p_sum, s.y_done) = (
        k.sem("fa_" + n) for n in ("x_turned", "xt_out", "projected", "squared", "norm2", "root", "inv",
        "normed", "q_turned", "qt_out", "cumulated", "p_main", "p_cross", "p_sum", "y_done"))
    n2 = k.sb("norms", [P, 2, 2 * H])
    qk = k.shared[:, 2304:3328].rearrange("p (q n) -> p q n", q=2)
    pr = k.shared[:, 3328:4096].rearrange("p (q c n) -> p q c n", q=2, c=3)
    cr = k.shared[:, 4096:4352].rearrange("p (c n) -> p c n", c=2)
    sq = k.wide[:, 0, 0:2 * D]
    s.staged = [k.sem("fa_staged_even"), k.sem("fa_staged_odd")]
    XT, QT, C, Y = ps[:, 0, 0:D], ps[:, 2, 0:D], ps[:, 3, 0:D], ps[:, 4, 0:D]
    A = (ps[:, 1, :], ps[:, 5, :])

    def sync(e):
        if past(b):
            e.wait_ge(k.x_ready, b)

        def step(t, p):
            if live(t, 0):
                stage_rows(k, e, t, p, s.staged, s.x_turned)
        over_tiles(e, 4, step)

    def gpsimd(e):
        def step(t, p):
            q = 1 - p
            if live(t, 2):
                e.wait_ge(s.p_cross, 2 * (t - 1))
                if past(t - 3):
                    e.wait_ge(s.y_done, t - 3)
                e.tensor_tensor(pr[:, p, 2, :], cr[:, 0, :], cr[:, 1, :], ALU.add).then_inc(s.p_sum, 1)
            if live(t, 3):
                norm_rstd(k, e, ph, t - 3, q)
        over_tiles(e, 4, step)

    def tensor(e):
        def step(t, p):
            q = 1 - p
            if live(t, 1):
                e.wait_ge(s.xt_out, t)
                if past(t - 2):
                    e.wait_ge(s.normed, t - 2)
                for i in range(KC):
                    m = e.matmul(A[q], k.xt1[:, i, :], k.f_in[:, i, :], start=(i == 0), stop=(i == KC - 1))
                m.then_inc(s.projected, 1)
            if live(t, 0):
                e.wait_ge(s.staged[p], landed(t, p, 1))
                if past(t):
                    e.wait_ge(s.xt_out, t)
                for c in range(KC):
                    m = e.transpose(XT[:, c * P:(c + 1) * P], k.xs[:, p, c * P:(c + 1) * P], k.ident[:])
                m.then_inc(s.x_turned, 1)
            if live(t, 2):
                e.wait_ge(s.normed, t - 1)
                if past(t - 2):
                    e.wait_ge(s.qt_out, t - 2)
                if past(2 * (t - 2)):
                    e.wait_ge(s.p_cross, 2 * (t - 2))
                if past(t - 2):
                    e.wait_ge(s.p_main, t - 2)
                for c in range(KC):
                    m = e.transpose(QT[:, c * P:(c + 1) * P], qk[:, p, c * P:(c + 1) * P], k.ident[:])
                m.then_inc(s.q_turned, 1)
                for c in range(KC):
                    m = e.matmul(C[:, c * P:(c + 1) * P], qk[:, p, D + c * P:D + (c + 1) * P], k.tri[:],
                                 start=True, stop=True)
                m.then_inc(s.cumulated, 1)
            if live(t, 3):
                e.wait_ge(s.p_main, t - 2)
                e.wait_ge(s.p_sum, t - 2)
                if past(b + t - 3):
                    e.wait_ge(k.ln_sum, b + t - 3)
                for c in range(3):
                    m = e.matmul(Y, pr[:, q, c, :], k.f_out[:, c, :], start=(c == 0), stop=(c == 2))
                m.then_inc(s.y_done, 1)
        over_tiles(e, 4, step)
        e.wait_ge(k.x_ready, b + NT)

    def scalar(e):
        def step(t, p):
            q = 1 - p
            if live(t, 1):
                e.wait_ge(s.projected, t)
                if past(t - 1):
                    e.wait_ge(s.norm2, t - 1)
                nc.scalar.activation(sq, A[q], ACT.Square).then_inc(s.squared, 1)
            if live(t, 0):
                e.wait_ge(s.x_turned, t + 1)
                if past(t):
                    e.wait_ge(s.projected, t)
                nc.scalar.copy(k.xt1[:], XT.rearrange("p (c n) -> p c n", c=KC)).then_inc(s.xt_out, 1)
            if live(t, 1):
                e.wait_ge(s.norm2, t)
                nc.scalar.activation(n2[:, q], n2[:, q], ACT.Sqrt).then_inc(s.root, 1)
            if live(t, 2):
                e.wait_ge(s.q_turned, t - 1)
                if past(t - 2):
                    e.wait_ge(s.p_main, t - 2)
                if past(2 * (t - 2)):
                    e.wait_ge(s.p_cross, 2 * (t - 2))
                nc.scalar.copy(k.qt[:, 0], QT.rearrange("p (c n) -> p c n", c=KC)).then_inc(s.qt_out, 1)
        over_tiles(e, 4, step)

    def vector(e):
        def step(t, p):
            q = 1 - p
            if live(t, 4):
                norm_apply(k, e, ph, t - 4, p, k.x[:, t - 4, :])
            if live(t, 1):
                e.wait_ge(s.squared, t)
                e.tensor_reduce(n2[:, q].rearrange("p (s h) -> p s h", s=2),
                                sq.rearrange("p (s r h) -> p s h r", s=2, h=H), X, ALU.add).then_inc(s.norm2, 1)
            if live(t, 2):
                e.wait_ge(s.qt_out, t - 1)
                e.wait_ge(s.cumulated, t - 1)
                if past(t - 3):
                    e.wait_ge(s.y_done, t - 3)
                if past(t - 2):
                    e.wait_ge(s.p_sum, t - 2)
                e.tensor_tensor(cr[:, 0, :], k.qt[:, 0, 0, :], C[:, P:D], ALU.mult).then_inc(s.p_cross, 1)
                e.tensor_tensor(cr[:, 1, :], k.qt[:, 0, 1, :], C[:, 0:P], ALU.mult).then_inc(s.p_cross, 1)
                e.tensor_tensor(pr[:, p, 0:2, :], k.qt[:, 0], C.rearrange("p (c n) -> p c n", c=2),
                                ALU.mult).then_inc(s.p_main, 1)
            if live(t, 1):
                e.wait_ge(s.root, t)
                e.reciprocal(n2[:, q], n2[:, q]).then_inc(s.inv, 1)
                e.wait_ge(s.inv, t)
                if past(t - 2):
                    e.wait_ge(s.cumulated, t - 2)
                inv = n2[:, q].rearrange("p (s h) -> p s h", s=2).unsqueeze(2).broadcast_to([P, 2, 16, H])
                e.tensor_tensor(qk[:, q].rearrange("p (s r h) -> p s r h", s=2, h=H),
                                A[q].rearrange("p (s r h) -> p s r h", s=2, h=H), inv, ALU.mult).then_inc(s.normed, 1)
            if live(t, 3):
                e.wait_ge(s.y_done, t - 2)
                e.tensor_tensor(k.r[:, q, :], Y, k.x[:, t - 3, :], ALU.add).then_inc(k.ln_sum, 1)
                norm_stats(k, e, ph, t - 3, q)
        over_tiles(e, 4, step)

    return {"sync": sync, "gpsimd": gpsimd, "vector": vector, "tensor": tensor, "scalar": scalar}


def router(k, ph):
    nc, sb, ps = k.nc, k.sb, k.ps
    b = ph * NT
    s = Named()
    (s.x_turned, s.xt_out, s.logit, s.exped) = (
        k.sem("ro_" + n) for n in ("x_turned", "xt_out", "logit", "exped"))
    s.logged, s.chain, k.coef_ready = k.sem("ro_logged"), k.sem("ro_chain"), k.sem("coef_ready")
    s.staged = [k.sem("ro_staged_even"), k.sem("ro_staged_odd")]
    NE = E8 + 1
    lg = sb("logits", [P, NT, NE])
    k.coef = sb("coef", [P, NT, NE])
    w8 = [k.wide[:, i // 2, 256 * (i % 2):256 * (i % 2) + 256].rearrange("p (t e) -> p t e", e=E8) for i in range(4)]
    m1, rank = sb("router_max", [P, NT]), k.rank
    XT, L = ps[:, 0, 0:D], ps[:, 1, 0:NE]

    xt = (k.xt1, k.ot)

    def sync(e):
        if past(b):
            e.wait_ge(k.x_ready, b)

        def step(t, p):
            if live(t, 0):
                stage_rows(k, e, t, p, s.staged, s.x_turned)
        over_tiles(e, 1, step)

    def tensor(e):
        def step(t, p):
            q = 1 - p
            if live(t, 0):
                e.wait_ge(s.staged[p], landed(t, p, 1))
                if past(t):
                    e.wait_ge(s.xt_out, t)
                for c in range(KC):
                    m = e.transpose(XT[:, c * P:(c + 1) * P], k.xs[:, p, c * P:(c + 1) * P], k.ident[:])
                m.then_inc(s.x_turned, 1)
            if live(t, 1):
                e.wait_ge(s.xt_out, t)
                if past(t - 1):
                    e.wait_ge(s.logged, t - 1)
                for i in range(KC):
                    m = e.matmul(L, xt[q][:, i, :], k.wr[:, i, :], start=(i == 0), stop=(i == KC - 1))
                m.then_inc(s.logit, 1)
        over_tiles(e, 1, step)
        e.wait_ge(s.logged, NT)

    def scalar(e):
        def step(t, p):
            if live(t, 0):
                e.wait_ge(s.x_turned, t + 1)
                if past(t - 1):
                    e.wait_ge(s.logit, t - 1)
                nc.scalar.copy(xt[p][:], XT.rearrange("p (c n) -> p c n", c=KC)).then_inc(s.xt_out, 1)
        over_tiles(e, 1, step)
        e.wait_ge(s.chain, 2)
        nc.scalar.activation(w8[0], w8[0], ACT.Exp).then_inc(s.exped, 1)
        nc.scalar.activation(k.coef[:, :, E8], lg[:, :, E8], ACT.Exp, scale=-1.0).then_inc(s.exped, 1)

    def vector(e):
        n = [0]

        def link(ins):
            n[0] += 1
            ins.then_inc(s.chain, 1)
            e.wait_ge(s.chain, n[0])

        def step(t, p):
            if live(t, 0):
                e.wait_ge(s.logit, t + 1)
                e.tensor_copy(lg[:, t, :], L).then_inc(s.logged, 1)
        over_tiles(e, 1, step)
        e.wait_ge(s.logged, NT)
        wide = [P, NT, E8]
        m = m1[:].unsqueeze(2).broadcast_to(wide)
        by_rank = rank[:].unsqueeze(1).broadcast_to(wide)
        pr, w, one, two = w8
        link(e.tensor_reduce(m1[:], lg[:, :, 0:E8], X, ALU.max))
        link(e.tensor_tensor(pr, lg[:, :, 0:E8], m, ALU.subtract))
        e.wait_ge(s.exped, 2)
        link(e.tensor_reduce(m1[:], pr, X, ALU.add))
        link(e.reciprocal(m1[:], m1[:]))
        link(e.tensor_tensor(pr, pr, m, ALU.mult))
        link(e.tensor_scalar(k.coef[:, :, E8], k.coef[:, :, E8], 1.0, None, ALU.add))
        link(e.reciprocal(k.coef[:, :, E8], k.coef[:, :, E8]))
        link(e.tensor_copy(w, pr))
        for mark in (one, two):
            link(e.tensor_reduce(m1[:], w, X, ALU.max))
            link(e.tensor_tensor(mark, w, m, ALU.is_equal))
            link(e.tensor_tensor(mark, mark, by_rank, ALU.mult))
            link(e.tensor_reduce(m1[:], mark, X, ALU.max))
            link(e.tensor_tensor(mark, mark, m, ALU.is_equal))
            link(e.tensor_tensor(w, w, mark, ALU.subtract))
        link(e.tensor_tensor(one, one, two, ALU.add))
        link(e.tensor_tensor(k.coef[:, :, 0:E8], pr, one, ALU.mult))
        e.tensor_copy(m1[:], m1[:]).then_inc(k.coef_ready, 1)

    return {"sync": sync, "vector": vector, "tensor": tensor, "scalar": scalar}


def experts(k, ph):
    nc, io, ps = k.nc, k.io, k.ps
    b = ph * NT
    s = Named()
    (s.x_turned, s.xt_out, s.gate_up, s.silu, s.hidden, s.h_turned, s.ht_out, s.down) = (
        k.sem("ex_" + n) for n in ("x_turned", "xt_out", "gate_up", "silu", "hidden",
        "h_turned", "ht_out", "down"))
    s.staged = [k.sem("ex_staged_even"), k.sem("ex_staged_odd")]
    s.coef_in = [k.sem("ex_coef_in_even"), k.sem("ex_coef_in_odd")]
    s.stored = [k.sem("ex_stored_even"), k.sem("ex_stored_odd")]
    co = k.sb("coef_tile", [P, 2, E8 + 1])
    act = k.shared[:, 6400:7104].rearrange("p (q u n) -> p q u n", q=2, u=2)
    out = k.shared[:, 7104:7616].rearrange("p (q n) -> p q n", q=2)
    XT, Y = ps[:, 0, 0:D], ps[:, 7, 0:D]
    GU = [ps[:, 1:3, :], ps[:, 3:5, :]]
    HT = [ps[:, 5, :], ps[:, 6, :]]
    PAIRS, GROUPS = NU // 2, -(-NH // 4)
    chunks = [[(n, min(P, FH - n * P)) for n in range(4 * g, min(4 * g + 4, NH))] for g in range(GROUPS)]
    h, ht = k.h_rows, k.h_t

    xt = (k.xt1, k.ot)

    def gpsimd(e):
        def step(t, p):
            if live(t, 2):
                norm_rstd(k, e, ph, t - 2, p)
        over_tiles(e, 3, step)

    def tensor(e):
        def step(t, p):
            q = 1 - p
            for j in range(PAIRS):
                if live(t, 1):
                    if j == 0:
                        e.wait_ge(s.xt_out, t)
                    if past(NU * (t - 1) + 2 * j - 2):
                        e.wait_ge(s.hidden, NU * (t - 1) + 2 * j - 2)
                    for u in range(2):
                        for i in range(KC):
                            m = e.matmul(GU[j % 2][:, u, 0:2 * FE], xt[q][:, i, :], k.gu[:, i, 2 * j + u, :],
                                         start=(i == 0), stop=(i == KC - 1))
                    m.then_inc(s.gate_up, 1)
                if live(t, 0) and j == 2:
                    e.wait_ge(s.staged[p], landed(t, p, 1))
                    if past(t):
                        e.wait_ge(s.xt_out, t)
                    for c in range(KC):
                        m = e.transpose(XT[:, c * P:(c + 1) * P], k.xs[:, p, c * P:(c + 1) * P], k.ident[:])
                    m.then_inc(s.x_turned, 1)
                if live(t, 2) and j >= 1:
                    g = j - 1
                    e.wait_ge(s.ht_out, GROUPS * (t - 2) + g + 1)
                    if g == 0:
                        if past(b + t - 2):
                            e.wait_ge(k.ln_sum, b + t - 2)
                    for n, rows in chunks[g]:
                        m = e.matmul(Y, ht[0:rows, n, :], k.dn[0:rows, n, :], start=(n == 0), stop=(n == NH - 1))
                    m.then_inc(s.down, 1)
                if live(t, 2) and j < GROUPS:
                    apart(k, e, NU * (t - 1), GROUPS * (t - 2) + j - 1)
                    e.wait_ge(s.hidden, NU * (t - 1))
                    if past(GROUPS * (t - 2) + j - 1):
                        e.wait_ge(s.ht_out, GROUPS * (t - 2) + j - 1)
                    for n, rows in chunks[j]:
                        m = e.transpose(HT[j % 2][0:rows, (n - 4 * j) * P:(n - 4 * j + 1) * P],
                                        h[:, p, n * P:n * P + rows], k.ident[:])
                    m.then_inc(s.h_turned, 1)
        over_tiles(e, 3, step)

    def scalar(e):
        def step(t, p):
            for j in range(PAIRS):
                if live(t, 1):
                    e.wait_ge(s.gate_up, PAIRS * (t - 1) + j + 1)
                    if past(NU * (t - 1) + 2 * j - 2):
                        e.wait_ge(s.hidden, NU * (t - 1) + 2 * j - 2)
                    nc.scalar.activation(act[:, j % 2], GU[j % 2][:, :, 0:FE], ACT.Silu).then_inc(s.silu, 1)
                if live(t, 0) and j == 2:
                    e.wait_ge(s.x_turned, t + 1)
                    if past(PAIRS * (t - 1)):
                        e.wait_ge(s.gate_up, PAIRS * (t - 1))
                    nc.scalar.copy(xt[p][:], XT.rearrange("p (c n) -> p c n", c=KC)).then_inc(s.xt_out, 1)
                if live(t, 2) and j < GROUPS:
                    e.wait_ge(s.h_turned, GROUPS * (t - 2) + j + 1)
                    if past(GROUPS * (t - 3) + j + 1):
                        e.wait_ge(s.down, GROUPS * (t - 3) + j + 1)
                    n0, nn, rows = chunks[j][0][0], len(chunks[j]), chunks[j][0][1]
                    nc.scalar.copy(ht[0:rows, n0:n0 + nn, :], HT[j % 2][0:rows, 0:nn * P].rearrange(
                        "p (n i) -> p n i", n=nn)).then_inc(s.ht_out, 1)
        over_tiles(e, 3, step)

    def vector(e):
        def step(t, p):
            q = 1 - p
            for j in range(PAIRS):
                if live(t, 1):
                    e.wait_ge(s.silu, PAIRS * (t - 1) + j + 1)
                    if j == 0:
                        e.wait_ge(s.coef_in[q], landed(t - 1, q, 1))
                        if past(GROUPS * (t - 2)):
                            e.wait_ge(s.h_turned, GROUPS * (t - 2))
                    for u in range(2):
                        unit = 2 * j + u
                        e.scalar_tensor_tensor(out=h[:, q, unit * FE:(unit + 1) * FE], in0=act[:, j % 2, u, :],
                                               scalar=co[:, q, min(unit, E8):min(unit, E8) + 1],
                                               in1=GU[j % 2][:, u, FE:2 * FE], op0=ALU.mult,
                                               op1=ALU.mult).then_inc(s.hidden, 1)
                if live(t, 3) and j == 0:
                    if past(t - 4):
                        e.wait_ge(s.stored[q], landed(t - 5, q, 1))
                    norm_apply(k, e, ph, t - 3, q, out[:, q, :])
            if live(t, 2):
                e.wait_ge(s.down, GROUPS * (t - 1))
                e.tensor_tensor(k.r[:, p, :], Y, k.x[:, t - 2, :], ALU.add).then_inc(k.ln_sum, 1)
                norm_stats(k, e, ph, t - 2, p)
        over_tiles(e, 4, step)

    def sync(e):
        e.wait_ge(k.coef_ready, 1)

        def step(t, p):
            q = 1 - p
            if live(t, 0):
                stage_rows(k, e, t, p, s.staged, s.x_turned)
                if past(NU * (t - 1)):
                    e.wait_ge(s.hidden, NU * (t - 1))
                e.dma_start(co[:, p], k.coef[:, t, :]).then_inc(s.coef_in[p], 16)
            if live(t, 3):
                e.wait_ge(k.x_ready, b + t - 2)
                e.dma_start(io["out"][t - 3], out[:, q, :]).then_inc(s.stored[q], 16)
        over_tiles(e, 3, step)
        for stored in s.stored:
            e.wait_ge(stored, 8 * NT)

    return {"sync": sync, "gpsimd": gpsimd, "vector": vector, "tensor": tensor, "scalar": scalar}


STAGES = 7


def decoder_kernel(nc, io):
    with ExitStack() as ctx:
        k = declare(nc, ctx, io)
        stages = [setup(k), heads_attention(k, 0, False), wide_attention(k, 1), quantised_ffn(k, 2),
                  fourier_attention(k, 3), quantised_queries(k, 4), heads_attention(k, 4, True),
                  router(k, 5), experts(k, 5)]
        block = ctx.enter_context(nc.Block())

        @block.sync
        def _(e):
            for st in stages:
                if "sync" in st:
                    st["sync"](e)

        @block.gpsimd
        def _(e):
            for st in stages:
                if "gpsimd" in st:
                    st["gpsimd"](e)

        @block.scalar
        def _(e):
            for st in stages:
                if "scalar" in st:
                    st["scalar"](e)

        @block.vector
        def _(e):
            for st in stages:
                if "vector" in st:
                    st["vector"](e)

        @block.tensor
        def _(e):
            for st in stages:
                if "tensor" in st:
                    st["tensor"](e)


def head_order():
    return [((c * 8 + rg * HQ + hh) * HD + d) for rg in range(2) for c in range(KC) for hh in range(HQ)
            for d in range(HD)]


def constants():
    i = np.arange(P)
    c = {"ident": np.eye(P), "mask4": (i[:, None] // HD) % HQ == np.arange(HQ)[None],
         "mask2": i[:, None] // SEQ == np.arange(2)[None],
         "dist": -np.abs((i % SEQ)[:, None] - np.arange(SEQ)[None]),
         "tri": (i[:, None] // SEQ == i[None] // SEQ) & (i[:, None] <= i[None]),
         "rank": np.tile(E8 - np.arange(E8), (P, 1))}
    dft, idft = np.zeros((D, D)), np.zeros((D, 3 * P))
    n = np.arange(HD)
    for h in range(H):
        f = h * HD + n
        for j in range(8):
            re, im = j * H + h, P + j * H + h
            cos, sin = np.cos(2 * np.pi * j * n / HD), np.sin(2 * np.pi * j * n / HD)
            if j == 0:
                dft[f, re], dft[f, im] = 0.25, 0.25 * (-1.0) ** n
                idft[f, re], idft[f, im] = 1 / HD, (-1.0) ** n / HD
            else:
                dft[f, re], dft[f, im] = 2 ** 0.5 / 4 * cos, -(2 ** 0.5) / 4 * sin
                idft[f, re], idft[f, im], idft[f, 2 * P + re] = cos / HD, -cos / HD, -sin / HD
    c["dft"], c["idft"] = (a.reshape(KC, P, -1).transpose(1, 0, 2) for a in (dft, idft))
    return {n: np.ascontiguousarray(a, dtype=np.float32) for n, a in c.items()}


def layouts(a):
    def wt(w):
        return w.T.reshape(-1, P, w.shape[0]).transpose(1, 0, 2)

    def nat(w):
        return w.reshape(-1, P, w.shape[1]).transpose(1, 0, 2)

    def col(v):
        return v.reshape(-1, P).T

    def row(v):
        return np.broadcast_to(v[None], (P, v.shape[0]))

    def tiles_t(x):
        x = x.reshape(NT, 2, SEQ, KC, P).transpose(0, 4, 3, 1, 2)[:, :, :, :, None]
        return np.broadcast_to(x, (NT, P, KC, 2, 2, SEQ))
    o = head_order()
    x, ctx = a["x"].reshape(-1, D), a["ctx_2048"].reshape(-1, D)
    up = np.concatenate([a["L1_ffn_Wu"].transpose(1, 0, 2), a["L1_ffn_Su"].reshape(D, NU - E8, FE)], 1)
    gate = np.concatenate([a["L1_ffn_Wg"].transpose(1, 0, 2), a["L1_ffn_Sg"].reshape(D, NU - E8, FE)], 1)
    gu = np.concatenate([gate, up], 2).reshape(KC, P, NU, 2 * FE).transpose(1, 0, 2, 3)
    dn = np.concatenate([a["L1_ffn_Wd"].reshape(-1, D), a["L1_ffn_Sd"]], 0)
    main = (NH - 1) * P
    out = {
        "x": x.reshape(NT, P, D).transpose(1, 0, 2), "x_t": tiles_t(x), "ctx_t": tiles_t(ctx),
        "ctx": ctx.reshape(NT, 2, SEQ, D).transpose(0, 2, 1, 3),
        "mask": a["mask_BxSxS2_ff0"].reshape(NT, P, SEQ),
        "a0_wq": wt(a["L0_attn_Wq"]), "a0_wk": wt(a["L0_attn_Wk"]), "a0_wv": wt(a["L0_attn_Wv"][o]),
        "a0_wo": wt(a["L0_attn_Wo"][:, o]), "a0_bq": col(a["L0_attn_bq"]), "a0_bk": col(a["L0_attn_bk"]),
        "a0_bv": col(a["L0_attn_bv"][o]), "a0_bo": row(a["L0_attn_bo"]),
        "slopes": row(a["L0_attn_slopes"].reshape(KC, 2, HQ).transpose(1, 0, 2).reshape(-1)),
        "c0_wq": wt(a["L0_xattn_wq"]), "c0_wk": wt(a["L0_xattn_wk"]), "c0_wv": wt(a["L0_xattn_wv"]),
        "c0_wo": wt(a["L0_xattn_wo"]),
        "w1": wt(a["L0_ffn_W1"]), "w2": wt(a["L0_ffn_W2"]), "b1": row(a["L0_ffn_B1"]), "b2": row(a["L0_ffn_B2"]),
        "f_wq": nat(a["L1_attn_W_q"]), "f_wkv": nat(a["L1_attn_W_kv"]), "f_wo": wt(a["L1_attn_W_o"]),
        "c1_wq": nat(a["L1_xattn_wq"]), "c1_wo": nat(a["L1_xattn_wo"][:, o]), "c1_wk": wt(a["L1_xattn_wk"]),
        "c1_wv": wt(a["L1_xattn_wv"][o]), "c1_bk": col(a["L1_xattn_bk"]), "c1_bq": row(a["L1_xattn_bq"]),
        "c1_bv": row(a["L1_xattn_bv"][o]), "c1_bo": row(a["L1_xattn_bo"]),
        "wr": nat(np.concatenate([a["L1_ffn_Wr"], a["L1_ffn_Wsg"]], 1)), "gu": gu,
        "dn": nat(dn[:main]), "dn_tail": dn[main:],
    }
    out = {n: np.ascontiguousarray(v) for n, v in out.items()}
    out.update(constants())
    return out


def kernel(**inputs):
    import concourse.bacc as _bacc
    from concourse.bass_utils import run_bass_kernel_spmd as _run

    nc = _bacc.Bacc("TRN2", target_bir_lowering=False, num_devices=1)
    arrays = layouts({n: np.asarray(v) for n, v in inputs.items()})
    io = {n: nc.dram_tensor(f"in_{n}", a.shape, mybir.dt.from_np(a.dtype), kind="ExternalInput").ap()
          for n, a in arrays.items()}
    io["out"] = nc.dram_tensor("out_0", (NT, P, D), F32, kind="ExternalOutput").ap()
    decoder_kernel(nc, io)
    r = _run(nc, [{f"in_{n}": a for n, a in arrays.items()}], core_ids=[0])
    return r.results[0]["out_0"].reshape(BATCH, SEQ, D)
```

```python
from contextlib import ExitStack

import numpy as np

import concourse.bass as bass
from concourse import mybir
from concourse.alu_op_type import AluOpType as ALU

F32 = mybir.dt.float32
F16 = mybir.dt.float16
BF16 = mybir.dt.bfloat16
ACT = mybir.ActivationFunctionType
X = mybir.AxisListType.X
XY = mybir.AxisListType.XY
ABSMAX = bass.bass_isa.ReduceOp.absmax

BATCH, SEQ, D = 64, 64, 256
P = 128
NT = BATCH * SEQ // P
KC = D // P
H, HD = 16, 16
HQ = 4
F1 = 1024
E8, FE, FS = 8, 176, 704
NU = E8 + FS // FE
FH = NU * FE
NH = -(-FH // P)
QMAX = 127.0
QEPS = 1e-8
EPS = 1e-5
ROUND = 1.5 * 2.0 ** 23
N_FIRST, N_READY = 4, 18
GW, EW = KC * NU * 2 * FE, KC * NU * 2 * FE + NH * D
EC = EW // NT
X_SCALE, W_SCALE, H_SCALE = 2.0 ** 10, 2.0 ** 10, 2.0 ** 4


class Named:
    pass


def past(count):
    return not isinstance(count, int) or count > 0


def apart(k, eng, *counts):
    for count in counts:
        if not isinstance(count, int):
            eng.compute_val(count)
    eng.wait_ge(k.filled, 4)


def over_tiles(eng, skew, step, body=2):
    lead = 6 if skew > 3 else 4
    lead += (NT - lead) % body
    for t in range(lead):
        step(t, t % 2)
    with eng.Fori(lead, NT - body + 1, body) as i:
        for n in range(body):
            step(i + n if n else i, n % 2)
    for t in range(NT, NT + skew):
        step(t, t % 2)


def landed(u, parity, n):
    return 8 * n * (u - parity) + 16 * n


def live(t, s):
    return not isinstance(t, int) or 0 <= t - s < NT


def stage_rows(k, sp, t, p, staged, x_turned):
    if past(t - 1):
        sp.wait_ge(x_turned, t - 1)
    sp.dma_start(k.xs[:, p, :], k.x[:, t, :]).then_inc(staged[p], 16)


def declare(nc, ctx, io):
    def sb(name, shape, dt=F32):
        return ctx.enter_context(nc.sbuf_tensor(name, shape, dt))

    k = Named()
    k.nc, k.io, k.sb = nc, io, sb
    k.sem = lambda name: ctx.enter_context(nc.semaphore(name))
    k.ps = ctx.enter_context(nc.psum_tensor("ps", [P, 8, 512], F32))
    k.x = sb("x_res", [P, NT, D])
    k.shared = sb("shared", [P, 8192])
    k.q_all = k.shared[:].rearrange("p (t c n) -> p t c n", t=NT, c=KC)
    k.h_rows = k.shared[:, 0:2 * FH].rearrange("p (b n) -> p b n", b=2)
    k.h_t = k.shared[:, 2 * FH:2 * FH + NH * P].bitcast(F16).rearrange("p (s c n) -> p s c n", s=2, c=NH)
    k.ident = sb("ident", [P, P])
    k.ones = sb("ones", [P, P])
    k.mask4 = sb("mask4", [P, HQ])
    k.mask2 = sb("mask2", [P, 2])
    k.half = sb("minus_half", [P, 32])
    k.xs = sb("x_rows", [P, 2, D])
    k.xt1 = sb("x_turned", [P, KC, P])
    k.xtq = sb("x_turned_q", [P, KC, P], BF16)
    k.sc = sb("scores", [P, 2, H, SEQ])
    k.wide = k.sc[:].rearrange("p b h j -> p b (h j)")
    k.mx, k.ri = sb("row_max", [P, 2, H]), sb("row_inv", [P, H])
    k.pt = sb("probs_t", [P, 8, P])
    k.qt, k.kt = sb("q_t", [P, 2, KC, P]), sb("k_masked", [P, KC, HQ, P])
    k.vb = sb("v_pairs", [P, 2, 2, 2, 8, HD + 1])
    k.v_moved = sb("v_moved", [P, 2, 8, HD + 1])
    k.on, k.ot = sb("o_rows", [P, D]), sb("o_t", [P, KC, P])
    k.xt = sb("x_t", [P, 2, KC, P])
    k.om = sb("o_quant", [P, 2, 4])
    k.msk = sb("mask_in", [P, 2, SEQ])
    k.r = sb("r", [P, 2, D])
    k.bn = sb("bn", [P, 2, 6])
    k.mv = sb("mv", [P, 2, 2])
    k.rstd = sb("rstd", [P, 2, 1])
    k.ln_sum, k.ln_stats, k.ln_mv, k.ln_eps, k.ln_rstd, k.x_ready = (
        k.sem("ln_" + n) for n in ("sum", "stats", "mv", "eps", "rstd", "x_ready"))
    return k


def norm_stats(k, dve, ph, u, p):
    dve.wait_ge(k.ln_sum, ph * NT + u + 1)
    dve.bn_stats(k.bn[:, p, :], k.r[:, p, :]).then_inc(k.ln_stats, 1)
    apart(k, dve, ph * NT + u + 1)
    dve.wait_ge(k.ln_stats, ph * NT + u + 1)
    dve.bn_aggr(k.mv[:, p, :], k.bn[:, p, :]).then_inc(k.ln_mv, 1)


def norm_rstd(k, pool, ph, u, p):
    apart(k, pool, ph * NT + u + 1)
    pool.wait_ge(k.ln_mv, ph * NT + u + 1)
    pool.tensor_scalar(k.rstd[:, p, :], k.mv[:, p, 1:2], EPS, None, ALU.add).then_inc(k.ln_eps, 1)
    pool.wait_ge(k.ln_eps, ph * NT + u + 1)
    pool.tensor_tensor(k.rstd[:, p, :], k.rstd[:, p, :], k.half[:, 0:1], ALU.pow).then_inc(k.ln_rstd, 1)


def norm_apply(k, dve, ph, u, p, out):
    dve.wait_ge(k.ln_rstd, ph * NT + u + 1)
    dve.tensor_scalar(out, k.r[:, p, :], k.mv[:, p, 0:1], k.rstd[:, p, :], ALU.subtract,
                      ALU.mult).then_inc(k.x_ready, 1)


def setup(k):
    nc, io, sb = k.nc, k.io, k.sb
    s_ld, s_rest, s_fill = k.sem("w_loaded"), k.sem("w_rest_loaded"), k.sem("filled")
    k.x_first, k.x_rest = k.sem("x_first_loaded"), k.sem("x_rest_loaded")
    k.filled = s_fill
    first, loads = [], []

    def w(name, shape, to=loads):
        t = sb("w_" + name, shape)
        to.append((t, io[name]))
        return t
    k.a0 = {n: w("a0_" + n, [P, KC, D], first) for n in ("wq", "wk", "wv", "wo")}
    k.a0_bq, k.a0_bk, k.a0_bv = (w("a0_" + n, [P, KC], first) for n in ("bq", "bk", "bv"))
    k.a0_bo = w("a0_bo", [P, D], first)
    slopes, dist = w("slopes", [P, H], first), w("dist", [P, SEQ], first)
    k.alibi = sb("alibi", [P, H, SEQ])
    k.c0 = {n: w("c0_" + n, [P, KC, D]) for n in ("wq", "wk", "wv", "wo")}
    k.w1q = sb("w1q", [P, KC, F1], BF16)
    k.w2q = sb("w2q", [P, F1 // P, D], BF16)
    k.b1, k.b2 = w("b1", [P, F1]), w("b2", [P, D])
    w1f = k.shared[:, 0:2048].rearrange("p (c n) -> p c n", c=KC)
    w2f = k.shared[:, 2048:4096].rearrange("p (c n) -> p c n", c=F1 // P)
    k.gmax, k.wscale = sb("gmax", [P, 2]), sb("wscale", [P, 2])
    amax, wrq = sb("amax", [P, 6]), sb("wrq", [P, 6])
    k.f_in, k.f_out = sb("f_in", [P, KC, 2 * D]), sb("f_out", [P, 3, D])
    k.tri = w("tri", [P, P])
    fnat = {n: k.shared[:, 4096 + 512 * i:4608 + 512 * i].rearrange("p (c n) -> p c n", c=KC)
            for i, n in enumerate(("f_wq", "f_wkv", "f_wo", "dft"))}
    idft = k.shared[:, 6144:6912].rearrange("p (c n) -> p c n", c=KC)
    k.c1 = {n: w("c1_" + n, [P, KC, D]) for n in ("wk", "wv")}
    k.c1_bk, k.c1_bq, k.c1_bv, k.c1_bo = (w("c1_bk", [P, KC]), w("c1_bq", [P, D]),
                                          w("c1_bv", [P, D]), w("c1_bo", [P, D]))
    k.c1_bkm = sb("c1_bk_masked", [P, HQ])
    k.c1_wqq, k.c1_woq = sb("c1_wqq", [P, KC, D], BF16), sb("c1_woq", [P, KC, D], BF16)
    k.c1_sq, k.c1_so = sb("c1_sq", [P, D]), sb("c1_so", [P, D])
    cnat = [k.shared[:, 6912:7424].rearrange("p (c n) -> p c n", c=KC),
            k.shared[:, 7424:7936].rearrange("p (c n) -> p c n", c=KC)]
    wsr = sb("wsr", [P, 4])
    diag = sb("diag", [P, 4, P])
    k.rank = w("rank", [P, E8])
    wr = w("wr", [P, KC, E8 + 1])
    k.wr = sb("wr_parts", [P, 2, KC, E8 + 1], F16)
    k.w_hi, k.w_lo = sb("w_hi", [P, EW], F16), sb("w_lo", [P, EW], F16)
    loads += [(w1f, io["w1"]), (w2f, io["w2"]), (idft, io["idft"]),
              (cnat[0], io["c1_wq"]), (cnat[1], io["c1_wo"])]
    loads += [(fnat[n], io[n]) for n in fnat]
    first += [(k.ident, io["ident"]), (k.mask4, io["mask4"]), (k.mask2, io["mask2"])]
    s_am, s_gm, s_ws, s_q, s_tr, s_ev = (k.sem("w_" + n) for n in
                                         ("absmax", "allmax", "scale", "quant", "turned", "done"))
    s_mm = k.sem("w_mm")
    k.w_done = s_ev
    NX = 8

    def load(sp, pairs, loaded):
        for dst, src in pairs:
            sp.dma_start(dst if isinstance(dst, bass.AP) else dst[:], src).then_inc(loaded, 16)

    def load_first(sp):
        load(sp, first, s_ld)
        load_x(sp, 0, k.x_first)

    def load_x(eng, i, loaded):
        tiles = slice(NT // NX * i, NT // NX * (i + 1))
        eng.dma_start(k.x[:, tiles, :], io["x"][:, tiles, :]).then_inc(loaded, 16)

    k.x_loads = NX - 1

    def load_later(eng, part, parts):
        n = -(-(NX - 1 + len(loads)) // parts)
        for i in range(n * part, min(n * part + n, NX - 1 + len(loads))):
            if i < NX - 1:
                load_x(eng, i + 1, k.x_rest)
            else:
                load(eng, loads[i - NX + 1:i - NX + 2], s_rest)

    k.load_later = load_later

    def pool_first(e):
        e.memset(k.vb[:], 0.0).then_inc(s_fill, 1)
        e.memset(k.v_moved[:], 1.0).then_inc(s_fill, 1)
        e.memset(k.half[:], -0.5).then_inc(s_fill, 1)
        e.memset(k.ones[:], 1.0).then_inc(s_fill, 1)
        e.wait_ge(s_ld, 16 * len(first))
        e.wait_ge(s_fill, 4)

    def done(ins):
        ins.then_inc(s_ev, 1)

    def vector_first(e):
        e.wait_ge(s_ld, 16 * len(first))
        e.wait_ge(s_fill, 4)
        for q in range(2):
            done(e.tensor_copy(k.vb[:, q, :, :, :, HD], k.mask2[:].unsqueeze(1).unsqueeze(3).broadcast_to(
                [P, 2, 2, 8])))
        done(e.tensor_tensor(k.alibi[:], slopes[:].unsqueeze(2).broadcast_to([P, H, SEQ]),
                             dist[:].unsqueeze(1).broadcast_to([P, H, SEQ]), ALU.mult))
        done(e.tensor_scalar(k.a0_bq[:], k.a0_bq[:], 0.25, None, ALU.mult))

    def tensor_first(e):
        e.wait_ge(s_ld, 16 * len(first))
        e.wait_ge(s_ev, N_FIRST)

    def scalar_first(e):
        e.wait_ge(s_ld, 16 * len(first))
        e.wait_ge(s_ev, N_FIRST)

    def pool(e):
        e.wait_ge(s_am, 2)
        e.partition_all_reduce(k.gmax[:], amax[:, 0:2], P, ABSMAX).then_inc(s_gm, 1)

    def vector(e):
        e.wait_ge(s_rest, 16 * len(loads))
        e.tensor_reduce(amax[:, 0:1], w1f, XY, ALU.max, apply_absolute_value=True).then_inc(s_am, 1)
        e.tensor_reduce(amax[:, 1:2], w2f, XY, ALU.max, apply_absolute_value=True).then_inc(s_am, 1)
        e.tensor_reduce(amax[:, 2:4], cnat[0], X, ALU.max, apply_absolute_value=True).then_inc(s_am, 1)
        e.tensor_reduce(amax[:, 4:6], cnat[1], X, ALU.max, apply_absolute_value=True).then_inc(s_am, 1)
        done(e.tensor_scalar(k.c1_bq[:], k.c1_bq[:], 0.25, None, ALU.mult))
        done(e.tensor_scalar(k.c1_bkm[:], k.mask4[:], k.c1_bk[:, 1:2], None, ALU.mult))
        e.wait_ge(s_am, 4)
        e.tensor_scalar(wsr[:], amax[:, 2:6], 1.0 / QMAX, QEPS, ALU.mult, ALU.max).then_inc(s_ws, 1)
        e.wait_ge(s_ws, 1)
        e.reciprocal(wrq[:, 2:6], wsr[:]).then_inc(s_ws, 1)
        e.wait_ge(s_ws, 2)
        for j in range(4):
            e.tensor_scalar(cnat[j // 2][:, j % 2, :], cnat[j // 2][:, j % 2, :], wrq[:, 2 + j:3 + j], ROUND,
                            ALU.mult, ALU.add).then_inc(s_q, 1)
            e.tensor_scalar(diag[:, j, :], k.ident[:], wsr[:, j:j + 1], None, ALU.mult).then_inc(s_q, 1)
        e.wait_ge(s_gm, 1)
        e.reciprocal(wrq[:, 0:2], k.gmax[:]).then_inc(s_ws, 1)
        done(e.tensor_scalar(k.wscale[:], k.gmax[:], 1.0 / (QMAX * QMAX), None, ALU.mult))
        e.wait_ge(s_ws, 3)
        e.tensor_scalar(wrq[:, 0:2], wrq[:, 0:2], QMAX, None, ALU.mult).then_inc(s_ws, 1)
        e.wait_ge(s_ws, 4)
        e.tensor_scalar(w1f, w1f, wrq[:, 0:1], ROUND, ALU.mult, ALU.add).then_inc(s_q, 1)
        e.tensor_scalar(w2f, w2f, wrq[:, 1:2], ROUND, ALU.mult, ALU.add).then_inc(s_q, 1)
        e.wait_ge(s_q, 10)
        done(e.tensor_scalar(k.w2q[:], w2f, ROUND, None, ALU.subtract))
        e.tensor_scalar(k.wr[:, 0], wr[:], W_SCALE, None, ALU.mult).then_inc(s_ws, 1)
        e.wait_ge(s_ws, 5)
        done(e.scalar_tensor_tensor(out=k.wr[:, 1], in0=wr[:], scalar=W_SCALE, in1=k.wr[:, 0], op0=ALU.mult,
                                    op1=ALU.subtract))
        e.wait_ge(s_ev, N_READY)

    def tensor(e):
        e.wait_ge(s_rest, 16 * len(loads))
        e.wait_ge(s_fill, 4)
        for i, n in enumerate(("f_wq", "f_wkv")):
            for c in range(KC):
                for f in range(KC):
                    m = e.matmul(k.ps[:, 3 + i, c * D:(c + 1) * D], fnat[n][:, f, c * P:(c + 1) * P],
                                 fnat["dft"][:, f, :], start=(f == 0), stop=(f == KC - 1))
        for c in range(3):
            for f in range(KC):
                m = e.matmul(k.ps[:, 5 + c // 2, c % 2 * D:(c % 2 + 1) * D], idft[:, f, c * P:(c + 1) * P],
                             fnat["f_wo"][:, f, :], start=(f == 0), stop=(f == KC - 1))
        m.then_inc(s_mm, 1)
        e.wait_ge(s_q, 8)
        for j in range(2):
            for o in range(KC):
                for c in range(KC):
                    m = e.transpose(k.ps[:, j, (o * KC + c) * P:(o * KC + c + 1) * P],
                                    cnat[j][:, o, c * P:(c + 1) * P], k.ident[:])
            m.then_inc(s_tr, 1)
        for j in range(4):
            m = e.matmul(k.ps[:, 2, j * P:(j + 1) * P], k.ones[:], diag[:, j, :], start=True, stop=True)
        m.then_inc(s_mm, 1)
        e.wait_ge(k.w_done, N_READY)

    def scalar(e):
        def out(dst, src, **how):
            done(nc.scalar.activation(dst, src, ACT.Copy, **how))
        e.wait_ge(s_rest, 16 * len(loads))
        e.wait_ge(s_mm, 1)
        for i in range(2):
            out(k.f_in[:, :, D * i:D * i + D], k.ps[:, 3 + i, :].rearrange("p (c n) -> p c n", c=KC))
        out(k.f_out[:, 0:2, :], k.ps[:, 5, :].rearrange("p (c n) -> p c n", c=2))
        out(k.f_out[:, 2, :], k.ps[:, 6, 0:D])
        for j in range(2):
            e.wait_ge(s_tr, j + 1)
            out((k.c1_wqq, k.c1_woq)[j][:].rearrange("p c (o n) -> p c o n", o=KC),
                k.ps[:, j, :].rearrange("p (o c n) -> p c o n", o=KC, c=KC), bias=-ROUND)
        e.wait_ge(s_mm, 2)
        out(k.c1_sq[:], k.ps[:, 2, 0:D], scale=0.25)
        out(k.c1_so[:], k.ps[:, 2, D:2 * D])
        e.wait_ge(s_q, 10)
        out(k.w1q[:], w1f, bias=-ROUND)
        e.wait_ge(s_ev, N_READY)

    return ({"sync": load_first, "gpsimd": pool_first, "vector": vector_first, "tensor": tensor_first,
             "scalar": scalar_first},
            {"gpsimd": pool, "vector": vector, "tensor": tensor, "scalar": scalar})


def heads_attention(k, ph, cross):
    nc, io, sb, ps = k.nc, k.io, k.sb, k.ps
    b = ph * NT
    name = f"h{ph}_"
    if not cross:
        k.heads = Named()
        (k.heads.kproj, k.heads.vproj, k.heads.q_out, k.heads.k_out, k.heads.v_out, k.heads.scored,
            k.heads.biased, k.heads.maxed, k.heads.shifted, k.heads.exped, k.heads.inverted,
            k.heads.turned, k.heads.p_a, k.heads.weighed, k.heads.o_norm, k.heads.o_turned,
            k.heads.ot_out, k.heads.y_done, k.heads.bias_in, k.heads.v_to_move) = (
            k.sem("h_" + n) for n in ("kproj", "vproj", "q_out", "k_out", "v_out", "scored", "biased", "maxed",
            "shifted", "exped", "inverted", "turned", "p_a", "weighed", "o_norm", "o_turned",
            "ot_out", "y_done", "bias_in", "v_to_move"))
    s = k.heads
    base = NT if cross else 0
    if cross:
        cs = Named()
        (cs.k_low, cs.o_out, cs.v_bias, cs.o_max, cs.o_scale, cs.o_inv, cs.y_scaled) = (
            k.sem("hc_" + n) for n in ("k_low", "o_out", "v_bias", "o_max", "o_scale", "o_inv", "y_scaled"))
    loaded = [k.sem(name + "loaded_even"), k.sem(name + "loaded_odd")]
    v_moved = [k.sem(name + "v_moved_even"), k.sem(name + "v_moved_odd")]
    S, PT, QK, V, O, Y = ps[:, 0:2, :], ps[:, 2:4, :], ps[:, 4, :], ps[:, 5, 0:D], ps[:, 6, 0:272], ps[:, 7, :]
    O = O.rearrange("p (g h n) -> p g h n", g=8, h=2)
    OT, YY = Y[:, 0:D], Y[:, D:2 * D]
    wk, wv = (k.c1["wk"], k.c1["wv"]) if cross else (k.a0["wk"], k.a0["wv"])
    bk = k.c1_bk if cross else k.a0_bk
    n_in = 3 if cross else 1

    def sync(e):
        def step(t, p):
            if live(t, 0):
                if past(t - 1):
                    e.wait_ge(s.vproj, base + t - 1)
                if cross:
                    if past(t - 1):
                        e.wait_ge(s.scored, base + t - 1)
                    if past(t - 1):
                        e.wait_ge(s.biased, base + t - 1)
                e.dma_start(k.xt[:, p], io["ctx_t" if cross else "x_t"][t]).then_inc(loaded[p], 16)
                if cross:
                    e.wait_ge(k.q_ready, NT)
                    e.dma_start(k.qt[:, p], k.q_all[:, t]).then_inc(loaded[p], 16)
                    e.dma_start(k.msk[:, p], io["mask"][t]).then_inc(loaded[p], 16)
            if live(t, 1):
                q = 1 - p
                e.wait_ge(s.v_to_move, base + t)
                e.dma_start(k.vb[SEQ:P, q, 0, 1], k.v_moved[0:SEQ, q]).then_inc(v_moved[q], 16)
                e.dma_start(k.vb[0:SEQ, q, 1, 0], k.v_moved[SEQ:P, q]).then_inc(v_moved[q], 16)
            if not cross and isinstance(t, int) and t < 6:
                k.load_later(e, t, 6)
        over_tiles(e, 4, step)

    def tensor(e):
        def step(t, p):
            q = 1 - p
            if live(t, 1):
                apart(k, e, base + t, base + t - 1)
                if not cross:
                    e.wait_ge(s.q_out, base + t)
                e.wait_ge(s.k_out, base + t)
                if past(t - 1):
                    e.wait_ge(s.biased, base + t - 1)
                for rg in range(2):
                    for c in range(KC):
                        for bt in range(2):
                            rows = slice(64 * rg, 64 * rg + 64)
                            m = e.matmul(S[64 * bt:64 * bt + 64, rg, c * D:(c + 1) * D],
                                         k.qt[rows, q, c, 64 * bt:64 * bt + 64],
                                         k.kt[rows, c, :, 64 * bt:64 * bt + 64], start=True, stop=True)
                m.then_inc(s.scored, 1)
            if live(t, 2):
                e.wait_ge(s.exped, base + t - 1)
                if past(t - 2):
                    e.wait_ge(s.p_a, base + t - 2)
                for n in range(8):
                    m = e.transpose(PT[:, n // 4, n % 4 * P:(n % 4 + 1) * P], k.sc[:, p, 2 * n:2 * n + 2, :], k.ident[:])
                m.then_inc(s.turned, 1)
            if live(t, 3):
                if cross:
                    e.wait_ge(cs.o_out, t - 2)
                else:
                    e.wait_ge(s.o_norm, base + t - 2)
                if cross:
                    if past(t - 3):
                        e.wait_ge(cs.y_scaled, t - 3)
                elif past(b + t - 3):
                    e.wait_ge(k.ln_sum, b + t - 3)
                for c in range(KC):
                    m = e.transpose(OT[:, c * P:(c + 1) * P], k.on[:, c * P:(c + 1) * P], k.ident[:])
                m.then_inc(s.o_turned, 1)
            if live(t, 0):
                e.wait_ge(loaded[p], landed(t, p, n_in))
                if not cross:
                    if past(t):
                        e.wait_ge(s.q_out, base + t)
                if past(t):
                    e.wait_ge(s.k_out, base + t)
                for o, wt in ((0, None if cross else k.a0["wq"]), (1, wk)):
                    if wt is None:
                        continue
                    for c in range(KC):
                        for i in range(KC):
                            m = e.matmul(QK[:, (2 * o + c) * P:(2 * o + c + 1) * P], wt[:, i, c * P:(c + 1) * P],
                                         k.xt[:, p, i, :], start=(i == 0), stop=(i == KC - 1))
                m.then_inc(s.kproj, 1)
            if live(t, 2):
                e.wait_ge(s.p_a, base + t - 1)
                e.wait_ge(s.v_out, base + t - 1)
                e.wait_ge(v_moved[p], landed(t - 2, p, 2))
                if past(t - 2):
                    e.wait_ge(s.o_norm, base + t - 2)
                for n in range(8):
                    for bt in range(2):
                        m = e.matmul(O[64 * bt:64 * bt + 64, n], k.pt[:, n, 64 * bt:64 * bt + 64],
                                     k.vb[:, p, bt, :, n, :], start=True, stop=True)
                m.then_inc(s.weighed, 1)
            if live(t, 3):
                e.wait_ge(s.ot_out, base + t - 2)
                for c in range(KC):
                    m = e.matmul(YY, (k.xtq if cross else k.ot)[:, c, :], (k.c1_woq if cross else k.a0["wo"])[:, c, :],
                                 start=(c == 0), stop=(c == KC - 1))
                m.then_inc(s.y_done, 1)
            if live(t, 0):
                if past(t):
                    e.wait_ge(s.v_out, base + t)
                for i in range(KC):
                    m = e.matmul(V, k.xt[:, p, i, :], wv[:, i, :], start=(i == 0), stop=(i == KC - 1))
                m.then_inc(s.vproj, 1)
        over_tiles(e, 4, step)
        e.wait_ge(k.ln_sum, b + NT)

    def scalar(e):
        def step(t, p):
            q = 1 - p
            if live(t, 2):
                e.wait_ge(s.turned, base + t - 1)
                if past(t - 2):
                    e.wait_ge(s.weighed, base + t - 2)
                nc.scalar.copy(k.pt[:], PT.rearrange("p r (n i) -> p (r n) i", n=4)).then_inc(s.p_a, 1)
            if live(t, 3):
                e.wait_ge(s.o_turned, base + t - 2)
                if past(t - 3):
                    e.wait_ge(s.y_done, base + t - 3)
                if cross:
                    nc.scalar.activation(k.xtq[:], OT.rearrange("p (c n) -> p c n", c=KC), ACT.Copy,
                                         bias=-ROUND).then_inc(s.ot_out, 1)
                else:
                    for c in range(KC):
                        m = nc.scalar.activation(k.ot[:, c, :], OT[:, c * P:(c + 1) * P], ACT.Identity,
                                                 bias=k.a0_bv[:, c:c + 1])
                    m.then_inc(s.ot_out, 1)
            if live(t, 0) and cross:
                e.wait_ge(cs.k_low, t + 1)
                if past(t):
                    e.wait_ge(s.scored, base + t)
                for hh in range(HQ):
                    m = nc.scalar.activation(k.kt[:, 1, hh], QK[:, 3 * P:4 * P], ACT.Identity,
                                             bias=k.c1_bkm[:, hh:hh + 1], scale=k.mask4[:, hh:hh + 1])
                m.then_inc(s.k_out, 1)
            if live(t, 0) and not cross:
                e.wait_ge(s.k_out, base + t + 1)
                if past(t):
                    e.wait_ge(s.scored, base + t)
                for c in range(KC):
                    m = nc.scalar.activation(k.qt[:, p, c, :], QK[:, c * P:(c + 1) * P], ACT.Identity,
                                             bias=k.a0_bq[:, c:c + 1], scale=0.25)
                m.then_inc(s.q_out, 1)
            if live(t, 1):
                e.wait_ge(s.shifted, base + t)
                nc.scalar.activation(k.sc[:, q], k.sc[:, q], ACT.Exp).then_inc(s.exped, 1)
            if live(t, 0):
                e.wait_ge(s.vproj, base + t + 1)
                if past(t - 1):
                    e.wait_ge(s.weighed, base + t - 1)
                vv = V.rearrange("p (g h d) -> p h g d", g=8, h=2)
                if past(t - 1):
                    e.wait_ge(v_moved[p], landed(t - 2, p, 2))
                nc.scalar.copy(k.v_moved[0:SEQ, p, :, 0:HD], vv[0:SEQ, 1])
                nc.scalar.copy(k.v_moved[SEQ:P, p, :, 0:HD], vv[SEQ:P, 0]).then_inc(s.v_to_move, 1)
                nc.scalar.copy(k.vb[0:SEQ, p, 0, 0, :, 0:HD], vv[0:SEQ, 0])
                nc.scalar.copy(k.vb[SEQ:P, p, 1, 1, :, 0:HD], vv[SEQ:P, 1]).then_inc(s.v_out, 1)
        over_tiles(e, 4, step)

    def vector(e):
        def step(t, p):
            q = 1 - p
            if live(t, 1):
                e.wait_ge(s.scored, base + t)
                if past(t - 2):
                    e.wait_ge(s.turned, base + t - 2)
                if cross:
                    other = k.msk[:, q].unsqueeze(1).broadcast_to([P, H, SEQ])
                else:
                    other = k.alibi[:]
                e.tensor_tensor(k.sc[:, q], S.rearrange("p r (h j) -> p (r h) j", j=SEQ), other,
                                ALU.add).then_inc(s.biased, 1)
                e.wait_ge(s.biased, base + t)
                e.tensor_reduce(k.mx[:, q], k.sc[:, q], X, ALU.max).then_inc(s.maxed, 1)
            if live(t, 0):
                e.wait_ge(s.kproj, base + t + 1)
                if past(t):
                    e.wait_ge(s.scored, base + t)
                for c in range(1 if cross else KC):
                    m = e.scalar_tensor_tensor(
                        out=k.kt[:, c], in0=QK[:, (2 + c) * P:(3 + c) * P].unsqueeze(1).broadcast_to([P, HQ, P]),
                        scalar=bk[:, c:c + 1], in1=k.mask4[:].unsqueeze(2).broadcast_to([P, HQ, P]),
                        op0=ALU.add, op1=ALU.mult)
                m.then_inc(cs.k_low if cross else s.k_out, 1)
            if live(t, 4):
                norm_apply(k, e, ph, t - 4, p, k.x[:, t - 4, :])
            if live(t, 2):
                e.wait_ge(s.weighed, base + t - 1)
                e.reciprocal(k.ri[:].rearrange("p (g h) -> p g h", g=8), O[:, :, :, HD]).then_inc(s.inverted, 1)
                e.wait_ge(s.inverted, base + t - 1)
                if past(t - 2):
                    e.wait_ge(s.o_turned, base + t - 2)
                inv = k.ri[:].rearrange("p (g h) -> p g h", g=8).unsqueeze(3).broadcast_to([P, 8, 2, HD])
                e.tensor_tensor(k.on[:].rearrange("p (g h d) -> p g h d", g=8, h=2),
                                O[:, :, :, 0:HD], inv, ALU.mult).then_inc(s.o_norm, 1)
            if live(t, 3):
                e.wait_ge(s.y_done, base + t - 2)
                e.wait_ge(s.bias_in, base + t - 2)
                if cross:
                    e.scalar_tensor_tensor(out=k.r[:, q, :], in0=YY, scalar=k.om[:, q, 1:2], in1=k.c1_so[:],
                                           op0=ALU.mult, op1=ALU.mult).then_inc(cs.y_scaled, 1)
                else:
                    e.tensor_tensor(k.r[:, q, :], YY, k.x[:, t - 3, :], ALU.add).then_inc(k.ln_sum, 1)
            if live(t, 2) and cross:
                e.wait_ge(s.o_norm, base + t - 1)
                e.tensor_tensor(k.on[:], k.on[:], k.c1_bv[:], ALU.add).then_inc(cs.v_bias, 1)
                e.wait_ge(cs.v_bias, t - 1)
                e.tensor_reduce(k.om[:, p, 0:1], k.on[:], X, ALU.max, apply_absolute_value=True).then_inc(cs.o_max, 1)
                e.wait_ge(cs.o_max, t - 1)
                e.tensor_scalar(k.om[:, p, 1:2], k.om[:, p, 0:1], 1.0 / QMAX, QEPS, ALU.mult,
                                ALU.max).then_inc(cs.o_scale, 1)
                e.wait_ge(cs.o_scale, t - 1)
                e.reciprocal(k.om[:, p, 2:3], k.om[:, p, 1:2]).then_inc(cs.o_inv, 1)
            if live(t, 3):
                norm_stats(k, e, ph, t - 3, q)
            if live(t, 2) and cross:
                e.wait_ge(cs.o_inv, t - 1)
                e.tensor_scalar(k.on[:], k.on[:], k.om[:, p, 2:3], ROUND, ALU.mult, ALU.add).then_inc(cs.o_out, 1)
        over_tiles(e, 4, step, 4)

    def gpsimd(e):
        def step(t, p):
            q = 1 - p
            if live(t, 1):
                e.wait_ge(s.maxed, base + t)
                e.tensor_tensor(k.sc[:, q], k.sc[:, q], k.mx[:, q].unsqueeze(2).broadcast_to([P, H, SEQ]),
                                ALU.subtract).then_inc(s.shifted, 1)
            if live(t, 3) and cross:
                e.wait_ge(cs.y_scaled, t - 2)
                e.tensor_tensor(k.r[:, q, :], k.r[:, q, :], k.x[:, t - 3, :], ALU.add).then_inc(k.ln_sum, 1)
            if live(t, 3):
                norm_rstd(k, e, ph, t - 3, q)
            if live(t, 0):
                if cross:
                    e.wait_ge(k.q_ready, NT)
                elif isinstance(t, int) and t == 0:
                    e.wait_ge(k.x_first, 16)
                elif isinstance(t, int) and t == 4:
                    e.wait_ge(k.x_rest, 16 * k.x_loads)
                e.tensor_tensor(k.x[:, t, :], k.x[:, t, :], (k.c1_bo if cross else k.a0_bo)[:],
                                ALU.add).then_inc(s.bias_in, 1)
        over_tiles(e, 4, step)

    return {"sync": sync, "gpsimd": gpsimd, "vector": vector, "tensor": tensor, "scalar": scalar}


def quantised_queries(k, ph):
    nc, ps = k.nc, k.ps
    b = ph * NT
    s = Named()
    (s.maxed, s.scaled, s.inverted, s.rounded, s.turned, s.xt_out, s.projected, s.dequant, s.q_rows, s.q_turned) = (
        k.sem("qq_" + n) for n in ("maxed", "scaled", "inverted", "rounded", "turned", "xt_out", "projected",
        "dequant", "q_rows", "q_turned"))
    k.q_ready = k.sem("q_ready")
    XT, Q, QT = ps[:, 0, 0:D], ps[:, 1, 0:D], ps[:, 2, 0:D]

    def vector(e):
        if past(b):
            e.wait_ge(k.x_ready, b)

        def step(t, p):
            if live(t, 0):
                if past(t - 1):
                    e.wait_ge(s.rounded, t - 1)
                e.tensor_reduce(k.om[:, p, 0:1], k.x[:, t, :], X, ALU.max, apply_absolute_value=True).then_inc(s.maxed, 1)
            if live(t, 2):
                e.wait_ge(s.projected, t - 1)
                if past(t - 3):
                    e.wait_ge(s.q_turned, t - 3)
                e.scalar_tensor_tensor(out=k.r[:, p, :], in0=Q, scalar=k.om[:, p, 1:2], in1=k.c1_sq[:],
                                       op0=ALU.mult, op1=ALU.mult).then_inc(s.dequant, 1)
            if live(t, 0):
                e.wait_ge(s.maxed, t + 1)
                if past(t - 1):
                    e.wait_ge(s.dequant, t - 1)
                e.tensor_scalar(k.om[:, p, 1:2], k.om[:, p, 0:1], 1.0 / QMAX, QEPS, ALU.mult,
                                ALU.max).then_inc(s.scaled, 1)
            if live(t, 2):
                e.wait_ge(s.dequant, t - 1)
                e.tensor_tensor(k.r[:, p, :], k.r[:, p, :], k.c1_bq[:], ALU.add).then_inc(s.q_rows, 1)
            if live(t, 0):
                e.wait_ge(s.scaled, t + 1)
                e.reciprocal(k.om[:, p, 2:3], k.om[:, p, 1:2]).then_inc(s.inverted, 1)
                e.wait_ge(s.inverted, t + 1)
                if past(t - 1):
                    e.wait_ge(s.turned, t - 1)
                e.tensor_scalar(k.xs[:, p, :], k.x[:, t, :], k.om[:, p, 2:3], ROUND, ALU.mult,
                                ALU.add).then_inc(s.rounded, 1)
        over_tiles(e, 3, step, 4)

    def tensor(e):
        def step(t, p):
            q = 1 - p
            if live(t, 3):
                e.wait_ge(s.q_rows, t - 2)
                if past(t - 3):
                    e.wait_ge(k.q_ready, t - 3)
                for c in range(KC):
                    m = e.transpose(QT[:, c * P:(c + 1) * P], k.r[:, q, c * P:(c + 1) * P], k.ident[:])
                m.then_inc(s.q_turned, 1)
            if live(t, 1):
                e.wait_ge(s.xt_out, t)
                if past(t - 1):
                    e.wait_ge(s.dequant, t - 1)
                for c in range(KC):
                    m = e.matmul(Q, k.xtq[:, c, :], k.c1_wqq[:, c, :], start=(c == 0), stop=(c == KC - 1))
                m.then_inc(s.projected, 1)
            if live(t, 0):
                e.wait_ge(s.rounded, t + 1)
                if past(t):
                    e.wait_ge(s.xt_out, t)
                for c in range(KC):
                    m = e.transpose(XT[:, c * P:(c + 1) * P], k.xs[:, p, c * P:(c + 1) * P], k.ident[:])
                m.then_inc(s.turned, 1)
        over_tiles(e, 3, step)
        e.wait_ge(k.q_ready, NT)

    def scalar(e):
        def step(t, p):
            if live(t, 3):
                e.wait_ge(s.q_turned, t - 2)
                nc.scalar.copy(k.q_all[:, t - 3], QT.rearrange("p (c n) -> p c n", c=KC)).then_inc(k.q_ready, 1)
            if live(t, 0):
                e.wait_ge(s.turned, t + 1)
                if past(t):
                    e.wait_ge(s.projected, t)
                nc.scalar.activation(k.xtq[:], XT.rearrange("p (c n) -> p c n", c=KC), ACT.Copy,
                                     bias=-ROUND).then_inc(s.xt_out, 1)
        over_tiles(e, 3, step)

    return {"vector": vector, "tensor": tensor, "scalar": scalar}


def wide_attention(k, ph):
    nc, io, sb, ps = k.nc, k.io, k.sb, k.ps
    b = ph * NT
    s = Named()
    (s.x_turned, s.xt_out, s.qk, s.v, s.q_out, s.k_out, s.v_out, s.scored, s.maxed, s.negated,
        s.exped, s.inverted, s.turned, s.pt_out, s.weighed, s.o_out, s.y_done) = (
        k.sem("wa_" + n) for n in ("x_turned", "xt_out", "qk", "v", "q_out", "k_out", "v_out",
        "scored", "maxed", "negated", "exped", "inverted", "turned", "pt_out", "weighed", "o_out", "y_done"))
    s.staged = [k.sem("wa_staged_even"), k.sem("wa_staged_odd")]
    s.ctx = [k.sem("wa_ctx_even"), k.sem("wa_ctx_odd")]
    s.ctx_v = [k.sem("wa_ctx_v_even"), k.sem("wa_ctx_v_odd")]
    kk = k.shared[:, 0:1024].rearrange("p (q c b o j) -> p q c b o j", q=2, c=KC, b=2, o=2)
    vv = k.shared[:, 1024:2048].rearrange("p (q b n) -> p q b n", q=2, b=2)
    pr, ptt = k.shared[:, 2048:2176], k.shared[:, 2176:2304]
    st = sb("wide_stats", [P, 2, 4])
    XT, V, S, PT, O, Y = (ps[:, 0, 0:D], ps[:, 2, :], ps[:, 3, 0:P], ps[:, 4, 0:P], ps[:, 5, 0:D],
                          ps[:, 6, 0:D])
    QK = (ps[:, 1, 0:D], ps[:, 7, 0:D])
    W, SCALE = k.c0, D ** -0.5

    def sync(e):
        def step(t, p):
            q = 1 - p
            if live(t, 0):
                apart(k, e, b - NT + t + 1, t - 1)
                e.wait_ge(k.x_ready, b - NT + t + 1)
                stage_rows(k, e, t, p, s.staged, s.x_turned)
            if live(t, 1):
                if isinstance(t, int) and t == 1:
                    e.wait_ge(k.w_done, N_READY)
                if past(t - 2):
                    e.wait_ge(s.scored, t - 2)
                for c in range(KC):
                    e.dma_start(kk[:, q, c, :, 0, :], io["ctx_t"][t - 1, :, c].rearrange("p (b j) -> p b j", b=2)).then_inc(s.ctx[q], 16)
                if past(t - 2):
                    e.wait_ge(s.weighed, t - 2)
                e.dma_start(vv[0:SEQ, q], io["ctx"][t - 1]).then_inc(s.ctx_v[q], 16)
        over_tiles(e, 4, step)

    def gpsimd(e):
        def step(t, p):
            if live(t, 3):
                norm_rstd(k, e, ph, t - 3, 1 - p)
        over_tiles(e, 4, step)

    def tensor(e):
        def step(t, p):
            q = 1 - p
            if live(t, 3):
                e.wait_ge(s.exped, t - 2)
                if past(t - 3):
                    e.wait_ge(s.pt_out, t - 3)
                e.transpose(PT, pr, k.ident[:]).then_inc(s.turned, 1)
            if live(t, 2):
                e.wait_ge(s.q_out, t - 1)
                e.wait_ge(s.k_out, t - 1)
                e.wait_ge(s.ctx[p], landed(t - 2, p, 2))
                if past(t - 2):
                    e.wait_ge(s.exped, t - 2)
                for bt in range(2):
                    for c in range(KC):
                        m = e.matmul(S[64 * bt:64 * bt + 64, :], k.qt[:, 0, c, 64 * bt:64 * bt + 64],
                                     kk[:, p, c, bt], start=(c == 0), stop=(c == KC - 1))
                m.then_inc(s.scored, 1)
            if live(t, 3):
                e.wait_ge(s.pt_out, t - 2)
                e.wait_ge(s.v_out, t - 2)
                e.wait_ge(s.ctx_v[q], landed(t - 3, q, 1))
                if past(t - 3):
                    e.wait_ge(s.o_out, t - 3)
                for c in range(KC):
                    for bt in range(2):
                        m = e.matmul(O[:, c * P + 64 * bt:c * P + 64 * bt + 64], vv[:, q, bt, c * P:(c + 1) * P],
                                     ptt[:, 64 * bt:64 * bt + 64], start=True, stop=True)
                m.then_inc(s.weighed, 1)
            if live(t, 1):
                e.wait_ge(s.xt_out, t)
                if past(t - 1):
                    e.wait_ge(s.q_out, t - 1)
                if past(t - 1):
                    e.wait_ge(s.k_out, t - 1)
                for o, n in enumerate(("wq", "wk")):
                    for c in range(KC):
                        for i in range(KC):
                            m = e.matmul(QK[o][:, c * P:(c + 1) * P], W[n][:, i, c * P:(c + 1) * P],
                                         k.xt1[:, i, :], start=(i == 0), stop=(i == KC - 1))
                m.then_inc(s.qk, 1)
            if live(t, 1):
                if past(t - 1):
                    e.wait_ge(s.v_out, t - 1)
                for bt in range(2):
                    for i in range(KC):
                        m = e.matmul(V[SEQ:P, bt * D:(bt + 1) * D], k.xt1[:, i, 64 * bt:64 * bt + 64],
                                     W["wv"][:, i, :], start=(i == 0), stop=(i == KC - 1))
                m.then_inc(s.v, 1)
            if live(t, 0):
                e.wait_ge(s.staged[p], landed(t, p, 1))
                if past(t):
                    e.wait_ge(s.xt_out, t)
                for c in range(KC):
                    m = e.transpose(XT[:, c * P:(c + 1) * P], k.xs[:, p, c * P:(c + 1) * P], k.ident[:])
                m.then_inc(s.x_turned, 1)
            if live(t, 3):
                e.wait_ge(s.o_out, t - 2)
                if past(b + t - 3):
                    e.wait_ge(k.ln_sum, b + t - 3)
                for c in range(KC):
                    m = e.matmul(Y, k.ot[:, c, :], W["wo"][:, c, :], start=(c == 0), stop=(c == KC - 1))
                m.then_inc(s.y_done, 1)
        over_tiles(e, 4, step)
        e.wait_ge(k.ln_sum, b + NT)

    def scalar(e):
        def step(t, p):
            q = 1 - p
            if live(t, 3):
                e.wait_ge(s.turned, t - 2)
                if past(t - 3):
                    e.wait_ge(s.weighed, t - 3)
                nc.scalar.copy(ptt, PT).then_inc(s.pt_out, 1)
            if live(t, 2):
                e.wait_ge(s.negated, t - 1)
                if past(t - 2):
                    e.wait_ge(s.turned, t - 2)
                nc.scalar.activation(pr, S, ACT.Exp, bias=st[:, p, 1:2], scale=SCALE,
                                     accum_out=st[:, p, 2:3]).then_inc(s.exped, 1)
            if live(t, 1):
                e.wait_ge(s.qk, t)
                if past(t - 1):
                    e.wait_ge(s.scored, t - 1)
                nc.scalar.copy(k.qt[:, 0], QK[0].rearrange("p (c n) -> p c n", c=KC)).then_inc(s.q_out, 1)
                e.wait_ge(s.v, t)
                if past(t - 2):
                    e.wait_ge(s.weighed, t - 2)
                nc.scalar.copy(vv[SEQ:P, q], V[SEQ:P, :].rearrange("p (b n) -> p b n", b=2)).then_inc(s.v_out, 1)
            if live(t, 0):
                e.wait_ge(s.x_turned, t + 1)
                if past(t):
                    e.wait_ge(s.v, t)
                nc.scalar.copy(k.xt1[:], XT.rearrange("p (c n) -> p c n", c=KC)).then_inc(s.xt_out, 1)
        over_tiles(e, 4, step)

    def vector(e):
        def step(t, p):
            q = 1 - p
            if live(t, 2):
                e.wait_ge(s.scored, t - 1)
                e.tensor_reduce(st[:, p, 0:1], S, X, ALU.max).then_inc(s.maxed, 1)
                e.wait_ge(s.maxed, t - 1)
                e.tensor_scalar(st[:, p, 1:2], st[:, p, 0:1], -SCALE, None, ALU.mult).then_inc(s.negated, 1)
            if live(t, 4):
                norm_apply(k, e, ph, t - 4, p, k.x[:, t - 4, :])
            if live(t, 3):
                e.wait_ge(s.exped, t - 2)
                e.reciprocal(st[:, q, 3:4], st[:, q, 2:3]).then_inc(s.inverted, 1)
                e.wait_ge(s.weighed, t - 2)
                if past(t - 3):
                    e.wait_ge(s.y_done, t - 3)
                e.tensor_copy(k.ot[:], O.rearrange("p (c n) -> p c n", c=KC)).then_inc(s.o_out, 1)
            if live(t, 1):
                e.wait_ge(s.qk, t)
                if past(t - 2):
                    e.wait_ge(s.scored, t - 2)
                for c in range(KC):
                    m = e.tensor_copy(kk[:, q, c, :, 1, :], QK[1][:, c * P:(c + 1) * P].rearrange(
                        "p (b j) -> p b j", b=2))
                m.then_inc(s.k_out, 1)
            if live(t, 3):
                e.wait_ge(s.y_done, t - 2)
                e.wait_ge(s.inverted, t - 2)
                e.scalar_tensor_tensor(out=k.r[:, q, :], in0=Y, scalar=st[:, q, 3:4], in1=k.x[:, t - 3, :],
                                       op0=ALU.mult, op1=ALU.add).then_inc(k.ln_sum, 1)
                norm_stats(k, e, ph, t - 3, q)
        over_tiles(e, 4, step)

    return {"sync": sync, "gpsimd": gpsimd, "vector": vector, "tensor": tensor, "scalar": scalar}


def quantised_ffn(k, ph):
    nc, ps = k.nc, k.ps
    b = ph * NT
    s = Named()
    (s.bias_in, s.maxed, s.inverted, s.scaled, s.out_scale, s.rounded, s.x_turned, s.xt_out, s.hidden, s.pre,
        s.gelu, s.h_max, s.h_inv, s.h_scale, s.h_out_scale, s.h_rounded, s.h_turned, s.ht_a, s.y_done) = (
        k.sem("ff_" + n) for n in ("bias_in", "maxed", "inverted", "scaled", "out_scale", "rounded", "x_turned",
        "xt_out", "hidden", "pre", "gelu", "h_max", "h_inv", "h_scale", "h_out_scale", "h_rounded", "h_turned",
        "ht_a", "y_done"))
    ht = k.shared[:, 3968:4480].bitcast(BF16).rearrange("p (c n) -> p c n", c=F1 // P)
    fs = k.sb("ffn_scales", [P, 2, 8])
    XT, HB, HT, Y = ps[:, 0, 0:D], ps[:, 1:3, :], ps[:, 3:5, :], ps[:, 5, 0:D]

    def gpsimd(e):
        def step(t, p):
            q = 1 - p
            if live(t, 4):
                norm_rstd(k, e, ph, t - 4, p)
            if live(t, 2):
                apart(k, e, t - 1)
                e.wait_ge(s.h_scale, t - 1)
                e.tensor_scalar(k.wide[:, p], k.wide[:, p], fs[:, p, 7:8], ROUND, ALU.mult,
                                ALU.add).then_inc(s.h_rounded, 1)
            if live(t, 0):
                e.wait_ge(s.rounded, t + 1)
                e.tensor_tensor(k.x[:, t, :], k.x[:, t, :], k.b2[:], ALU.add).then_inc(s.bias_in, 1)
        over_tiles(e, 5, step)

    def vector(e):
        if past(b):
            e.wait_ge(k.x_ready, b)

        def step(t, p):
            q = 1 - p
            if live(t, 2):
                e.wait_ge(s.hidden, t - 1)
                e.wait_ge(s.out_scale, t - 1)
                if past(t - 3):
                    e.wait_ge(s.h_turned, t - 3)
                e.scalar_tensor_tensor(out=k.wide[:, p], in0=HB.rearrange("p b n -> p (b n)"),
                                       scalar=fs[:, p, 2:3], in1=k.b1[:], op0=ALU.mult,
                                       op1=ALU.add).then_inc(s.pre, 1)
            if live(t, 0):
                e.tensor_reduce(fs[:, p, 0:1], k.x[:, t, :], X, ALU.max, apply_absolute_value=True).then_inc(s.maxed, 1)
            if live(t, 5):
                norm_apply(k, e, ph, t - 5, q, k.x[:, t - 5, :])
            if live(t, 0):
                e.wait_ge(s.maxed, t + 1)
                e.reciprocal(fs[:, p, 1:2], fs[:, p, 0:1]).then_inc(s.inverted, 1)
                if past(t - 1):
                    e.wait_ge(s.pre, t - 1)
                e.tensor_scalar(fs[:, p, 2:3], fs[:, p, 0:1], k.wscale[:, 0:1], None, ALU.mult).then_inc(s.out_scale, 1)
                e.wait_ge(s.inverted, t + 1)
                e.tensor_scalar(fs[:, p, 3:4], fs[:, p, 1:2], QMAX, None, ALU.mult).then_inc(s.scaled, 1)
                e.wait_ge(s.scaled, t + 1)
                if past(t - 1):
                    e.wait_ge(s.x_turned, t - 1)
                e.tensor_scalar(k.xs[:, p, :], k.x[:, t, :], fs[:, p, 3:4], ROUND, ALU.mult,
                                ALU.add).then_inc(s.rounded, 1)
            if live(t, 2):
                e.wait_ge(s.gelu, t - 1)
                e.tensor_reduce(fs[:, p, 4:5], k.wide[:, p], X, ALU.max, apply_absolute_value=True).then_inc(s.h_max, 1)
            if live(t, 4):
                e.wait_ge(s.y_done, t - 3)
                e.wait_ge(s.bias_in, t - 3)
                e.wait_ge(s.h_out_scale, t - 3)
                e.scalar_tensor_tensor(out=k.r[:, p, :], in0=Y, scalar=fs[:, p, 6:7], in1=k.x[:, t - 4, :],
                                       op0=ALU.mult, op1=ALU.add).then_inc(k.ln_sum, 1)
            if live(t, 2):
                e.wait_ge(s.h_max, t - 1)
                e.reciprocal(fs[:, p, 5:6], fs[:, p, 4:5]).then_inc(s.h_inv, 1)
                if past(t - 3):
                    e.wait_ge(k.ln_sum, b + t - 3)
                e.tensor_scalar(fs[:, p, 6:7], fs[:, p, 4:5], k.wscale[:, 1:2], None, ALU.mult).then_inc(s.h_out_scale, 1)
                e.wait_ge(s.h_inv, t - 1)
                e.tensor_scalar(fs[:, p, 7:8], fs[:, p, 5:6], QMAX, None, ALU.mult).then_inc(s.h_scale, 1)
            if live(t, 4):
                norm_stats(k, e, ph, t - 4, p)
        over_tiles(e, 5, step, 4)

    def tensor(e):
        def step(t, p):
            q = 1 - p
            if live(t, 2):
                e.wait_ge(s.xt_out, t - 1)
                if past(t - 2):
                    e.wait_ge(s.pre, t - 2)
                for n in range(2):
                    for c in range(KC):
                        m = e.matmul(HB[:, n, :], k.xtq[:, c, :], k.w1q[:, c, n * 512:(n + 1) * 512],
                                     start=(c == 0), stop=(c == KC - 1))
                m.then_inc(s.hidden, 1)
            if live(t, 4):
                e.wait_ge(s.ht_a, t - 3)
                if past(b + t - 4):
                    e.wait_ge(k.ln_sum, b + t - 4)
                for n in range(F1 // P):
                    m = e.matmul(Y, ht[:, n, :], k.w2q[:, n, :], start=(n == 0), stop=(n == F1 // P - 1))
                m.then_inc(s.y_done, 1)
            if live(t, 1):
                e.wait_ge(s.rounded, t)
                if past(t - 1):
                    e.wait_ge(s.xt_out, t - 1)
                for c in range(KC):
                    m = e.transpose(XT[:, c * P:(c + 1) * P], k.xs[:, q, c * P:(c + 1) * P], k.ident[:])
                m.then_inc(s.x_turned, 1)
            if live(t, 3):
                e.wait_ge(s.h_rounded, t - 2)
                if past(t - 3):
                    e.wait_ge(s.ht_a, t - 3)
                for n in range(F1 // P):
                    m = e.transpose(HT[:, n // 4, n % 4 * P:(n % 4 + 1) * P], k.wide[:, q, n * P:(n + 1) * P],
                                    k.ident[:])
                m.then_inc(s.h_turned, 1)
        over_tiles(e, 5, step)
        e.wait_ge(k.ln_sum, b + NT)

    def scalar(e):
        def step(t, p):
            q = 1 - p
            if live(t, 1):
                e.wait_ge(s.x_turned, t)
                if past(t - 1):
                    e.wait_ge(s.hidden, t - 1)
                nc.scalar.activation(k.xtq[:], XT.rearrange("p (c n) -> p c n", c=KC), ACT.Copy,
                                     bias=-ROUND).then_inc(s.xt_out, 1)
            if live(t, 2):
                e.wait_ge(s.pre, t - 1)
                nc.scalar.activation(k.wide[:, p], k.wide[:, p], ACT.Gelu_apprx_tanh).then_inc(s.gelu, 1)
            if live(t, 3):
                e.wait_ge(s.h_turned, t - 2)
                if past(t - 3):
                    e.wait_ge(s.y_done, t - 3)
                nc.scalar.activation(ht, HT.rearrange("p b (n i) -> p (b n) i", n=4), ACT.Copy,
                                     bias=-ROUND).then_inc(s.ht_a, 1)
        over_tiles(e, 5, step)

    return {"gpsimd": gpsimd, "vector": vector, "tensor": tensor, "scalar": scalar}


def fourier_attention(k, ph):
    nc, ps = k.nc, k.ps
    b = ph * NT
    s = Named()
    (s.x_turned, s.xt_out, s.projected, s.squared, s.norm2, s.root, s.inv, s.normed, s.q_turned, s.qt_out,
        s.cumulated, s.p_main, s.p_cross, s.p_sum, s.y_done) = (
        k.sem("fa_" + n) for n in ("x_turned", "xt_out", "projected", "squared", "norm2", "root", "inv",
        "normed", "q_turned", "qt_out", "cumulated", "p_main", "p_cross", "p_sum", "y_done"))
    n2 = k.sb("norms", [P, 2, 2 * H])
    qk = k.shared[:, 2304:3328].rearrange("p (q n) -> p q n", q=2)
    pr = k.shared[:, 3328:4096].rearrange("p (q c n) -> p q c n", q=2, c=3)
    cr = k.shared[:, 4096:4352].rearrange("p (c n) -> p c n", c=2)
    s.w_in = [k.sem("fa_w_in_even"), k.sem("fa_w_in_odd")]
    s.w_hi, s.w_lo = k.sem("fa_w_hi"), k.sem("fa_w_lo")
    we = k.shared[:, 4352:4352 + 2 * EC].rearrange("p (q n) -> p q n", q=2)
    sq = k.wide[:, 0, 0:2 * D]
    s.staged = [k.sem("fa_staged_even"), k.sem("fa_staged_odd")]
    XT, QT, C, Y = ps[:, 0, 0:D], ps[:, 2, 0:D], ps[:, 3, 0:D], ps[:, 4, 0:D]
    A = (ps[:, 1, :], ps[:, 5, :])

    def sync(e):
        e.wait_ge(k.ln_sum, b)

        def step(t, p):
            if live(t, 0):
                apart(k, e, b - NT + t + 1, t - 1)
                e.wait_ge(k.x_ready, b - NT + t + 1)
                stage_rows(k, e, t, p, s.staged, s.x_turned)
                if past(t - 1):
                    e.wait_ge(s.w_lo, t - 1)
                e.dma_start(we[:, p, :], k.io["experts"][t]).then_inc(s.w_in[p], 16)
        over_tiles(e, 4, step)

    def gpsimd(e):
        def step(t, p):
            q = 1 - p
            if live(t, 2):
                e.wait_ge(s.p_cross, 2 * (t - 1))
                if past(t - 3):
                    e.wait_ge(s.y_done, t - 3)
                e.tensor_tensor(pr[:, p, 2, :], cr[:, 0, :], cr[:, 1, :], ALU.add).then_inc(s.p_sum, 1)
            if live(t, 3):
                norm_rstd(k, e, ph, t - 3, q)
        over_tiles(e, 4, step)

    def tensor(e):
        def step(t, p):
            q = 1 - p
            if live(t, 1):
                e.wait_ge(s.xt_out, t)
                if past(t - 2):
                    e.wait_ge(s.normed, t - 2)
                for i in range(KC):
                    m = e.matmul(A[q], k.xt1[:, i, :], k.f_in[:, i, :], start=(i == 0), stop=(i == KC - 1))
                m.then_inc(s.projected, 1)
            if live(t, 0):
                e.wait_ge(s.staged[p], landed(t, p, 1))
                if past(t):
                    e.wait_ge(s.xt_out, t)
                for c in range(KC):
                    m = e.transpose(XT[:, c * P:(c + 1) * P], k.xs[:, p, c * P:(c + 1) * P], k.ident[:])
                m.then_inc(s.x_turned, 1)
            if live(t, 2):
                e.wait_ge(s.normed, t - 1)
                if past(t - 2):
                    e.wait_ge(s.qt_out, t - 2)
                if past(2 * (t - 2)):
                    e.wait_ge(s.p_cross, 2 * (t - 2))
                if past(t - 2):
                    e.wait_ge(s.p_main, t - 2)
                for c in range(KC):
                    m = e.transpose(QT[:, c * P:(c + 1) * P], qk[:, p, c * P:(c + 1) * P], k.ident[:])
                m.then_inc(s.q_turned, 1)
                for c in range(KC):
                    m = e.matmul(C[:, c * P:(c + 1) * P], qk[:, p, D + c * P:D + (c + 1) * P], k.tri[:],
                                 start=True, stop=True)
                m.then_inc(s.cumulated, 1)
            if live(t, 3):
                e.wait_ge(s.p_main, t - 2)
                e.wait_ge(s.p_sum, t - 2)
                if past(b + t - 3):
                    e.wait_ge(k.ln_sum, b + t - 3)
                for c in range(3):
                    m = e.matmul(Y, pr[:, q, c, :], k.f_out[:, c, :], start=(c == 0), stop=(c == 2))
                m.then_inc(s.y_done, 1)
        over_tiles(e, 4, step)
        e.wait_ge(k.ln_sum, b + NT)

    def scalar(e):
        def step(t, p):
            q = 1 - p
            if live(t, 1):
                e.wait_ge(s.projected, t)
                if past(t - 1):
                    e.wait_ge(s.norm2, t - 1)
                nc.scalar.activation(sq, A[q], ACT.Square).then_inc(s.squared, 1)
                e.wait_ge(s.w_in[q], landed(t - 1, q, 1))
                nc.scalar.activation(k.w_hi[:].rearrange("p (t n) -> p t n", t=NT)[:, t - 1, :], we[:, q, :], ACT.Copy,
                                     scale=W_SCALE).then_inc(s.w_hi, 1)
            if live(t, 0):
                e.wait_ge(s.x_turned, t + 1)
                if past(t):
                    e.wait_ge(s.projected, t)
                nc.scalar.copy(k.xt1[:], XT.rearrange("p (c n) -> p c n", c=KC)).then_inc(s.xt_out, 1)
            if live(t, 2):
                e.wait_ge(s.q_turned, t - 1)
                if past(t - 2):
                    e.wait_ge(s.p_main, t - 2)
                if past(2 * (t - 2)):
                    e.wait_ge(s.p_cross, 2 * (t - 2))
                nc.scalar.copy(k.qt[:, 0], QT.rearrange("p (c n) -> p c n", c=KC)).then_inc(s.qt_out, 1)
            if live(t, 1):
                e.wait_ge(s.norm2, t)
                nc.scalar.activation(n2[:, q], n2[:, q], ACT.Sqrt).then_inc(s.root, 1)
        over_tiles(e, 4, step)

    def vector(e):
        def step(t, p):
            q = 1 - p
            if live(t, 1):
                e.wait_ge(s.squared, t)
                e.tensor_reduce(n2[:, q].rearrange("p (s h) -> p s h", s=2),
                                sq.rearrange("p (s r h) -> p s h r", s=2, h=H), X, ALU.add).then_inc(s.norm2, 1)
            if live(t, 2):
                e.wait_ge(s.qt_out, t - 1)
                e.wait_ge(s.cumulated, t - 1)
                if past(t - 3):
                    e.wait_ge(s.y_done, t - 3)
                if past(t - 2):
                    e.wait_ge(s.p_sum, t - 2)
                e.tensor_tensor(cr[:, 0, :], k.qt[:, 0, 0, :], C[:, P:D], ALU.mult).then_inc(s.p_cross, 1)
                e.tensor_tensor(cr[:, 1, :], k.qt[:, 0, 1, :], C[:, 0:P], ALU.mult).then_inc(s.p_cross, 1)
                e.tensor_tensor(pr[:, p, 0:2, :], k.qt[:, 0], C.rearrange("p (c n) -> p c n", c=2),
                                ALU.mult).then_inc(s.p_main, 1)
            if live(t, 4):
                norm_apply(k, e, ph, t - 4, p, k.x[:, t - 4, :])
            if live(t, 1):
                e.wait_ge(s.root, t)
                e.reciprocal(n2[:, q], n2[:, q]).then_inc(s.inv, 1)
                e.wait_ge(s.inv, t)
                if past(t - 2):
                    e.wait_ge(s.cumulated, t - 2)
                inv = n2[:, q].rearrange("p (s h) -> p s h", s=2).unsqueeze(2).broadcast_to([P, 2, 16, H])
                e.tensor_tensor(qk[:, q].rearrange("p (s r h) -> p s r h", s=2, h=H),
                                A[q].rearrange("p (s r h) -> p s r h", s=2, h=H), inv, ALU.mult).then_inc(s.normed, 1)
                e.wait_ge(s.w_hi, t)
                e.scalar_tensor_tensor(out=k.w_lo[:].rearrange("p (t n) -> p t n", t=NT)[:, t - 1, :], in0=we[:, q, :],
                                       scalar=W_SCALE, in1=k.w_hi[:].rearrange("p (t n) -> p t n", t=NT)[:, t - 1, :],
                                       op0=ALU.mult, op1=ALU.subtract).then_inc(s.w_lo, 1)
            if live(t, 3):
                e.wait_ge(s.y_done, t - 2)
                e.tensor_tensor(k.r[:, q, :], Y, k.x[:, t - 3, :], ALU.add).then_inc(k.ln_sum, 1)
                norm_stats(k, e, ph, t - 3, q)
        over_tiles(e, 4, step)

    return {"sync": sync, "gpsimd": gpsimd, "vector": vector, "tensor": tensor, "scalar": scalar}


def experts(k, ph):
    nc, io, ps = k.nc, k.io, k.ps
    b = ph * NT
    s = Named()
    (s.x_turned, s.xt_out, s.xl_out, s.gate_up, s.silu, s.hidden, s.h_turned, s.ht_out, s.hl_out, s.down) = (
        k.sem("ex_" + n) for n in ("x_turned", "xt_out", "xl_out", "gate_up", "silu", "hidden",
        "h_turned", "ht_out", "hl_out", "down"))
    s.staged = [k.sem("ex_staged_even"), k.sem("ex_staged_odd")]
    s.logits, s.shift, s.exped, s.chain, s.maxed = (
        k.sem("ex_" + n) for n in ("logits", "shift", "exped", "chain", "maxed"))
    s.stored = [k.sem("ex_stored_even"), k.sem("ex_stored_odd")]
    NE = E8 + 1
    co = k.sb("coef_tile", [P, 2, NE])
    CO_SCALE = H_SCALE / (X_SCALE * W_SCALE)
    rt = k.sb("router", [P, 4, E8])
    pr, rest, one, two = (rt[:, i, 0:E8] for i in range(4))
    st = k.sb("router_stats", [P, 8])
    act = k.shared[:, 6400:7104].rearrange("p (q u n) -> p q u n", q=2, u=2)
    out = k.shared[:, 7104:7616].rearrange("p (q n) -> p q n", q=2)
    XT, L, Y = ps[:, 0, 0:D], ps[:, 0, D:D + NE], ps[:, 7, 0:D]
    GU = [ps[:, 1:3, :], ps[:, 3:5, :]]
    HT = [ps[:, 5, :], ps[:, 6, :]]
    PAIRS, GROUPS = NU // 2, -(-NH // 4)
    chunks = [[(n, min(P, FH - n * P)) for n in range(4 * g, min(4 * g + 4, NH))] for g in range(GROUPS)]
    h, ht = k.h_rows, k.h_t
    xt = [buf[:].rearrange("p c n -> p (c n)").bitcast(F16).rearrange("p (s c n) -> p s c n", s=2, c=KC)
          for buf in (k.xt1, k.ot)]
    gu = [part[:, 0:GW].rearrange("p (i u n) -> p i u n", i=KC, u=NU) for part in (k.w_hi, k.w_lo)]
    dn = [part[:, GW:EW].rearrange("p (n d) -> p n d", n=NH) for part in (k.w_hi, k.w_lo)]
    PARTS = ((0, 0), (0, 1), (1, 0))

    def gpsimd(e):
        def step(t, p):
            if live(t, 2):
                norm_rstd(k, e, ph, t - 2, p)
        over_tiles(e, 3, step)

    def tensor(e):
        def step(t, p):
            q = 1 - p
            for j in range(PAIRS):
                if live(t, 1):
                    if j == 0:
                        e.wait_ge(s.xt_out, t)
                    if past(NU * (t - 1) + 2 * j - 2):
                        e.wait_ge(s.hidden, NU * (t - 1) + 2 * j - 2)
                    for u in range(2):
                        for a, c in PARTS:
                            if (j, u, a) == (0, 0, 1):
                                e.wait_ge(s.xl_out, t)
                            for i in range(KC):
                                m = e.matmul(GU[j % 2][:, u, 0:2 * FE], xt[q][:, a, i, :], gu[c][:, i, 2 * j + u, :],
                                             start=(a + c + i == 0), stop=(a == 1 and i == KC - 1))
                    m.then_inc(s.gate_up, 1)
                if live(t, 0) and j == 0:
                    e.wait_ge(s.staged[p], landed(t, p, 1))
                    if past(t):
                        e.wait_ge(s.xl_out, t)
                    if past(2 * t):
                        e.wait_ge(s.exped, 2 * t)
                    for c in range(KC):
                        m = e.transpose(XT[:, c * P:(c + 1) * P], k.xs[:, p, c * P:(c + 1) * P], k.ident[:])
                    m.then_inc(s.x_turned, 1)
                if live(t, 2) and j >= 1:
                    g = j - 1
                    e.wait_ge(s.hl_out, GROUPS * (t - 2) + g + 1)
                    if g == 0:
                        if past(b + t - 2):
                            e.wait_ge(k.ln_sum, b + t - 2)
                    for n, rows in chunks[g]:
                        for a, c in PARTS:
                            m = e.matmul(Y, ht[0:rows, a, n, :], dn[c][0:rows, n, :], start=(n + a + c == 0),
                                         stop=(a == 1 and n == NH - 1))
                    m.then_inc(s.down, 1)
                if live(t, 2) and j < GROUPS:
                    apart(k, e, NU * (t - 1), GROUPS * (t - 2) + j - 1)
                    e.wait_ge(s.hidden, NU * (t - 1))
                    if past(GROUPS * (t - 2) + j - 1):
                        e.wait_ge(s.hl_out, GROUPS * (t - 2) + j - 1)
                    for n, rows in chunks[j]:
                        m = e.transpose(HT[j % 2][0:rows, (n - 4 * j) * P:(n - 4 * j + 1) * P],
                                        h[:, p, n * P:n * P + rows], k.ident[:])
                    m.then_inc(s.h_turned, 1)
                if live(t, 0) and j == 1:
                    e.wait_ge(s.xt_out, t + 1)
                    e.wait_ge(s.xl_out, t + 1)
                    for a, c in PARTS:
                        for i in range(KC):
                            m = e.matmul(L, xt[p][:, a, i, :], k.wr[:, c, i, :], start=(a + c + i == 0),
                                         stop=(a == 1 and i == KC - 1))
                    m.then_inc(s.logits, 1)
        over_tiles(e, 3, step)

    def scalar(e):
        def step(t, p):
            for j in range(PAIRS):
                if live(t, 1):
                    e.wait_ge(s.gate_up, PAIRS * (t - 1) + j + 1)
                    if past(NU * (t - 1) + 2 * j - 2):
                        e.wait_ge(s.hidden, NU * (t - 1) + 2 * j - 2)
                    nc.scalar.activation(act[:, j % 2], GU[j % 2][:, :, 0:FE], ACT.Silu,
                                         scale=1.0 / (X_SCALE * W_SCALE)).then_inc(s.silu, 1)
                if live(t, 0) and j == 2:
                    e.wait_ge(s.shift, t + 1)
                    nc.scalar.activation(pr, L[:, 0:E8], ACT.Exp, bias=st[:, 1:2], scale=1.0 / (X_SCALE * W_SCALE),
                                         accum_out=st[:, 2:3]).then_inc(s.exped, 1)
                    nc.scalar.activation(st[:, 3:4], L[:, E8:NE], ACT.Exp,
                                         scale=-1.0 / (X_SCALE * W_SCALE)).then_inc(s.exped, 1)
                if live(t, 0) and j == 0:
                    e.wait_ge(s.x_turned, t + 1)
                    if past(PAIRS * (t - 1)):
                        e.wait_ge(s.gate_up, PAIRS * (t - 1))
                    nc.scalar.activation(xt[p][:, 0], XT.rearrange("p (c n) -> p c n", c=KC), ACT.Copy,
                                         scale=X_SCALE).then_inc(s.xt_out, 1)
                if live(t, 2) and j < GROUPS:
                    e.wait_ge(s.h_turned, GROUPS * (t - 2) + j + 1)
                    if past(GROUPS * (t - 3) + j + 1):
                        e.wait_ge(s.down, GROUPS * (t - 3) + j + 1)
                    n0, nn, rows = chunks[j][0][0], len(chunks[j]), chunks[j][0][1]
                    nc.scalar.copy(ht[0:rows, 0, n0:n0 + nn, :], HT[j % 2][0:rows, 0:nn * P].rearrange(
                        "p (n i) -> p n i", n=nn)).then_inc(s.ht_out, 1)
        over_tiles(e, 3, step)

    def vector(e):
        LINKS = 16

        def best_two(t, p, part, n):
            def link(ins):
                n[0] += 1
                ins.then_inc(s.chain, 1)

            def ready():
                e.wait_ge(s.chain, LINKS * t + n[0])

            if part == 0:
                e.wait_ge(s.exped, 2 * (t + 1))
                link(e.reciprocal(st[:, 4:5], st[:, 2:3]))
                link(e.tensor_scalar(st[:, 5:6], st[:, 3:4], 1.0, None, ALU.add))
                ready()
                link(e.tensor_scalar(pr, pr, st[:, 4:5], None, ALU.mult))
                link(e.reciprocal(st[:, 6:7], st[:, 5:6]))
            if part == 1:
                ready()
                if past(NU * (t - 1)):
                    e.wait_ge(s.hidden, NU * (t - 1))
                link(e.tensor_scalar(co[:, p, E8:NE], st[:, 6:7], CO_SCALE, None, ALU.mult))
            if part in (1, 2):
                mark, of = (one, pr) if part == 1 else (two, rest)
                if part == 2:
                    ready()
                link(e.tensor_reduce(st[:, 7:8], of, X, ALU.max))
                ready()
                link(e.scalar_tensor_tensor(out=mark, in0=of, scalar=st[:, 7:8], in1=k.rank[:], op0=ALU.is_equal,
                                            op1=ALU.mult))
                ready()
                link(e.tensor_reduce(st[:, 0:1], mark, X, ALU.max))
                ready()
                link(e.tensor_scalar(mark, mark, st[:, 0:1], 2.0, ALU.is_equal, ALU.mult))
            if part == 3:
                ready()
                link(e.tensor_tensor(one, one, two, ALU.add))
                ready()
                link(e.scalar_tensor_tensor(out=co[:, p, 0:E8], in0=pr, scalar=0.5 * CO_SCALE, in1=one, op0=ALU.mult,
                                            op1=ALU.mult))
                assert n[0] == LINKS
            if part == 1:
                ready()
                link(e.tensor_tensor(rest, pr, one, ALU.subtract))

        def step(t, p):
            q = 1 - p
            n = [0]
            for j in range(PAIRS):
                if live(t, 1):
                    e.wait_ge(s.silu, PAIRS * (t - 1) + j + 1)
                    if j == 0:
                        apart(k, e, LINKS * t)
                        e.wait_ge(s.chain, LINKS * t)
                        if past(GROUPS * (t - 2)):
                            e.wait_ge(s.h_turned, GROUPS * (t - 2))
                    for u in range(2):
                        unit = 2 * j + u
                        e.scalar_tensor_tensor(out=h[:, q, unit * FE:(unit + 1) * FE], in0=act[:, j % 2, u, :],
                                               scalar=co[:, q, min(unit, E8):min(unit, E8) + 1],
                                               in1=GU[j % 2][:, u, FE:2 * FE], op0=ALU.mult,
                                               op1=ALU.mult).then_inc(s.hidden, 1)
                if live(t, 2) and j < GROUPS:
                    e.wait_ge(s.ht_out, GROUPS * (t - 2) + j + 1)
                    n0, nn, rows = chunks[j][0][0], len(chunks[j]), chunks[j][0][1]
                    e.tensor_tensor(ht[0:rows, 1, n0:n0 + nn, :], HT[j % 2][0:rows, 0:nn * P].rearrange(
                        "p (n i) -> p n i", n=nn), ht[0:rows, 0, n0:n0 + nn, :], ALU.subtract).then_inc(s.hl_out, 1)
                if live(t, 0) and j == 0:
                    e.wait_ge(s.xt_out, t + 1)
                    e.scalar_tensor_tensor(out=xt[p][:, 1], in0=XT.rearrange("p (c n) -> p c n", c=KC), scalar=X_SCALE,
                                           in1=xt[p][:, 0], op0=ALU.mult, op1=ALU.subtract).then_inc(s.xl_out, 1)
                if live(t, 3) and j == 0:
                    if past(t - 4):
                        e.wait_ge(s.stored[q], landed(t - 5, q, 1))
                    norm_apply(k, e, ph, t - 3, q, out[:, q, :])
                if live(t, 0) and j == 1:
                    e.wait_ge(s.logits, t + 1)
                    if past(LINKS * t):
                        e.wait_ge(s.chain, LINKS * t)
                    e.tensor_reduce(st[:, 0:1], L[:, 0:E8], X, ALU.max).then_inc(s.maxed, 1)
                    e.wait_ge(s.maxed, t + 1)
                    e.tensor_scalar(st[:, 1:2], st[:, 0:1], -1.0 / (X_SCALE * W_SCALE), None,
                                    ALU.mult).then_inc(s.shift, 1)
                if live(t, 0) and j >= 2:
                    best_two(t, p, j - 2, n)
            if live(t, 2):
                e.wait_ge(s.down, GROUPS * (t - 1))
                e.scalar_tensor_tensor(out=k.r[:, p, :], in0=Y, scalar=1.0 / (H_SCALE * W_SCALE), in1=k.x[:, t - 2, :],
                                       op0=ALU.mult, op1=ALU.add).then_inc(k.ln_sum, 1)
                norm_stats(k, e, ph, t - 2, p)
        over_tiles(e, 4, step)

    def sync(e):
        def step(t, p):
            q = 1 - p
            if live(t, 0):
                apart(k, e, b - NT + t + 1, t - 1)
                e.wait_ge(k.x_ready, b - NT + t + 1)
                stage_rows(k, e, t, p, s.staged, s.x_turned)
            if live(t, 3):
                e.wait_ge(k.x_ready, b + t - 2)
                e.dma_start(io["out"][t - 3], out[:, q, :]).then_inc(s.stored[q], 16)
        over_tiles(e, 3, step)
        for stored in s.stored:
            e.wait_ge(stored, 8 * NT)

    return {"sync": sync, "gpsimd": gpsimd, "vector": vector, "tensor": tensor, "scalar": scalar}


def decoder_kernel(nc, io):
    with ExitStack() as ctx:
        k = declare(nc, ctx, io)
        prepare_first, prepare = setup(k)
        stages = [prepare_first, heads_attention(k, 0, False), prepare, wide_attention(k, 1), quantised_ffn(k, 2),
                  fourier_attention(k, 3), quantised_queries(k, 4), heads_attention(k, 4, True),
                  experts(k, 5)]
        block = ctx.enter_context(nc.Block())

        @block.sync
        def _(e):
            for st in stages:
                if "sync" in st:
                    st["sync"](e)

        @block.gpsimd
        def _(e):
            for st in stages:
                if "gpsimd" in st:
                    st["gpsimd"](e)

        @block.scalar
        def _(e):
            for st in stages:
                if "scalar" in st:
                    st["scalar"](e)

        @block.vector
        def _(e):
            for st in stages:
                if "vector" in st:
                    st["vector"](e)

        @block.tensor
        def _(e):
            for st in stages:
                if "tensor" in st:
                    st["tensor"](e)


def head_order():
    return [((c * 8 + rg * HQ + hh) * HD + d) for rg in range(2) for c in range(KC) for hh in range(HQ)
            for d in range(HD)]


def constants():
    i = np.arange(P)
    c = {"ident": np.eye(P), "mask4": (i[:, None] // HD) % HQ == np.arange(HQ)[None],
         "mask2": i[:, None] // SEQ == np.arange(2)[None],
         "dist": -np.abs((i % SEQ)[:, None] - np.arange(SEQ)[None]),
         "tri": (i[:, None] // SEQ == i[None] // SEQ) & (i[:, None] <= i[None]),
         "rank": np.tile(E8 - np.arange(E8), (P, 1))}
    dft, idft = np.zeros((D, D)), np.zeros((D, 3 * P))
    n = np.arange(HD)
    for h in range(H):
        f = h * HD + n
        for j in range(8):
            re, im = j * H + h, P + j * H + h
            cos, sin = np.cos(2 * np.pi * j * n / HD), np.sin(2 * np.pi * j * n / HD)
            if j == 0:
                dft[f, re], dft[f, im] = 0.25, 0.25 * (-1.0) ** n
                idft[f, re], idft[f, im] = 1 / HD, (-1.0) ** n / HD
            else:
                dft[f, re], dft[f, im] = 2 ** 0.5 / 4 * cos, -(2 ** 0.5) / 4 * sin
                idft[f, re], idft[f, im], idft[f, 2 * P + re] = cos / HD, -cos / HD, -sin / HD
    c["dft"], c["idft"] = (a.reshape(KC, P, -1).transpose(1, 0, 2) for a in (dft, idft))
    return {n: np.ascontiguousarray(a, dtype=np.float32) for n, a in c.items()}


def layouts(a):
    def wt(w):
        return w.T.reshape(-1, P, w.shape[0]).transpose(1, 0, 2)

    def nat(w):
        return w.reshape(-1, P, w.shape[1]).transpose(1, 0, 2)

    def col(v):
        return v.reshape(-1, P).T

    def row(v):
        return np.broadcast_to(v[None], (P, v.shape[0]))

    def tiles_t(x):
        return x.reshape(NT, P, KC, P).transpose(0, 3, 2, 1)
    o = head_order()
    x, ctx = a["x"].reshape(-1, D), a["ctx_2048"].reshape(-1, D)
    up = np.concatenate([a["L1_ffn_Wu"].transpose(1, 0, 2), a["L1_ffn_Su"].reshape(D, NU - E8, FE)], 1)
    gate = np.concatenate([a["L1_ffn_Wg"].transpose(1, 0, 2), a["L1_ffn_Sg"].reshape(D, NU - E8, FE)], 1)
    gu = np.concatenate([gate, up], 2).reshape(KC, P, NU, 2 * FE).transpose(1, 0, 2, 3)
    dn = np.concatenate([a["L1_ffn_Wd"].reshape(-1, D), a["L1_ffn_Sd"], np.zeros((NH * P - FH, D), np.float32)], 0)
    moe = np.concatenate([gu.reshape(P, GW), nat(dn).reshape(P, EW - GW)], 1)
    out = {
        "x": x.reshape(NT, P, D).transpose(1, 0, 2), "x_t": tiles_t(x), "ctx_t": tiles_t(ctx),
        "ctx": ctx.reshape(NT, 2, SEQ, D).transpose(0, 2, 1, 3),
        "mask": a["mask_BxSxS2_ff0"].reshape(NT, P, SEQ),
        "a0_wq": wt(a["L0_attn_Wq"]), "a0_wk": wt(a["L0_attn_Wk"]), "a0_wv": wt(a["L0_attn_Wv"][o]),
        "a0_wo": wt(a["L0_attn_Wo"][:, o]), "a0_bq": col(a["L0_attn_bq"]), "a0_bk": col(a["L0_attn_bk"]),
        "a0_bv": col(a["L0_attn_bv"][o]), "a0_bo": row(a["L0_attn_bo"]),
        "slopes": row(a["L0_attn_slopes"].reshape(KC, 2, HQ).transpose(1, 0, 2).reshape(-1)),
        "c0_wq": wt(a["L0_xattn_wq"]), "c0_wk": wt(a["L0_xattn_wk"]), "c0_wv": wt(a["L0_xattn_wv"]),
        "c0_wo": wt(a["L0_xattn_wo"]),
        "w1": wt(a["L0_ffn_W1"]), "w2": wt(a["L0_ffn_W2"]), "b1": row(a["L0_ffn_B1"]), "b2": row(a["L0_ffn_B2"]),
        "f_wq": nat(a["L1_attn_W_q"]), "f_wkv": nat(a["L1_attn_W_kv"]), "f_wo": wt(a["L1_attn_W_o"]),
        "c1_wq": nat(a["L1_xattn_wq"]), "c1_wo": nat(a["L1_xattn_wo"][:, o]), "c1_wk": wt(a["L1_xattn_wk"]),
        "c1_wv": wt(a["L1_xattn_wv"][o]), "c1_bk": col(a["L1_xattn_bk"]), "c1_bq": row(a["L1_xattn_bq"]),
        "c1_bv": row(a["L1_xattn_bv"][o]), "c1_bo": row(a["L1_xattn_bo"]),
        "wr": nat(np.concatenate([a["L1_ffn_Wr"], a["L1_ffn_Wsg"]], 1)),
        "experts": moe.reshape(P, NT, EC).transpose(1, 0, 2),
    }
    out = {n: np.ascontiguousarray(v) for n, v in out.items()}
    out.update(constants())
    return out


def kernel(**inputs):
    import concourse.bacc as _bacc
    from concourse.bass_utils import run_bass_kernel_spmd as _run

    nc = _bacc.Bacc("TRN2", target_bir_lowering=False, num_devices=1)
    arrays = layouts({n: np.asarray(v) for n, v in inputs.items()})
    io = {n: nc.dram_tensor(f"in_{n}", a.shape, mybir.dt.from_np(a.dtype), kind="ExternalInput").ap()
          for n, a in arrays.items()}
    io["out"] = nc.dram_tensor("out_0", (NT, P, D), F32, kind="ExternalOutput").ap()
    decoder_kernel(nc, io)
    r = _run(nc, [{f"in_{n}": a for n, a in arrays.items()}], core_ids=[0])
    return r.results[0]["out_0"].reshape(BATCH, SEQ, D)
```
